# Optimizing a Trainium2 kernel written in Bass

```python
import numpy as np
import jax
import jax.numpy as jnp

def _softmax(x, axis=-1):
    return jax.nn.softmax(x, axis=axis)

def _gelu(x):
    return jax.nn.gelu(x, approximate=True)

def _silu(x):
    return jax.nn.silu(x)

def _sigmoid(x):
    return jax.nn.sigmoid(x)

def _layernorm(x, axis=-1, eps=1e-05):
    m = jnp.mean(x, axis=axis, keepdims=True)
    v = jnp.var(x, axis=axis, keepdims=True)
    return (x - m) / jnp.sqrt(v + eps)

def _scatter_add(tgt, idx, src, axis=0):
    return tgt.at[idx].add(src)

def _segment_sum(src, seg, n):
    return jax.ops.segment_sum(src, seg, n)
kernel_name = 'mk_cond_seq_d4_seqx_r8_67f8dc'

def setup_inputs(seed: int=0):
    np.random.seed(seed)
    _w = jnp.asarray

    def _rec_inputs():
        import jax
        import jax.numpy as jnp
        _rk = jax.random.key(seed)
        x = -0.0002928 + 1 * jax.random.normal(jax.random.fold_in(_rk, 1), (32, 128, 128), jnp.float32)
        _lenS = 128 - jax.random.randint(jax.random.fold_in(_rk, 7), (32,), 0, max(1, 128 // 4) + 1, jnp.int32)
        _lenS2 = 128 - jax.random.randint(jax.random.fold_in(_rk, 8), (32,), 0, max(1, 128 // 4) + 1, jnp.int32)
        cond_1024 = 0.0061147 + 1.02565 * jax.random.normal(jax.random.fold_in(_rk, 11), (32, 128), jnp.float32)
        _validS = jnp.arange(128)[None, :] < _lenS[:, None]
        _validS2 = jnp.arange(128)[None, :] < _lenS2[:, None]
        _causal = jnp.tril(jnp.ones((128, 128), dtype=bool))
        mask_BxSxSx11_ik0 = jnp.where(jnp.ones((32, 128, 128, 11), dtype=bool), 0, 1).astype(jnp.int32)
        return (x, cond_1024, mask_BxSxSx11_ik0)
    x, cond_1024, mask_BxSxSx11_ik0 = _rec_inputs()

    def _L0_cond_setup():
        import jax, jax.numpy as jnp
        import numpy as np
        B, T, DIM = (4, 128, 128)
        COND = 128
        HEADS, DH = (16, 64)
        INNER = HEADS * DH
        MLP = 512
        EPS = 1e-05

        def _layernorm(x):
            mu = jnp.mean(x, axis=-1, keepdims=True)
            var = jnp.mean(jnp.square(x - mu), axis=-1, keepdims=True)
            return (x - mu) * jax.lax.rsqrt(var + EPS)

        def _modulate(x, shift, scale):
            return x * (1.0 + scale) + shift

        def _attention(x, W_qkv, W_out, b_out):
            Bq, Tq, _ = x.shape
            qkv = x @ W_qkv
            q, k, v = jnp.split(qkv, 3, axis=-1)
            q = q.reshape(Bq, Tq, HEADS, DH)
            k = k.reshape(Bq, Tq, HEADS, DH)
            v = v.reshape(Bq, Tq, HEADS, DH)
            scale = DH ** (-0.5)
            attn = jnp.einsum('bqhd,bkhd->bhqk', q, k) * scale
            attn = jax.nn.softmax(attn, axis=-1)
            out = jnp.einsum('bhqk,bkhd->bqhd', attn, v).reshape(Bq, Tq, INNER)
            return out @ W_out + b_out

        def _ff(x, W1, b1, W2, b2):
            return jax.nn.gelu(x @ W1 + b1, approximate=False) @ W2 + b2
        key = jax.random.key(seed)
        ks = jax.random.split(key, 12)
        s = 0.02
        return {'x': jax.random.normal(ks[0], (B, T, DIM), jnp.float32), 'c': jax.random.normal(ks[1], (B, 1, COND), jnp.float32), 'W_mod': jax.random.normal(ks[2], (COND, 6 * DIM), jnp.float32) * s, 'b_mod': jax.random.normal(ks[3], (6 * DIM,), jnp.float32) * s, 'W_qkv': jax.random.normal(ks[4], (DIM, 3 * INNER), jnp.float32) * s, 'W_out': jax.random.normal(ks[5], (INNER, DIM), jnp.float32) * s, 'b_out': jax.random.normal(ks[6], (DIM,), jnp.float32) * s, 'W1': jax.random.normal(ks[7], (DIM, MLP), jnp.float32) * s, 'b1': jax.random.normal(ks[8], (MLP,), jnp.float32) * s, 'W2': jax.random.normal(ks[9], (MLP, DIM), jnp.float32) * s, 'b2': jax.random.normal(ks[10], (DIM,), jnp.float32) * s}
    _L0_cond_all = _L0_cond_setup()
    _L0_cond_in = {k: v for k, v in _L0_cond_all.items() if k in ('W_mod', 'b_mod', 'W_qkv', 'W_out', 'b_out', 'W1', 'b1', 'W2', 'b2')}
    del _L0_cond_all

    def _L1_cond_setup():
        import jax, jax.numpy as jnp
        import numpy as np
        DIM = 128
        MLP_RATIO = 4
        EPS = 1e-06

        def rmsnorm(x, w):
            return x * jax.lax.rsqrt(jnp.mean(x * x, axis=-1, keepdims=True) + EPS) * w

        def film(x, cond, w, b):
            ss = cond @ w + b
            scale, shift = jnp.split(ss, 2, axis=-1)
            return x * (1.0 + scale[:, None, :]) + shift[:, None, :]
        key = jax.random.key(seed)
        ks = jax.random.split(key, 16)
        B, N, D = (4, 256, DIM)
        H = D * MLP_RATIO
        s = lambda fan_in: 1.0 / np.sqrt(fan_in)
        return {'x': jax.random.normal(ks[0], (B, N, D), jnp.float32), 'cond': jax.random.normal(ks[1], (B, D), jnp.float32), 'norm1_w': jnp.ones((D,), jnp.float32), 'film1_w': jax.random.normal(ks[2], (D, 2 * D), jnp.float32) * s(D), 'film1_b': jnp.zeros((2 * D,), jnp.float32), 'q_w': jax.random.normal(ks[3], (D, D), jnp.float32) * s(D), 'q_b': jnp.zeros((D,), jnp.float32), 'k_w': jax.random.normal(ks[4], (D, D), jnp.float32) * s(D), 'k_b': jnp.zeros((D,), jnp.float32), 'v_w': jax.random.normal(ks[5], (D, D), jnp.float32) * s(D), 'v_b': jnp.zeros((D,), jnp.float32), 'proj_w': jax.random.normal(ks[6], (D, D), jnp.float32) * s(D), 'proj_b': jnp.zeros((D,), jnp.float32), 'norm2_w': jnp.ones((D,), jnp.float32), 'film2_w': jax.random.normal(ks[7], (D, 2 * D), jnp.float32) * s(D), 'film2_b': jnp.zeros((2 * D,), jnp.float32), 'mlp_w1': jax.random.normal(ks[8], (D, H), jnp.float32) * s(D), 'mlp_b1': jnp.zeros((H,), jnp.float32), 'mlp_w2': jax.random.normal(ks[9], (H, D), jnp.float32) * s(H), 'mlp_b2': jnp.zeros((D,), jnp.float32)}
    _L1_cond_all = _L1_cond_setup()
    _L1_cond_in = {k: v for k, v in _L1_cond_all.items() if k in ('norm1_w', 'film1_w', 'film1_b', 'q_w', 'q_b', 'k_w', 'k_b', 'v_w', 'v_b', 'proj_w', 'proj_b', 'norm2_w', 'film2_w', 'film2_b', 'mlp_w1', 'mlp_b1', 'mlp_w2', 'mlp_b2')}
    del _L1_cond_all

    def _L2_cond_setup():
        import jax, jax.numpy as jnp
        import numpy as np
        D_MODEL = 128
        NHEAD = 16
        HEAD_DIM = D_MODEL // NHEAD
        D_FF = 512
        EPS = 1e-05

        def _layernorm(x):
            mu = jnp.mean(x, axis=-1, keepdims=True)
            var = jnp.var(x, axis=-1, keepdims=True)
            return (x - mu) * jax.lax.rsqrt(var + EPS)
        key = jax.random.key(seed)
        ks = jax.random.split(key, 16)
        B, N = (4, 256)
        s = 0.02
        inp = {'x': jax.random.normal(ks[0], (B, N, D_MODEL), jnp.float32), 'c': jax.random.normal(ks[1], (B, D_MODEL), jnp.float32), 'W_ada': jax.random.normal(ks[2], (D_MODEL, 6 * D_MODEL), jnp.float32) * s, 'b_ada': jnp.zeros((6 * D_MODEL,), jnp.float32), 'Wq': jax.random.normal(ks[3], (D_MODEL, D_MODEL), jnp.float32) * s, 'bq': jnp.zeros((D_MODEL,), jnp.float32), 'Wk': jax.random.normal(ks[4], (D_MODEL, D_MODEL), jnp.float32) * s, 'bk': jnp.zeros((D_MODEL,), jnp.float32), 'Wv': jax.random.normal(ks[5], (D_MODEL, D_MODEL), jnp.float32) * s, 'bv': jnp.zeros((D_MODEL,), jnp.float32), 'Wo': jax.random.normal(ks[6], (D_MODEL, D_MODEL), jnp.float32) * s, 'bo': jnp.zeros((D_MODEL,), jnp.float32), 'W1': jax.random.normal(ks[7], (D_MODEL, D_FF), jnp.float32) * s, 'b1': jnp.zeros((D_FF,), jnp.float32), 'W2': jax.random.normal(ks[8], (D_FF, D_MODEL), jnp.float32) * s, 'b2': jnp.zeros((D_MODEL,), jnp.float32)}
        return inp
    _L2_cond_all = _L2_cond_setup()
    _L2_cond_in = {k: v for k, v in _L2_cond_all.items() if k in ('W_ada', 'b_ada', 'Wq', 'bq', 'Wk', 'bk', 'Wv', 'bv', 'Wo', 'bo', 'W1', 'b1', 'W2', 'b2')}
    del _L2_cond_all

    def _L3_cond_setup():
        import jax, jax.numpy as jnp
        import numpy as np
        NONGT = 20
        H = 16
        NEG = -9000000000000000.0

        def _gat_attention(self_feat, cond_adj, label_bias, Wq, bq, Wk, bk, Wout, bout):
            B, N, F = self_feat.shape
            ng = min(NONGT, N)
            dh = F // H
            kv = self_feat[:, :ng]
            qh = (self_feat @ Wq.T + bq).reshape(B, N, H, dh)
            kh = (kv @ Wk.T + bk).reshape(B, ng, H, dh)
            aff = jnp.einsum('bnhd,bmhd->bnhm', qh, kh) * (1.0 / np.sqrt(dh))
            mask = cond_adj[:, :, None, :] > 0
            aff = jnp.where(mask, aff, NEG) + label_bias[:, :, None, :]
            w = jax.nn.softmax(aff, axis=-1)
            out_t = jnp.einsum('bnhm,bmf->bnhf', w, kv)
            out = jnp.einsum('bnhf,hgf->bnhg', out_t, Wout) + bout.reshape(H, F // H)
            return out.reshape(B, N, F)

        def _forward(v, q, adj, W_self, b_self, w_bias, b_bias, Wq, bq, Wk, bk, Wout, bout):
            adj_f = adj.astype(jnp.float32)
            exp_v = v
            row_zero = exp_v.sum(-1) == 0
            q_exp = jnp.where(row_zero[..., None], 0.0, q[:, None, :])
            vcq = jnp.concatenate([exp_v, q_exp], axis=-1)
            self_feat = vcq @ W_self.T + b_self
            output = self_feat
            for d in range(2):
                A = adj_f if d == 0 else jnp.swapaxes(adj_f, 1, 2)
                A = A[:, :, :NONGT, :]
                cond = A.sum(-1)
                vb = A @ w_bias + b_bias
                output = output + _gat_attention(self_feat, cond, vb, Wq[d], bq[d], Wk[d], bk[d], Wout[d], bout[d])
            rel = jax.nn.relu(output)
            return exp_v + rel
        key = jax.random.key(seed)
        ks = jax.random.split(key, 8)
        B, N, L, F, Q = (32, 36, 11, 128, 128)
        IN = F + Q
        s = 0.02
        return {'v': jax.random.normal(ks[0], (B, N, F), jnp.float32), 'q': jax.random.normal(ks[1], (B, Q), jnp.float32), 'adj': jax.random.randint(ks[2], (B, N, N, L), 0, 2, jnp.int32), 'W_self': jax.random.normal(ks[3], (F, IN), jnp.float32) * s, 'b_self': jnp.zeros((F,), jnp.float32), 'w_bias': jax.random.normal(ks[4], (L,), jnp.float32) * s, 'b_bias': jnp.zeros((), jnp.float32), 'Wq': jax.random.normal(ks[5], (2, F, F), jnp.float32) * s, 'bq': jnp.zeros((2, F), jnp.float32), 'Wk': jax.random.normal(ks[6], (2, F, F), jnp.float32) * s, 'bk': jnp.zeros((2, F), jnp.float32), 'Wout': jax.random.normal(ks[7], (2, H, F // H, F), jnp.float32) * s, 'bout': jnp.zeros((2, F), jnp.float32)}
    _L3_cond_all = _L3_cond_setup()
    _L3_cond_in = {k: v for k, v in _L3_cond_all.items() if k in ('W_self', 'b_self', 'w_bias', 'b_bias', 'Wq', 'bq', 'Wk', 'bk', 'Wout', 'bout')}
    del _L3_cond_all
    return {'x': x, 'cond_1024': cond_1024, 'mask_BxSxSx11_ik0': mask_BxSxSx11_ik0, 'L0_cond_W_mod': _L0_cond_in['W_mod'], 'L0_cond_b_mod': _L0_cond_in['b_mod'], 'L0_cond_W_qkv': _L0_cond_in['W_qkv'], 'L0_cond_W_out': _L0_cond_in['W_out'], 'L0_cond_b_out': _L0_cond_in['b_out'], 'L0_cond_W1': _L0_cond_in['W1'], 'L0_cond_b1': _L0_cond_in['b1'], 'L0_cond_W2': _L0_cond_in['W2'], 'L0_cond_b2': _L0_cond_in['b2'], 'L1_cond_norm1_w': _L1_cond_in['norm1_w'], 'L1_cond_film1_w': _L1_cond_in['film1_w'], 'L1_cond_film1_b': _L1_cond_in['film1_b'], 'L1_cond_q_w': _L1_cond_in['q_w'], 'L1_cond_q_b': _L1_cond_in['q_b'], 'L1_cond_k_w': _L1_cond_in['k_w'], 'L1_cond_k_b': _L1_cond_in['k_b'], 'L1_cond_v_w': _L1_cond_in['v_w'], 'L1_cond_v_b': _L1_cond_in['v_b'], 'L1_cond_proj_w': _L1_cond_in['proj_w'], 'L1_cond_proj_b': _L1_cond_in['proj_b'], 'L1_cond_norm2_w': _L1_cond_in['norm2_w'], 'L1_cond_film2_w': _L1_cond_in['film2_w'], 'L1_cond_film2_b': _L1_cond_in['film2_b'], 'L1_cond_mlp_w1': _L1_cond_in['mlp_w1'], 'L1_cond_mlp_b1': _L1_cond_in['mlp_b1'], 'L1_cond_mlp_w2': _L1_cond_in['mlp_w2'], 'L1_cond_mlp_b2': _L1_cond_in['mlp_b2'], 'L2_cond_W_ada': _L2_cond_in['W_ada'], 'L2_cond_b_ada': _L2_cond_in['b_ada'], 'L2_cond_Wq': _L2_cond_in['Wq'], 'L2_cond_bq': _L2_cond_in['bq'], 'L2_cond_Wk': _L2_cond_in['Wk'], 'L2_cond_bk': _L2_cond_in['bk'], 'L2_cond_Wv': _L2_cond_in['Wv'], 'L2_cond_bv': _L2_cond_in['bv'], 'L2_cond_Wo': _L2_cond_in['Wo'], 'L2_cond_bo': _L2_cond_in['bo'], 'L2_cond_W1': _L2_cond_in['W1'], 'L2_cond_b1': _L2_cond_in['b1'], 'L2_cond_W2': _L2_cond_in['W2'], 'L2_cond_b2': _L2_cond_in['b2'], 'L3_cond_W_self': _L3_cond_in['W_self'], 'L3_cond_b_self': _L3_cond_in['b_self'], 'L3_cond_w_bias': _L3_cond_in['w_bias'], 'L3_cond_b_bias': _L3_cond_in['b_bias'], 'L3_cond_Wq': _L3_cond_in['Wq'], 'L3_cond_bq': _L3_cond_in['bq'], 'L3_cond_Wk': _L3_cond_in['Wk'], 'L3_cond_bk': _L3_cond_in['bk'], 'L3_cond_Wout': _L3_cond_in['Wout'], 'L3_cond_bout': _L3_cond_in['bout']}

def reference(x, cond_1024, mask_BxSxSx11_ik0, L0_cond_W_mod, L0_cond_b_mod, L0_cond_W_qkv, L0_cond_W_out, L0_cond_b_out, L0_cond_W1, L0_cond_b1, L0_cond_W2, L0_cond_b2, L1_cond_norm1_w, L1_cond_film1_w, L1_cond_film1_b, L1_cond_q_w, L1_cond_q_b, L1_cond_k_w, L1_cond_k_b, L1_cond_v_w, L1_cond_v_b, L1_cond_proj_w, L1_cond_proj_b, L1_cond_norm2_w, L1_cond_film2_w, L1_cond_film2_b, L1_cond_mlp_w1, L1_cond_mlp_b1, L1_cond_mlp_w2, L1_cond_mlp_b2, L2_cond_W_ada, L2_cond_b_ada, L2_cond_Wq, L2_cond_bq, L2_cond_Wk, L2_cond_bk, L2_cond_Wv, L2_cond_bv, L2_cond_Wo, L2_cond_bo, L2_cond_W1, L2_cond_b1, L2_cond_W2, L2_cond_b2, L3_cond_W_self, L3_cond_b_self, L3_cond_w_bias, L3_cond_b_bias, L3_cond_Wq, L3_cond_bq, L3_cond_Wk, L3_cond_bk, L3_cond_Wout, L3_cond_bout):
    import jax
    import jax.numpy as jnp

    def _L0_cond_ref(x, c, W_mod, b_mod, W_qkv, W_out, b_out, W1, b1, W2, b2):
        import jax, jax.numpy as jnp
        import numpy as np
        B, T, DIM = (4, 128, 128)
        COND = 128
        HEADS, DH = (16, 64)
        INNER = HEADS * DH
        MLP = 512
        EPS = 1e-05

        def _layernorm(x):
            mu = jnp.mean(x, axis=-1, keepdims=True)
            var = jnp.mean(jnp.square(x - mu), axis=-1, keepdims=True)
            return (x - mu) * jax.lax.rsqrt(var + EPS)

        def _modulate(x, shift, scale):
            return x * (1.0 + scale) + shift

        def _attention(x, W_qkv, W_out, b_out):
            Bq, Tq, _ = x.shape
            qkv = x @ W_qkv
            q, k, v = jnp.split(qkv, 3, axis=-1)
            q = q.reshape(Bq, Tq, HEADS, DH)
            k = k.reshape(Bq, Tq, HEADS, DH)
            v = v.reshape(Bq, Tq, HEADS, DH)
            scale = DH ** (-0.5)
            attn = jnp.einsum('bqhd,bkhd->bhqk', q, k) * scale
            attn = jax.nn.softmax(attn, axis=-1)
            out = jnp.einsum('bhqk,bkhd->bqhd', attn, v).reshape(Bq, Tq, INNER)
            return out @ W_out + b_out

        def _ff(x, W1, b1, W2, b2):
            return jax.nn.gelu(x @ W1 + b1, approximate=False) @ W2 + b2
        mod = jax.nn.silu(c) @ W_mod + b_mod
        sh_msa, sc_msa, g_msa, sh_mlp, sc_mlp, g_mlp = jnp.split(mod, 6, axis=-1)
        x = x + g_msa * _attention(_modulate(_layernorm(x), sh_msa, sc_msa), W_qkv, W_out, b_out)
        x = x + g_mlp * _ff(_modulate(_layernorm(x), sh_mlp, sc_mlp), W1, b1, W2, b2)
        return x

    def _L1_cond_ref(x, cond, norm1_w, film1_w, film1_b, q_w, q_b, k_w, k_b, v_w, v_b, proj_w, proj_b, norm2_w, film2_w, film2_b, mlp_w1, mlp_b1, mlp_w2, mlp_b2):
        import jax, jax.numpy as jnp
        import numpy as np
        DIM = 128
        MLP_RATIO = 4
        EPS = 1e-06

        def rmsnorm(x, w):
            return x * jax.lax.rsqrt(jnp.mean(x * x, axis=-1, keepdims=True) + EPS) * w

        def film(x, cond, w, b):
            ss = cond @ w + b
            scale, shift = jnp.split(ss, 2, axis=-1)
            return x * (1.0 + scale[:, None, :]) + shift[:, None, :]
        B, N, D = x.shape
        x_in = x
        h = film(rmsnorm(x, norm1_w), cond, film1_w, film1_b)
        Q = h @ q_w + q_b
        K = h @ k_w + k_b
        V = h @ v_w + v_b
        scores = jnp.einsum('bnd,bmd->bnm', Q, K) * D ** (-0.5)
        attn = jax.nn.softmax(scores, axis=-1)
        out = jnp.einsum('bnm,bmd->bnd', attn, V)
        x = x_in + (out @ proj_w + proj_b)
        x_in = x
        h = film(rmsnorm(x, norm2_w), cond, film2_w, film2_b)
        h = jax.nn.gelu(h @ mlp_w1 + mlp_b1, approximate=False) @ mlp_w2 + mlp_b2
        return x_in + h

    def _L2_cond_ref(x, c, W_ada, b_ada, Wq, bq, Wk, bk, Wv, bv, Wo, bo, W1, b1, W2, b2):
        import jax, jax.numpy as jnp
        import numpy as np
        D_MODEL = 128
        NHEAD = 16
        HEAD_DIM = D_MODEL // NHEAD
        D_FF = 512
        EPS = 1e-05

        def _layernorm(x):
            mu = jnp.mean(x, axis=-1, keepdims=True)
            var = jnp.var(x, axis=-1, keepdims=True)
            return (x - mu) * jax.lax.rsqrt(var + EPS)
        B, N, _ = x.shape
        ada = (c @ W_ada + b_ada)[:, None, :]
        shift1, scale1, gate1, shift2, scale2, gate2 = jnp.split(ada, 6, axis=-1)
        h = _layernorm(x) * (1.0 + scale1) + shift1
        Q = (h @ Wq + bq).reshape(B, N, NHEAD, HEAD_DIM)
        K = (h @ Wk + bk).reshape(B, N, NHEAD, HEAD_DIM)
        V = (h @ Wv + bv).reshape(B, N, NHEAD, HEAD_DIM)
        scores = jnp.einsum('bqhd,bkhd->bhqk', Q, K) / np.sqrt(HEAD_DIM).astype(np.float32)
        attn = jax.nn.softmax(scores, axis=-1)
        attn_out = jnp.einsum('bhqk,bkhd->bqhd', attn, V).reshape(B, N, D_MODEL)
        attn_out = attn_out @ Wo + bo
        x = x + gate1 * attn_out
        h = _layernorm(x) * (1.0 + scale2) + shift2
        ff = jax.nn.gelu(h @ W1 + b1, approximate=False) @ W2 + b2
        return x + gate2 * ff

    def _L3_cond_ref(v, q, adj, W_self, b_self, w_bias, b_bias, Wq, bq, Wk, bk, Wout, bout):
        import jax, jax.numpy as jnp
        import numpy as np
        NONGT = 20
        H = 16
        NEG = -9000000000000000.0

        def _gat_attention(self_feat, cond_adj, label_bias, Wq, bq, Wk, bk, Wout, bout):
            B, N, F = self_feat.shape
            ng = min(NONGT, N)
            dh = F // H
            kv = self_feat[:, :ng]
            qh = (self_feat @ Wq.T + bq).reshape(B, N, H, dh)
            kh = (kv @ Wk.T + bk).reshape(B, ng, H, dh)
            aff = jnp.einsum('bnhd,bmhd->bnhm', qh, kh) * (1.0 / np.sqrt(dh))
            mask = cond_adj[:, :, None, :] > 0
            aff = jnp.where(mask, aff, NEG) + label_bias[:, :, None, :]
            w = jax.nn.softmax(aff, axis=-1)
            out_t = jnp.einsum('bnhm,bmf->bnhf', w, kv)
            out = jnp.einsum('bnhf,hgf->bnhg', out_t, Wout) + bout.reshape(H, F // H)
            return out.reshape(B, N, F)

        def _forward(v, q, adj, W_self, b_self, w_bias, b_bias, Wq, bq, Wk, bk, Wout, bout):
            adj_f = adj.astype(jnp.float32)
            exp_v = v
            row_zero = exp_v.sum(-1) == 0
            q_exp = jnp.where(row_zero[..., None], 0.0, q[:, None, :])
            vcq = jnp.concatenate([exp_v, q_exp], axis=-1)
            self_feat = vcq @ W_self.T + b_self
            output = self_feat
            for d in range(2):
                A = adj_f if d == 0 else jnp.swapaxes(adj_f, 1, 2)
                A = A[:, :, :NONGT, :]
                cond = A.sum(-1)
                vb = A @ w_bias + b_bias
                output = output + _gat_attention(self_feat, cond, vb, Wq[d], bq[d], Wk[d], bk[d], Wout[d], bout[d])
            rel = jax.nn.relu(output)
            return exp_v + rel
        return _forward(v, q, adj, W_self, b_self, w_bias, b_bias, Wq, bq, Wk, bk, Wout, bout)
    x = _L0_cond_ref(x, cond_1024[:, None, :], L0_cond_W_mod, L0_cond_b_mod, L0_cond_W_qkv, L0_cond_W_out, L0_cond_b_out, L0_cond_W1, L0_cond_b1, L0_cond_W2, L0_cond_b2)
    x = _L1_cond_ref(x, cond_1024, L1_cond_norm1_w, L1_cond_film1_w, L1_cond_film1_b, L1_cond_q_w, L1_cond_q_b, L1_cond_k_w, L1_cond_k_b, L1_cond_v_w, L1_cond_v_b, L1_cond_proj_w, L1_cond_proj_b, L1_cond_norm2_w, L1_cond_film2_w, L1_cond_film2_b, L1_cond_mlp_w1, L1_cond_mlp_b1, L1_cond_mlp_w2, L1_cond_mlp_b2)
    x = _L2_cond_ref(x, cond_1024, L2_cond_W_ada, L2_cond_b_ada, L2_cond_Wq, L2_cond_bq, L2_cond_Wk, L2_cond_bk, L2_cond_Wv, L2_cond_bv, L2_cond_Wo, L2_cond_bo, L2_cond_W1, L2_cond_b1, L2_cond_W2, L2_cond_b2)
    x = _L3_cond_ref(x, cond_1024, mask_BxSxSx11_ik0, L3_cond_W_self, L3_cond_b_self, L3_cond_w_bias, L3_cond_b_bias, L3_cond_Wq, L3_cond_bq, L3_cond_Wk, L3_cond_bk, L3_cond_Wout, L3_cond_bout)
    return x

_drawn_inputs = setup_inputs


def setup_inputs(seed=0):
    import zlib

    import numpy as np

    out = dict(_drawn_inputs(seed))
    spreads = {'L1_cond_norm1_w': (1.0, 0.2),
     'L1_cond_film1_b': (0.0, 0.455),
     'L1_cond_q_b': (0.0, 0.8),
     'L1_cond_k_b': (0.0, 2.0),
     'L1_cond_v_b': (0.0, 0.585),
     'L1_cond_proj_b': (0.0, 0.699),
     'L1_cond_norm2_w': (1.0, 0.2),
     'L1_cond_film2_b': (0.0, 0.588),
     'L1_cond_mlp_b1': (0.0, 0.8),
     'L1_cond_mlp_b2': (0.0, 0.581),
     'L2_cond_b_ada': (0.0, 0.8),
     'L2_cond_bq': (0.0, 0.8),
     'L2_cond_bk': (0.0, 2.0),
     'L2_cond_bv': (0.0, 0.8),
     'L2_cond_bo': (0.0, 0.651),
     'L2_cond_b1': (0.0, 0.8),
     'L2_cond_b2': (0.0, 0.704),
     'L3_cond_b_self': (0.0, 0.8),
     'L3_cond_bq': (0.0, 0.1),
     'L3_cond_bk': (0.0, 0.1),
     'L3_cond_bout': (0.0, 0.8)}
    factors = {'L0_cond_W_mod': 5.186,
     'L0_cond_b_mod': 8.0,
     'L0_cond_W_qkv': 8.0,
     'L0_cond_W_out': 8.0,
     'L0_cond_b_out': 28.033,
     'L0_cond_W1': 6.841,
     'L0_cond_b1': 8.0,
     'L0_cond_W2': 6.716,
     'L0_cond_b2': 29.036,
     'L2_cond_W_ada': 3.09,
     'L2_cond_Wq': 8.0,
     'L2_cond_Wk': 8.0,
     'L2_cond_Wv': 8.0,
     'L2_cond_Wo': 8.0,
     'L2_cond_W1': 8.0,
     'L2_cond_W2': 7.421}
    for name, (base, spread) in spreads.items():
        noise = np.random.default_rng([zlib.crc32(name.encode()), seed]).standard_normal(out[name].shape)
        drawn = base * np.exp(spread * noise) if base else spread * noise
        out[name] = jnp.asarray(drawn.astype(out[name].dtype))
    for name, factor in factors.items():
        out[name] = (out[name] * factor).astype(out[name].dtype)
    return out
```

```python
from contextlib import ExitStack

import concourse.bass as bass
from concourse import mybir

F32 = mybir.dt.float32
I32 = mybir.dt.int32
ALU = mybir.AluOpType
ACT = mybir.ActivationFunctionType
AX = mybir.AxisListType

D = 128
B = 32
G = 4
NG = B // G
T = G * D
H0, DH0 = 16, 64
C0 = H0 * DH0 // D
H2, DH2 = 16, 8
FF = 4
NK3 = 20
L3 = 11
H3, DH3 = 16, 8
HC = 6
CH3 = [(0, 6), (6, 6), (12, 4)]
NEG = -9000000000000000.0
EPS = (1e-5, 1e-5, 1e-6, 1e-6, 1e-5, 1e-5)
RMS = (False, False, True, True, False, False)

BIAS_ROWS = [("L0_cond_b_mod", 6), ("L1_cond_film1_b", 2), ("L1_cond_film2_b", 2), ("L2_cond_b_ada", 6),
             ("L0_cond_b_out", 1), ("L0_cond_b1", 4), ("L0_cond_b2", 1), ("L1_cond_norm1_w", 1),
             ("L1_cond_norm2_w", 1), ("L1_cond_q_b", 1), ("L1_cond_k_b", 1), ("L1_cond_v_b", 1),
             ("L1_cond_proj_b", 1), ("L1_cond_mlp_b1", 4), ("L1_cond_mlp_b2", 1), ("L2_cond_bq", 1),
             ("L2_cond_bk", 1), ("L2_cond_bv", 1), ("L2_cond_bo", 1), ("L2_cond_b1", 4), ("L2_cond_b2", 1),
             ("L3_cond_b_self", 1), ("L3_cond_bq", 2), ("L3_cond_bk", 2), ("L3_cond_bout", 2)]
ROW = {}
_n = 0
for _name, _k in BIAS_ROWS:
    ROW[_name] = _n
    _n += _k
NROWS = _n
NMOD = 16
SHIFT = (0, 3, 7, 9, 10, 13)
SCALE = (1, 4, 6, 8, 11, 14)
GATE = {"o0": 2, "g0": 5, "o2": 12, "g2": 15}

U0 = G * H0 // 4
U1 = U0 + 1
NU = U1 + G * H2 // 4
NJ = 2 * G
DVE_LINKS = 26


class Ring:

    def __init__(self, nc, ctx, name, banks, uses):
        self.ps = [ctx.enter_context(nc.psum_tensor(f"{name}{i}", [D, T], F32)) for i in range(banks)]
        self.full = [ctx.enter_context(nc.semaphore(f"{name}{i}_full")) for i in range(banks)]
        self.free = [ctx.enter_context(nc.semaphore(f"{name}{i}_free")) for i in range(banks)]
        self.at = {u: (i % banks, i // banks) for i, u in enumerate(uses)}
        self.per = [len(range(b, len(uses), banks)) for b in range(banks)]

    def start(self, eng):
        for s in self.free:
            eng.sem_inc(s, 1)

    def bank(self, use):
        return self.ps[self.at[use][0]]

    def open(self, eng, it, use):
        b, n = self.at[use]
        eng.wait_ge(self.free[b], it * self.per[b] + n + 1)
        return self.ps[b]

    def filled(self, ins, use):
        ins.then_inc(self.full[self.at[use][0]], 1)

    def wait_full(self, eng, it, use):
        b, n = self.at[use]
        eng.wait_ge(self.full[b], it * self.per[b] + n + 1)
        return self.ps[b]

    def drained(self, ins, use):
        ins.then_inc(self.free[self.at[use][0]], 1)

    def wait_drained(self, eng, it, use):
        b, n = self.at[use]
        eng.wait_ge(self.free[b], it * self.per[b] + n + 2)

    def wait_all_drained(self, eng, it, uses):
        for u in {self.at[u][0]: u for u in uses}.values():
            self.wait_drained(eng, it, u)


class Count:

    def __init__(self, nc, ctx, name, per):
        self.sem = ctx.enter_context(nc.semaphore(name))
        self.per = per

    def wait(self, eng, it, n):
        eng.wait_ge(self.sem, it * self.per + n + 1)

    def up(self, ins):
        ins.then_inc(self.sem, 1)


class Chain:

    def __init__(self, nc, ctx, name, per):
        self.sem = ctx.enter_context(nc.semaphore(name))
        self.per = per
        self.n = 0

    def link(self, eng, it, ins):
        ins.then_inc(self.sem, 1)
        self.n += 1
        eng.wait_ge(self.sem, it * self.per + self.n)


def build(nc, t, out):
    misc = ["ln0"]
    for c in range(C0):
        misc += [f"q0_{c}", f"k0_{c}"]
    misc += [f"v0_{b}_{j}" for b in range(G) for j in range(2)]
    for l in range(3):
        if l:
            misc += [f"ln{2 * l}"] + ([f"q{l}", f"k{l}"] if l == 1 else [f"k{l}", f"q{l}"]) + [f"v{l}"]
        misc += [f"o{l}", f"y{l}", f"ln{2 * l + 1}"] + [f"f{l}_{c}" for c in range(FF)] + [f"g{l}", f"z{l}"]
    misc += ["adj", "xt3", "sum3", "self3", "q3_0", "q3_1", "k3"]
    misc += [f"vbd_{c}_{i}" for c in range(3) for i in range(G // 2)] + ["y3"]

    with ExitStack() as ctx:
        def sb(name, shape, dt=F32):
            return ctx.enter_context(nc.sbuf_tensor(name, shape, dt))

        def sem(name):
            return ctx.enter_context(nc.semaphore(name))

        def flat(ap):
            return ap.rearrange("p a b -> p (a b)")

        def count(name, per):
            return Count(nc, ctx, name, per)

        w_qkv = sb("w_qkv", [D, 3 * H0 * DH0])
        w_out = sb("w_out", [D, C0, D])
        w_up = sb("w_up", [D, 3, FF * D])
        w_down = sb("w_down", [D, 3, FF, D])
        w_l1 = sb("w_l1", [D, 4, D])
        w_l2 = sb("w_l2", [D, 4, D])
        w3 = sb("w3", [D, 8, D])
        bias_rows = sb("bias_rows", [NROWS, D])
        col = sb("col", [D, NROWS])
        cond = sb("cond", [B, 2, D])
        cond_raw = sb("cond_raw", [B, D])
        condT = sb("condT", [D, 2, B])
        mod = sb("mod", [D, NMOD, B])
        gmod = sb("gmod", [D, NMOD, G])
        gcond = sb("gcond", [D, G])
        bout3 = sb("bout3", [D, 1])
        ident = sb("ident", [D, D])
        ones = sb("ones", [D, D])
        held = sb("held", [D, 2])
        half = sb("half", [D, G])
        head16 = sb("head16", [D, H3])
        head4 = sb("head4", [D, 4])
        blk3 = sb("blk3", [HC * NK3, 3, H3, DH3])
        wlab = sb("wlab", [D, L3])
        blab = sb("blab", [D, 1])

        x_in = sb("x_in", [D, G, D])
        x = sb("x", [D, G, D])
        z = sb("z", [D, G, D])
        x_out = sb("x_out", [D, G, D])
        stats = sb("stats", [D, G, 6])
        mv = sb("mv", [D, G, 2])
        msq = sb("msq", [D, G])
        veps = sb("veps", [D, G])
        rstd = sb("rstd", [D, G])
        hT = sb("hT", [D, T])
        qT = sb("qT", [D, C0, T])
        kT = sb("kT", [D, C0, T])
        v0 = sb("v0", [D, G, H0 * DH0])
        attnT = sb("attnT", [D, C0, T])
        w_mod = attnT[:, 0:4, :].rearrange("p c (k d) -> p (c k) d", d=D)
        w3_raw = attnT[:, 4:6, :].rearrange("p c (k d) -> p (c k) d", d=D)
        oT = sb("oT", [D, T])
        hid = sb("hid", [D, FF, T])
        yT = sb("yT", [D, T])
        negmax = sb("negmax", [D, NU, 4])
        rsum = sb("rsum", [D, NU, 4])
        rinv = sb("rinv", [D, NU, 4])
        NP = 4
        probs = sb("probs", [D, NP, 4, D])
        probsT = sb("probsT", [D, NP, 4, D])
        v1 = sb("v1", [D, G, D])
        km = attnT[:, 0:4, :]
        VW = H2 * (D + DH2)
        vm = sb("vm", [D, G, VW])
        adj0 = sb("adj0", [D, G * NK3 * L3], I32)
        adj1 = sb("adj1", [G * NK3, D * L3], I32)
        adjf = flat(hid[:, :, :])[:, 0:D * L3]
        edge0 = sb("edge0", [D, 2, 2, G * NK3])
        edge1 = sb("edge1", [G * NK3, 2, D])
        keep = sb("keep", [D, 2, G * NK3])
        nbias = sb("nbias", [D, 2, G * NK3])
        sT = sb("sT", [D, T])
        x3T = qT[:, 6, :]
        qx = qT[:, 7, :]
        q3 = kT[:, 6:8, :]
        k3 = sb("k3", [D, 2, G * NK3])
        kbd = flat(kT[:, 1:6, :]).rearrange("p (d b h m) -> p d b h m", d=2, b=G, h=H3)
        kvrep = flat(attnT[:, 4:7, :])[:, 0:G * H3 * NK3].rearrange("p (b h m) -> p b h m", b=G, h=H3)
        vbd = flat(v0[0:HC * NK3, :, :])[:, 0:3 * G * 2 * D].rearrange("p (c b d g) -> p c b d g", c=3, b=G, d=2)
        p3 = flat(qT[:, 1:6, :]).rearrange("p (j h m) -> p j h m", j=NJ, h=H3)
        p3T = sb("p3T", [HC * NK3, 2, 3, D])
        nmax3 = sb("nmax3", [D, NJ, H3])
        rsum3 = sb("rsum3", [D, NJ, H3])
        rinv3 = sb("rinv3", [D, NJ, H3])
        relT = yT

        units = [("A", u) for u in range(NU)] + [("J", j) for j in range(NJ)]
        M = Ring(nc, ctx, "misc", 3, misc)
        S = Ring(nc, ctx, "scores", 2, units)
        PT = Ring(nc, ctx, "probsT_ps", 2, units)
        AT = Ring(nc, ctx, "attn_ps", 1, [("L0", p) for p in range(U0 // 2)] + ["L1", "L2", "L3"])

        weights_in = sem("weights_in")
        early_in = sem("early_in")
        pool_setup = sem("pool_setup")
        consts_ready = sem("consts_ready")
        silu_ready = sem("silu_ready")
        dve_setup = sem("dve_setup")
        pe_setup = sem("pe_setup")
        setup_done = sem("setup_done")
        x_loaded = sem("x_loaded")
        adj_loaded = sem("adj_loaded")
        x_stored = sem("x_stored")
        adj_taken = count("adj_taken", 2)
        var_ready = count("var_ready", 6)
        rstd_ready = count("rstd_ready", 6)
        z_ready = count("z_ready", 6)
        max_ready = count("max_ready", NU)
        rinv_ready = count("rinv_ready", NU)
        normed = count("normed", NU)
        km_ready = count("km_ready", G)
        adjf_ready = count("adjf_ready", 2)
        adjw_ready = count("adjw_ready", 2)
        adj_summed = count("adj_summed", 2)
        adjf_free = count("adjf_free", 1)
        edge1_ready = count("edge1_ready", 1)
        kbd_ready = count("kbd_ready", 2)
        kvrep_ready = count("kvrep_ready", 1)
        bias_ready = count("bias_ready", 1)
        biased3 = count("biased3", NJ)
        max3_ready = count("max3_ready", NJ)
        shifted3 = count("shifted3", NJ)
        exp3_ready = count("exp3_ready", NJ)
        rinv3_ready = count("rinv3_ready", NJ)
        normed3 = count("normed3", NJ)
        rel_ready = count("rel_ready", 1)
        dve_chain = Chain(nc, ctx, "dve_chain", DVE_LINKS)

        def wide(ap, n):
            p, a = ap.shape
            return ap.unsqueeze(2).to_broadcast([p, a, n])

        def tok(b):
            return slice(b * D, (b + 1) * D)

        EARLY = [0]
        block = ctx.enter_context(nc.Block())

        @block.sync
        def _(sp):
            def early(dst, src):
                sp.dma_start(dst, src).then_inc(early_in, 16)
                EARLY[0] += 16

            r = 0
            early(cond_raw[:, :], t["cond_1024"])
            for name, k in BIAS_ROWS:
                src = t[name]
                src = src if len(src.shape) == 2 else src.rearrange("(k d) -> k d", d=D)
                early(bias_rows[r:r + k, :], src)
                r += k
            m = 0
            for name in ("L0_cond_W_mod", "L1_cond_film1_w", "L1_cond_film2_w", "L2_cond_W_ada"):
                k = t[name].shape[1] // D
                early(w_mod[:, m:m + k, :], t[name].rearrange("i (k d) -> i k d", d=D))
                m += k
            early(w3_raw[:, 0:2, :], t["L3_cond_W_self"].rearrange("o (k i) -> o k i", i=D))
            early(w3_raw[:, 2:4, :], t["L3_cond_Wq"].rearrange("d o i -> o d i"))
            early(w3_raw[:, 4:6, :], t["L3_cond_Wk"].rearrange("d o i -> o d i"))
            early(w3_raw[:, 6:8, :], t["L3_cond_Wout"].rearrange("d h g i -> (h g) d i"))
            early(wlab[:, :], t["L3_cond_w_bias"].rearrange("(a l) -> a l", a=1).to_broadcast([D, L3]))
            early(blab[:, :], t["L3_cond_b_bias"].rearrange("(a l) -> a l", a=1).to_broadcast([D, 1]))

            mask = t["mask_BxSxSx11_ik0"]

            def load_x(g):
                sp.dma_start(x_in[:, :, :], t["x"][bass.ds(g * G, G)].rearrange("b t d -> t b d")).then_inc(x_loaded, 16)

            def load_edges(g):
                sp.dma_start(adj0[:, :].rearrange("n (b k) -> n b k", b=G),
                             mask[bass.ds(g * G, G), :, 0:NK3, :].rearrange("b n m l -> n b (m l)")).then_inc(adj_loaded, 16)
                for b in range(G):
                    sp.dma_start(adj1[b * NK3:(b + 1) * NK3, :],
                                 mask[bass.ds(g * G + b, 1), 0:NK3, :, :].rearrange("b m n l -> (b m) (n l)")).then_inc(adj_loaded, 16)

            def store(g):
                M.wait_drained(sp, g, "y3")
                sp.dma_start(out[bass.ds(g * G, G)].rearrange("b t d -> t b d"), x_out[:, :, :]).then_inc(x_stored, 16)

            load_x(0)
            load_edges(0)
            with sp.Fori(0, NG - 1) as it:
                adj_taken.wait(sp, it, 1)
                load_edges(it + 1)
                M.wait_drained(sp, it, "y0")
                load_x(it + 1)
                store(it)
            store(NG - 1)
            sp.wait_ge(x_stored, 16 * NG + 16)

        NWEIGHTS = 1 + 1 + 3 + 3 + 4 + 4

        @block.gpsimd
        def _(pool):
            n = [0]

            def step(ins):
                ins.then_inc(pool_setup, 1)
                n[0] += 1
                pool.wait_ge(pool_setup, n[0])

            step(pool.memset(ident[:, :], 0.0))
            step(pool.affine_select(out=ident[:, :], in_=ident[:, :], compare_op=ALU.not_equal, fill=1.0,
                                    base=0, pattern=[[-1, D]], channel_multiplier=1))
            step(pool.memset(ones[:, :], 1.0))
            step(pool.memset(half[:, :], -0.5))
            step(pool.memset(vm[:, :, :], 0.0))
            step(pool.memset(head16[:, :], 1.0))
            step(pool.affine_select(out=head16[:, :], in_=head16[:, :], compare_op=ALU.is_ge, fill=0.0,
                                    base=0, pattern=[[-DH3, H3]], channel_multiplier=1))
            step(pool.affine_select(out=head16[:, :], in_=head16[:, :], compare_op=ALU.is_ge, fill=0.0,
                                    base=DH3 - 1, pattern=[[DH3, H3]], channel_multiplier=-1))
            step(pool.memset(blk3[:, :, :, :], 1.0))
            step(pool.affine_select(out=blk3[:, :, :, :], in_=blk3[:, :, :, :], compare_op=ALU.is_ge, fill=0.0,
                                    base=0, pattern=[[HC * NK3, 3], [-NK3, H3], [0, DH3]], channel_multiplier=1))
            pool.affine_select(out=blk3[:, :, :, :], in_=blk3[:, :, :, :], compare_op=ALU.is_ge, fill=0.0,
                               base=NK3 - 1, pattern=[[-HC * NK3, 3], [NK3, H3], [0, DH3]],
                               channel_multiplier=-1).then_inc(consts_ready, 1)
            pool.wait_ge(setup_done, 1)

            with pool.Fori(0, NG) as it:
                def rsqrt(k):
                    var_ready.wait(pool, it, k)
                    rstd_ready.up(pool.tensor_tensor(rstd[:, :], veps[:, :], half[:, :], ALU.pow))

                def norm(u):
                    rinv_ready.wait(pool, it, u)
                    p = probs[:, u % NP, :, :]
                    normed.up(pool.tensor_tensor(p, p, wide(rinv[:, u, :], D), ALU.mult))

                rsqrt(0)
                pool.wait_ge(adj_loaded, it * (16 * (1 + G)) + 16 * (1 + G))
                for d, (src, P, N) in enumerate(((adj0, D, G * NK3 * L3), (adj1, G * NK3, D * L3))):
                    if d:
                        adjf_free.wait(pool, it, 0)
                    pool.tensor_tensor(held[:, 1:2], half[:, 0:1], half[:, 1:2], ALU.mult)
                    ins = pool.tensor_copy(adjf[0:P, 0:N], src[0:P, 0:N])
                    ins.then_inc(adj_taken.sem, 1)
                    adj_summed.wait(pool, it, d)
                    f3 = adjf[0:P, 0:N].rearrange("p (a l) -> p a l", l=L3)
                    wl = wlab[0:P, :].unsqueeze(1).to_broadcast([P, N // L3, L3])
                    adjw_ready.up(pool.tensor_tensor(f3, f3, wl, ALU.mult))
                for u in range(U0):
                    norm(u)
                rsqrt(1)
                rsqrt(2)
                norm(U0)
                rsqrt(3)
                rsqrt(4)
                M.wait_drained(pool, it, "k2")
                for b in range(G):
                    kb = kT[:, 0, tok(b)].unsqueeze(1).to_broadcast([D, 4, D])
                    km_ready.up(pool.tensor_tensor(km[:, :, tok(b)], kb, wide(head4[:, :], D), ALU.mult))
                for u in range(U1, NU):
                    norm(u)
                rsqrt(5)
                M.wait_drained(pool, it, "k3")
                for d in range(2):
                    for b in range(G):
                        kk = k3[:, d, b * NK3:(b + 1) * NK3].unsqueeze(1).to_broadcast([D, H3, NK3])
                        ins = pool.tensor_tensor(kbd[:, d, b, :, :], kk, wide(head16[:, :], NK3), ALU.mult)
                    kbd_ready.up(ins)
                bias_ready.wait(pool, it, 0)
                for j in range(NJ):
                    S.wait_drained(pool, it, ("J", j))
                    d, b = j // G, j % G
                    nb = nbias[:, d, b * NK3:(b + 1) * NK3].unsqueeze(1).to_broadcast([D, H3, NK3])
                    biased3.up(pool.tensor_tensor(p3[:, j, :, :], p3[:, j, :, :], nb, ALU.add))
                for j in range(NJ):
                    max3_ready.wait(pool, it, j)
                    shifted3.up(pool.tensor_tensor(p3[:, j, :, :], p3[:, j, :, :], wide(nmax3[:, j, :], NK3), ALU.add))
                for j in range(NJ):
                    rinv3_ready.wait(pool, it, j)
                    normed3.up(pool.tensor_tensor(p3[:, j, :, :], p3[:, j, :, :], wide(rinv3[:, j, :], NK3), ALU.mult))

        @block.scalar
        def _(act):
            for dst, src in ((w_qkv[:, :], t["L0_cond_W_qkv"]),
                             (w_out[:, :, :], t["L0_cond_W_out"].rearrange("(c p) d -> p c d", p=D))):
                act.dma_start(dst, src).then_inc(weights_in, 16)
            for i, w in enumerate(("L1_cond_q_w", "L1_cond_k_w", "L1_cond_v_w", "L1_cond_proj_w")):
                act.dma_start(w_l1[:, i, :], t[w]).then_inc(weights_in, 16)
            for i, w in enumerate(("L2_cond_Wq", "L2_cond_Wk", "L2_cond_Wv", "L2_cond_Wo")):
                act.dma_start(w_l2[:, i, :], t[w]).then_inc(weights_in, 16)
            for i, (up, down) in enumerate((("L0_cond_W1", "L0_cond_W2"), ("L1_cond_mlp_w1", "L1_cond_mlp_w2"),
                                            ("L2_cond_W1", "L2_cond_W2"))):
                act.dma_start(w_up[:, i, :], t[up]).then_inc(weights_in, 16)
                act.dma_start(w_down[:, i, :, :], t[down].rearrange("(c p) d -> p c d", p=D)).then_inc(weights_in, 16)
            act.wait_ge(early_in, EARLY[0])
            act.activation(cond[:, 0, :], cond_raw[:, :], ACT.Silu).then_inc(silu_ready, 1)
            act.activation(cond[:, 1, :], cond_raw[:, :], ACT.Copy).then_inc(silu_ready, 1)
            act.wait_ge(setup_done, 1)

            with act.Fori(0, NG) as it:
                def biased(use, dst, b):
                    ps = M.wait_full(act, it, use)
                    M.drained(act.activation(dst, ps[:, :], ACT.Identity, bias=col[:, b:b + 1]), use)

                def copied(use, dst):
                    ps = M.wait_full(act, it, use)
                    M.drained(act.activation(dst, ps[:, :], ACT.Copy), use)

                def exps(u):
                    max_ready.wait(act, it, u)
                    if u >= NP:
                        PT.wait_full(act, it, ("A", u - NP))
                    ps = S.bank(("A", u))
                    for i in range(4):
                        ins = act.activation(probs[:, u % NP, i, :], ps[:, i * D:(i + 1) * D], ACT.Exp,
                                             bias=negmax[:, u, i:i + 1], accum_out=rsum[:, u, i:i + 1])
                    S.drained(ins, ("A", u))

                def gelus(l, b1):
                    for c in range(FF):
                        ps = M.wait_full(act, it, f"f{l}_{c}")
                        M.drained(act.activation(hid[:, c, :], ps[:, :], ACT.Gelu, bias=col[:, b1 + c:b1 + c + 1]), f"f{l}_{c}")

                for c in range(C0):
                    copied(f"k0_{c}", kT[:, c, :])
                for b in range(G):
                    copied(f"v0_{b}_1", v0[:, b, T:2 * T])
                for u in range(U0):
                    exps(u)
                gelus(0, ROW["L0_cond_b1"])
                biased("k1", kT[:, 0, :], ROW["L1_cond_k_b"])
                exps(U0)
                gelus(1, ROW["L1_cond_mlp_b1"])
                biased("k2", kT[:, 0, :], ROW["L2_cond_bk"])
                for u in range(U1, NU):
                    exps(u)
                gelus(2, ROW["L2_cond_b1"])
                copied("xt3", x3T[:, :])
                for j in range(NJ):
                    shifted3.wait(act, it, j)
                    exp3_ready.up(act.activation(p3[:, j, :, :], p3[:, j, :, :], ACT.Exp))

        @block.tensor
        def _(pe):
            pe.wait_ge(consts_ready, 1)
            pe.wait_ge(early_in, EARLY[0])
            for i in range(8):
                ins = pe.transpose(M.ps[i // 4][:, tok(i % 4)], w3_raw[:, i, :], ident[:, :])
            pe.transpose(M.ps[2][:, 0:NROWS], bias_rows[:, :], ident[0:NROWS, 0:NROWS])
            pe.wait_ge(silu_ready, 2)
            for i in range(2):
                ins = pe.transpose(M.ps[2][:, D + i * B:D + (i + 1) * B], cond[:, i, :], ident[0:B, 0:B])
            ins.then_inc(pe_setup, 1)
            pe.wait_ge(dve_setup, 3)
            for m in range(NMOD):
                ins = pe.matmul(S.ps[0][:, m * B:(m + 1) * B], w_mod[:, m, :], condT[:, 0 if m < 6 else 1, :],
                                start=True, stop=True)
            ins.then_inc(pe_setup, 1)
            pe.wait_ge(weights_in, 16 * NWEIGHTS)
            for ring in (M, S, PT, AT):
                ring.start(pe)
            pe.wait_ge(setup_done, 1)

            with pe.Fori(0, NG) as it:
                def turn(use, src, ready=None):
                    ps = M.open(pe, it, use)
                    for b in range(G):
                        ins = pe.transpose(ps[:, tok(b)], src[:, b, :] if len(src.shape) == 3 else src[:, tok(b)], ident[:, :])
                    M.filled(ins, use)

                def linear(use, terms):
                    ps = M.open(pe, it, use)
                    for i, (w, a) in enumerate(terms):
                        ins = pe.matmul(ps[:, :], w, a, start=(i == 0), stop=(i == len(terms) - 1))
                    M.filled(ins, use)

                def norm_turn(k):
                    z_ready.wait(pe, it, k)
                    turn(f"ln{k}", z)
                    M.wait_drained(pe, it, f"ln{k}")

                def probs_turn(u):
                    normed.wait(pe, it, u)
                    ps = PT.open(pe, it, ("A", u))
                    for i in range(4):
                        ins = pe.transpose(ps[:, tok(i)], probs[:, u % NP, i, :], ident[:, :])
                    PT.filled(ins, ("A", u))

                def back(use, turned):
                    M.wait_drained(pe, it, use)
                    turn(turned, yT)

                def mlp(l):
                    norm_turn(2 * l + 1)
                    for c in range(FF):
                        linear(f"f{l}_{c}", [(w_up[:, l, tok(c)], hT[:, :])])
                    M.wait_all_drained(pe, it, [f"f{l}_{c}" for c in range(FF)])
                    linear(f"g{l}", [(w_down[:, l, c, :], hid[:, c, :]) for c in range(FF)])
                    back(f"g{l}", f"z{l}")

                norm_turn(0)
                for c in range(C0):
                    linear(f"q0_{c}", [(w_qkv[:, tok(c)], hT[:, :])])
                    linear(f"k0_{c}", [(w_qkv[:, tok(C0 + c)], hT[:, :])])
                for b in range(G):
                    for j in range(2):
                        c0 = 2 * H0 * DH0 + j * T
                        linear(f"v0_{b}_{j}", [(hT[:, tok(b)], w_qkv[:, c0:c0 + T])])
                M.wait_all_drained(pe, it, [f"v0_{b}_{j}" for b in range(G) for j in range(2)])

                def scores0(u):
                    b, hf, r = u // 4, u // 2 % 2, u % 2
                    rows = slice(r * DH0, (r + 1) * DH0)
                    ps = S.open(pe, it, ("A", u))
                    for i in range(4):
                        ins = pe.matmul(ps[:, tok(i)], qT[rows, 4 * hf + i, tok(b)], kT[rows, 4 * hf + i, tok(b)],
                                        start=True, stop=True)
                    S.filled(ins, ("A", u))

                def values0(p):
                    b, hf = p // 2, p % 2
                    PT.wait_drained(pe, it, ("A", 2 * p))
                    PT.wait_drained(pe, it, ("A", 2 * p + 1))
                    ps = AT.open(pe, it, ("L0", p))
                    for i in range(4):
                        for r in range(2):
                            h = 2 * (4 * hf + i) + r
                            ins = pe.matmul(ps[r * DH0:(r + 1) * DH0, tok(i)], v0[:, b, h * DH0:(h + 1) * DH0],
                                            probsT[:, (2 * p + r) % NP, i, :], start=True, stop=True)
                    AT.filled(ins, ("L0", p))

                for s in range(U0 + 5):
                    if s < U0:
                        scores0(s)
                    if 0 <= s - 3 < U0:
                        probs_turn(s - 3)
                    if s >= 5 and s % 2 == 1 and (s - 5) // 2 < U0 // 2:
                        values0((s - 5) // 2)
                AT.wait_drained(pe, it, ("L0", U0 // 2 - 1))
                linear("o0", [(w_out[:, c, :], attnT[:, c, :]) for c in range(C0)])
                back("o0", "y0")
                mlp(0)

                norm_turn(2)
                linear("q1", [(w_l1[:, 0, :], hT[:, :])])
                linear("k1", [(w_l1[:, 1, :], hT[:, :])])
                for l, w in ((1, w_l1),):
                    ps = M.open(pe, it, "v1")
                    for b in range(G):
                        ins = pe.matmul(ps[:, tok(b)], hT[:, tok(b)], w[:, 2, :], start=True, stop=True)
                    M.filled(ins, "v1")
                M.wait_drained(pe, it, "q1")
                M.wait_drained(pe, it, "k1")
                ps = S.open(pe, it, ("A", U0))
                for b in range(G):
                    ins = pe.matmul(ps[:, tok(b)], qT[:, 0, tok(b)], kT[:, 0, tok(b)], start=True, stop=True)
                S.filled(ins, ("A", U0))
                probs_turn(U0)
                PT.wait_drained(pe, it, ("A", U0))
                M.wait_drained(pe, it, "v1")
                ps = AT.open(pe, it, "L1")
                for b in range(G):
                    ins = pe.matmul(ps[:, tok(b)], v1[:, b, :], probsT[:, U0 % NP, b, :], start=True, stop=True)
                AT.filled(ins, "L1")
                AT.wait_drained(pe, it, "L1")
                linear("o1", [(w_l1[:, 3, :], oT[:, :])])
                back("o1", "y1")
                mlp(1)

                norm_turn(4)
                linear("k2", [(w_l2[:, 1, :], hT[:, :])])
                linear("q2", [(w_l2[:, 0, :], hT[:, :])])
                ps = M.open(pe, it, "v2")
                for b in range(G):
                    ins = pe.matmul(ps[:, tok(b)], hT[:, tok(b)], w_l2[:, 2, :], start=True, stop=True)
                M.filled(ins, "v2")
                M.wait_drained(pe, it, "q2")
                M.wait_drained(pe, it, "v2")

                def scores2(u):
                    b, s = (u - U1) // 4, (u - U1) % 4
                    rows = slice(32 * s, 32 * s + 32)
                    if s == 0:
                        km_ready.wait(pe, it, b)
                    ps = S.open(pe, it, ("A", u))
                    S.filled(pe.matmul(ps[:, :], qT[rows, 0, tok(b)], km[rows, :, tok(b)], start=True, stop=True), ("A", u))

                def values2(u):
                    b, s = (u - U1) // 4, (u - U1) % 4
                    PT.wait_drained(pe, it, ("A", u))
                    ps = AT.open(pe, it, "L2") if u == U1 else AT.bank("L2")
                    for i in range(4):
                        h = 4 * s + i
                        ins = pe.matmul(ps[:, tok(b)], vm[:, b, h * D:(h + 1) * D], probsT[:, u % NP, i, :],
                                        start=(h == 0), stop=(h == H2 - 1))
                    if u == NU - 1:
                        AT.filled(ins, "L2")

                for s in range(U1, NU + 4):
                    if s < NU:
                        scores2(s)
                    if U1 <= s - 3 < NU:
                        probs_turn(s - 3)
                    if U1 <= s - 4 < NU:
                        values2(s - 4)
                AT.wait_drained(pe, it, "L2")
                linear("o2", [(w_l2[:, 3, :], oT[:, :])])
                back("o2", "y2")
                mlp(2)

                edge1_ready.wait(pe, it, 0)
                ps = M.open(pe, it, "adj")
                for i in range(2):
                    ins = pe.transpose(ps[:, i * G * NK3:(i + 1) * G * NK3], edge1[:, i, :], ident[0:G * NK3, 0:G * NK3])
                M.filled(ins, "adj")
                M.wait_drained(pe, it, "z2")
                turn("xt3", x)
                M.wait_drained(pe, it, "xt3")
                linear("sum3", [(ones[:, :], x3T[:, :])])
                M.wait_drained(pe, it, "sum3")
                linear("self3", [(w3[:, 0, :], x3T[:, :]), (w3[:, 1, :], qx[:, :])])
                M.wait_drained(pe, it, "self3")
                for d in range(2):
                    linear(f"q3_{d}", [(w3[:, 2 + d, :], sT[:, :])])
                ps = M.open(pe, it, "k3")
                for d in range(2):
                    ins = pe.matmul(ps[:, d * G * NK3:(d + 1) * G * NK3], w3[:, 4 + d, :],
                                    sT[:, :].rearrange("p (b n) -> p b n", b=G)[:, :, 0:NK3], start=True, stop=True)
                M.filled(ins, "k3")
                kvrep_ready.wait(pe, it, 0)
                for c, (h0, nh) in enumerate(CH3):
                    rows = nh * NK3
                    for i in range(G // 2):
                        ps = M.open(pe, it, f"vbd_{c}_{i}")
                        for b2 in range(2):
                            kv = kvrep[:, 2 * i + b2, h0:h0 + nh, :].rearrange("p h m -> p (h m)")
                            ins = pe.matmul(ps[0:rows, b2 * 2 * D:(b2 + 1) * 2 * D], kv,
                                            w3[:, 6:8, :].rearrange("p d g -> p (d g)"), start=True, stop=True)
                        M.filled(ins, f"vbd_{c}_{i}")
                for j in range(NJ):
                    d, b = j // G, j % G
                    kbd_ready.wait(pe, it, d)
                    ps = S.open(pe, it, ("J", j))
                    S.filled(pe.matmul(ps[:, 0:H3 * NK3], q3[:, d, tok(b)],
                                       kbd[:, d, b, :, :].rearrange("p h m -> p (h m)"), start=True, stop=True), ("J", j))
                M.wait_all_drained(pe, it, [f"vbd_{c}_{i}" for c in range(3) for i in range(G // 2)])
                order = [d * G + b for b in range(G) for d in range(2)]
                for n in range(NJ + 1):
                    if n < NJ:
                        j = order[n]
                        normed3.wait(pe, it, j)
                        ps = PT.open(pe, it, ("J", n))
                        for c, (h0, nh) in enumerate(CH3):
                            ins = pe.transpose(ps[0:nh * NK3, tok(c)],
                                               p3[:, j, h0:h0 + nh, :].rearrange("p h m -> p (h m)"), ident[:, :])
                        PT.filled(ins, ("J", n))
                    if n >= 1:
                        d, b = order[n - 1] // G, order[n - 1] % G
                        PT.wait_drained(pe, it, ("J", n - 1))
                        ps = AT.open(pe, it, "L3") if n == 1 else AT.bank("L3")
                        for c, (h0, nh) in enumerate(CH3):
                            rows = nh * NK3
                            ins = pe.matmul(ps[:, tok(b)], vbd[0:rows, c, b, d, :], p3T[0:rows, (n - 1) % 2, c, :],
                                            start=(d == 0 and c == 0), stop=(d == 1 and c == 2))
                AT.filled(ins, "L3")
                rel_ready.wait(pe, it, 0)
                turn("y3", relT)

        @block.vector
        def _(dve):
            def setup_step(ins):
                ins.then_inc(dve_setup, 1)

            dve.wait_ge(pe_setup, 1)
            setup_step(dve.tensor_copy(condT[:, :, :], M.ps[2][:, D:D + 2 * B].rearrange("p (a b) -> p a b", a=2)))
            setup_step(dve.tensor_copy(col[:, :], M.ps[2][:, 0:NROWS]))
            for i in range(2):
                ins = dve.tensor_copy(w3[:, 4 * i:4 * i + 4, :], M.ps[i][:, :].rearrange("p (a b) -> p a b", a=4))
            setup_step(ins)
            dve.wait_ge(pe_setup, 2)
            dve.wait_ge(dve_setup, 3)
            setup_step(dve.tensor_tensor(mod[:, :, :], S.ps[0][:, :].rearrange("p (m b) -> p m b", m=NMOD),
                                         wide(col[:, 0:NMOD], B), ALU.add))
            dve.wait_ge(dve_setup, 4)
            for k in range(6):
                m = SCALE[k]
                if RMS[k]:
                    w = ROW["L1_cond_norm1_w"] + (k - 2)
                    dve.tensor_scalar(mod[:, m, :], mod[:, m, :], 1.0, col[:, w:w + 1], ALU.add, ALU.mult)
                else:
                    dve.tensor_scalar(mod[:, m, :], mod[:, m, :], 1.0, None, ALU.add)
            dve.wait_ge(consts_ready, 1)
            dve.tensor_reduce(head4[:, :], head16[:, :].rearrange("p (s h) -> p h s", h=4), AX.X, ALU.add)
            r = ROW["L3_cond_bout"]
            dve.tensor_tensor(bout3[:, :], col[:, r:r + 1], col[:, r + 1:r + 2], ALU.add).then_inc(setup_done, 1)
            dve.wait_ge(setup_done, 1)
            dve.sem_inc(x_stored, 16)

            with dve.Fori(0, NG) as it:
                dve_chain.n = 0

                def link(ins):
                    dve_chain.link(dve, it, ins)

                def norm(k, src):
                    for b in range(G):
                        ins = dve.bn_stats(stats[:, b, :], src[:, b, :])
                    link(ins)
                    dve.memset(held[:, 0:1], 0.0)
                    for b in range(G):
                        ins = dve.bn_aggr(mv[:, b, :], stats[:, b, :])
                    link(ins)
                    if RMS[k]:
                        link(dve.tensor_tensor(msq[:, :], mv[:, :, 0], mv[:, :, 0], ALU.mult))
                        ins = dve.scalar_tensor_tensor(veps[:, :], mv[:, :, 1], EPS[k], msq[:, :], ALU.add, ALU.add)
                    else:
                        ins = dve.tensor_scalar(veps[:, :], mv[:, :, 1], EPS[k], None, ALU.add)
                    var_ready.up(ins)
                    rstd_ready.wait(dve, it, k)
                    for b in range(G):
                        if RMS[k]:
                            ins = dve.tensor_scalar(z[:, b, :], src[:, b, :], rstd[:, b:b + 1], None, ALU.mult)
                        else:
                            ins = dve.tensor_scalar(z[:, b, :], src[:, b, :], mv[:, b, 0:1], rstd[:, b:b + 1],
                                                    ALU.subtract, ALU.mult)
                    z_ready.up(ins)
                    ps = M.wait_full(dve, it, f"ln{k}")
                    for b in range(G):
                        ins = dve.tensor_scalar(hT[:, tok(b)], ps[:, tok(b)], modcol(SCALE[k], b), modcol(SHIFT[k], b),
                                                ALU.mult, ALU.add)
                    M.drained(ins, f"ln{k}")

                def modcol(m, b):
                    return gmod[:, m, b:b + 1]

                def gated(use, bias):
                    ps = M.wait_full(dve, it, use)
                    for b in range(G):
                        ins = dve.tensor_scalar(yT[:, tok(b)], ps[:, tok(b)], col[:, bias:bias + 1], modcol(GATE[use], b),
                                                ALU.add, ALU.mult)
                    M.drained(ins, use)

                def plus_bias(use, dst, bias):
                    ps = M.wait_full(dve, it, use)
                    M.drained(dve.tensor_scalar(dst, ps[:, :], col[:, bias:bias + 1], None, ALU.add), use)

                def scaled_q(use, dst, bias, scale):
                    ps = M.wait_full(dve, it, use)
                    M.drained(dve.tensor_scalar(dst, ps[:, :], col[:, bias:bias + 1], scale, ALU.add, ALU.mult), use)

                def residual(use, src):
                    ps = M.wait_full(dve, it, use)
                    ins = dve.tensor_tensor(flat(x[:, :, :]), ps[:, :], flat(src[:, :, :]), ALU.add)
                    M.drained(ins, use)
                    M.wait_drained(dve, it, use)

                def row_max(u):
                    ps = S.wait_full(dve, it, ("A", u))
                    max_ready.up(dve.tensor_reduce(negmax[:, u, :], ps[:, :].rearrange("p (h k) -> p h k", h=4), AX.X,
                                                   ALU.max, negate=True))

                def inverse(u):
                    S.wait_drained(dve, it, ("A", u))
                    rinv_ready.up(dve.reciprocal(rinv[:, u, :], rsum[:, u, :]))

                def probs_out(u):
                    ps = PT.wait_full(dve, it, ("A", u))
                    PT.drained(dve.tensor_copy(flat(probsT[:, u % NP, :, :]), ps[:, :]), ("A", u))

                link(dve.tensor_copy(gmod[:, :, :], mod[:, :, bass.ds(it * G, G)]))
                link(dve.tensor_copy(gcond[:, :], condT[:, 1, bass.ds(it * G, G)]))
                dve.wait_ge(x_loaded, it * 16 + 16)

                norm(0, x_in)
                for d, (P, N) in enumerate(((D, G * NK3 * L3), (G * NK3, D * L3))):
                    f3 = adjf[0:P, 0:N].rearrange("p (a l) -> p a l", l=L3)
                    dst = edge0[:, :, 0, :] if d == 0 else edge1[:, :, :]
                    dve.wait_ge(adj_taken.sem, it * 2 + d + 1)
                    adj_summed.up(dve.tensor_reduce(dst[:, 0, :], f3, AX.X, ALU.add))
                    if d == 0:
                        for c in range(4):
                            ps = M.wait_full(dve, it, f"q0_{c}")
                            M.drained(dve.tensor_scalar(qT[:, c, :], ps[:, :], DH0 ** -0.5, None, ALU.mult), f"q0_{c}")
                    else:
                        for c in range(4, C0):
                            ps = M.wait_full(dve, it, f"q0_{c}")
                            M.drained(dve.tensor_scalar(qT[:, c, :], ps[:, :], DH0 ** -0.5, None, ALU.mult), f"q0_{c}")
                        for b in range(G):
                            ps = M.wait_full(dve, it, f"v0_{b}_0")
                            M.drained(dve.tensor_copy(v0[:, b, 0:T], ps[:, :]), f"v0_{b}_0")
                    adjw_ready.wait(dve, it, d)
                    ins = dve.tensor_reduce(dst[:, 1, :], f3, AX.X, ALU.add)
                    (adjf_free if d == 0 else edge1_ready).up(ins)
                for s in range(U0 + 6):
                    if s < U0:
                        row_max(s)
                    if 0 <= s - 1 < U0:
                        inverse(s - 1)
                    if 0 <= s - 4 < U0:
                        probs_out(s - 4)
                    if s >= 6 and s % 2 == 0 and (s - 6) // 2 < U0 // 2:
                        p = (s - 6) // 2
                        ps = AT.wait_full(dve, it, ("L0", p))
                        AT.drained(dve.tensor_copy(attnT[:, 4 * (p % 2):4 * (p % 2) + 4, tok(p // 2)],
                                                   ps[:, :].rearrange("p (c q) -> p c q", c=4)), ("L0", p))
                gated("o0", ROW["L0_cond_b_out"])
                ps = M.wait_full(dve, it, "y0")
                ins = dve.tensor_tensor(flat(x[:, :, :]), ps[:, :], flat(x_in[:, :, :]), ALU.add)
                M.drained(ins, "y0")
                M.wait_drained(dve, it, "y0")
                norm(1, x)
                gated("g0", ROW["L0_cond_b2"])
                residual("z0", x)

                norm(2, x)
                scaled_q("q1", qT[:, 0, :], ROW["L1_cond_q_b"], D ** -0.5)
                ps = M.wait_full(dve, it, "v1")
                M.drained(dve.tensor_copy(flat(v1[:, :, :]), ps[:, :]), "v1")
                row_max(U0)
                inverse(U0)
                probs_out(U0)
                ps = AT.wait_full(dve, it, "L1")
                c = ROW["L1_cond_v_b"]
                AT.drained(dve.tensor_scalar(oT[:, :], ps[:, :], col[:, c:c + 1], None, ALU.add), "L1")
                plus_bias("o1", yT[:, :], ROW["L1_cond_proj_b"])
                residual("y1", x)
                norm(3, x)
                plus_bias("g1", yT[:, :], ROW["L1_cond_mlp_b2"])
                residual("z1", x)

                norm(4, x)
                scaled_q("q2", qT[:, 0, :], ROW["L2_cond_bq"], DH2 ** -0.5)
                ps = M.wait_full(dve, it, "v2")
                for b in range(G):
                    ins = dve.tensor_copy(vm[:, b, :].rearrange("p (h e) -> p h e", h=H2)[:, :, 0:DH2],
                                          ps[:, tok(b)].rearrange("p (h e) -> p h e", h=H2))
                M.drained(ins, "v2")
                for s in range(U1, NU + 4):
                    if s < NU:
                        row_max(s)
                    if U1 <= s - 1 < NU:
                        inverse(s - 1)
                    if U1 <= s - 4 < NU:
                        probs_out(s - 4)
                ps = AT.wait_full(dve, it, "L2")
                c = ROW["L2_cond_bv"]
                AT.drained(dve.tensor_scalar(oT[:, :], ps[:, :], col[:, c:c + 1], None, ALU.add), "L2")
                gated("o2", ROW["L2_cond_bo"])
                residual("y2", x)
                norm(5, x)
                gated("g2", ROW["L2_cond_b2"])
                residual("z2", x)

                ps = M.wait_full(dve, it, "adj")
                ins = dve.tensor_copy(edge0[:, :, 1, :], ps[:, 0:2 * G * NK3].rearrange("p (a e) -> p a e", a=2))
                M.drained(ins, "adj")
                M.wait_drained(dve, it, "adj")
                link(dve.tensor_scalar(keep[:, :, :], edge0[:, 0, :, :], 0.0, None, ALU.is_gt))
                link(dve.tensor_scalar(nbias[:, :, :], keep[:, :, :], -NEG, NEG, ALU.mult, ALU.add))
                bias_ready.up(dve.scalar_tensor_tensor(nbias[:, :, :], edge0[:, 1, :, :], blab[:, 0:1], nbias[:, :, :],
                                                       ALU.add, ALU.add))
                ps = M.wait_full(dve, it, "sum3")
                for b in range(G):
                    ins = dve.tensor_scalar(qx[:, tok(b)], ps[:, tok(b)], 0.0, gcond[:, b:b + 1], ALU.not_equal, ALU.mult)
                M.drained(ins, "sum3")
                plus_bias("self3", sT[:, :], ROW["L3_cond_b_self"])
                M.wait_drained(dve, it, "self3")
                kv = sT[:, :].rearrange("p (b n) -> p b n", b=G)[:, :, 0:NK3]
                for b in range(G):
                    ins = dve.tensor_copy(kvrep[:, b, :, :], kv[:, b, :].unsqueeze(1).to_broadcast([D, H3, NK3]))
                kvrep_ready.up(ins)
                for d in range(2):
                    scaled_q(f"q3_{d}", q3[:, d, :], ROW["L3_cond_bq"] + d, DH3 ** -0.5)
                ps = M.wait_full(dve, it, "k3")
                for d in range(2):
                    c = ROW["L3_cond_bk"] + d
                    ins = dve.tensor_scalar(k3[:, d, :], ps[:, d * G * NK3:(d + 1) * G * NK3], col[:, c:c + 1], None, ALU.add)
                M.drained(ins, "k3")
                for c, (h0, nh) in enumerate(CH3):
                    rows = nh * NK3
                    mask = blk3[0:rows, c, :, :].rearrange("p h g -> p (h g)").unsqueeze(1).to_broadcast([rows, G, D])
                    for i in range(G // 2):
                        ps = M.wait_full(dve, it, f"vbd_{c}_{i}")
                        dst = vbd[0:rows, c, 2 * i:2 * i + 2, :, :].rearrange("p b d g -> p (b d) g")
                        M.drained(dve.tensor_tensor(dst, ps[0:rows, :].rearrange("p (a g) -> p a g", a=4), mask, ALU.mult),
                                  f"vbd_{c}_{i}")
                for j in range(NJ):
                    d, b = j // G, j % G
                    ps = S.wait_full(dve, it, ("J", j))
                    kp = keep[:, d, b * NK3:(b + 1) * NK3].unsqueeze(1).to_broadcast([D, H3, NK3])
                    S.drained(dve.tensor_tensor(p3[:, j, :, :], ps[:, 0:H3 * NK3].rearrange("p (h m) -> p h m", h=H3), kp,
                                                ALU.mult), ("J", j))
                for j in range(NJ):
                    biased3.wait(dve, it, j)
                    max3_ready.up(dve.tensor_reduce(nmax3[:, j, :], p3[:, j, :, :], AX.X, ALU.max, negate=True))
                for j in range(NJ):
                    exp3_ready.wait(dve, it, j)
                    link(dve.tensor_reduce(rsum3[:, j, :], p3[:, j, :, :], AX.X, ALU.add))
                    rinv3_ready.up(dve.reciprocal(rinv3[:, j, :], rsum3[:, j, :]))
                for n in range(NJ):
                    ps = PT.wait_full(dve, it, ("J", n))
                    dve.tensor_copy(p3T[:, n % 2, 0:2, :], ps[0:HC * NK3, 0:2 * D].rearrange("p (c q) -> p c q", c=2))
                    PT.drained(dve.tensor_copy(p3T[0:CH3[2][1] * NK3, n % 2, 2, :], ps[0:CH3[2][1] * NK3, 2 * D:3 * D]),
                               ("J", n))
                ps = AT.wait_full(dve, it, "L3")
                ins = dve.scalar_tensor_tensor(relT[:, :], ps[:, :], bout3[:, 0:1], sT[:, :], ALU.add, ALU.add)
                AT.drained(ins, "L3")
                AT.wait_drained(dve, it, "L3")
                rel_ready.up(dve.tensor_scalar(relT[:, :], relT[:, :], 0.0, None, ALU.max))
                dve.wait_ge(x_stored, it * 16 + 16)
                ps = M.wait_full(dve, it, "y3")
                ins = dve.tensor_tensor(flat(x_out[:, :, :]), ps[:, :], flat(x[:, :, :]), ALU.add)
                M.drained(ins, "y3")
                assert dve_chain.n == DVE_LINKS, dve_chain.n


def kernel(**inputs):
    import numpy as np
    import concourse.bacc as bacc
    from concourse.bass_utils import run_bass_kernel_spmd

    nc = bacc.Bacc("TRN2", target_bir_lowering=False, num_devices=1)
    arrays, t = {}, {}
    for name, a in inputs.items():
        a = np.ascontiguousarray(a)
        a = a.reshape(1) if a.shape == () else a
        arrays[f"in_{name}"] = a
        t[name] = nc.dram_tensor(f"in_{name}", a.shape, mybir.dt.from_np(a.dtype), kind="ExternalInput").ap()
    out = nc.dram_tensor("out_0", (B, D, D), F32, kind="ExternalOutput").ap()
    build(nc, t, out)
    r = run_bass_kernel_spmd(nc, [arrays], core_ids=[0])
    return r.results[0]["out_0"]
```

```python
from contextlib import ExitStack

import concourse.bass as bass
from concourse import mybir

F32 = mybir.dt.float32
I32 = mybir.dt.int32
ALU = mybir.AluOpType
ACT = mybir.ActivationFunctionType
AX = mybir.AxisListType

D = 128
B = 32
G = 4
NG = B // G
T = G * D
H0, DH0 = 16, 64
C0 = H0 * DH0 // D
H2, DH2 = 16, 8
FF = 4
NK3 = 20
L3 = 11
H3, DH3 = 16, 8
HC = 6
CH3 = [(0, 6), (6, 6), (12, 4)]
NEG = -9000000000000000.0
EPS = (1e-5, 1e-5, 1e-6, 1e-6, 1e-5, 1e-5)
RMS = (False, False, True, True, False, False)

BIAS_ROWS = [("L0_cond_b_mod", 6), ("L1_cond_film1_b", 2), ("L1_cond_film2_b", 2), ("L2_cond_b_ada", 6),
             ("L0_cond_b_out", 1), ("L0_cond_b1", 4), ("L0_cond_b2", 1), ("L1_cond_norm1_w", 1),
             ("L1_cond_norm2_w", 1), ("L1_cond_q_b", 1), ("L1_cond_k_b", 1), ("L1_cond_v_b", 1),
             ("L1_cond_proj_b", 1), ("L1_cond_mlp_b1", 4), ("L1_cond_mlp_b2", 1), ("L2_cond_bq", 1),
             ("L2_cond_bk", 1), ("L2_cond_bv", 1), ("L2_cond_bo", 1), ("L2_cond_b1", 4), ("L2_cond_b2", 1),
             ("L3_cond_b_self", 1), ("L3_cond_bq", 2), ("L3_cond_bk", 2), ("L3_cond_bout", 2)]
ROW = {}
_n = 0
for _name, _k in BIAS_ROWS:
    ROW[_name] = _n
    _n += _k
NROWS = _n
NMOD = 16
SHIFT = (0, 3, 7, 9, 10, 13)
SCALE = (1, 4, 6, 8, 11, 14)
GATE = {"o0": 2, "g0": 5, "o2": 12, "g2": 15}

UA = 2 * C0
UB = 1 + G * H2 // 4
NJ = 2 * G
NP = 4
DVE_LINKS = 24
PIECES = [(0, 0, 40), (0, 40, 40), (1, 0, 32), (1, 32, 32), (1, 64, 32), (1, 96, 32)]

ATT_STEPS = UA + 5
FRONT_STEPS = ATT_STEPS + 3
L2_STEPS = G * H2 // 4 + 3
L3_STEPS = NJ + 5
MLP_PLAN = [2, 1, 0, 0, 1, 0]
PLAN = (MLP_PLAN
        + [2, 1, 1, 1, 0, 1, 0, 0] + MLP_PLAN
        + [2, 1, 0, 0] + [1 if i % 4 == 1 else 0 for i in range(L2_STEPS)] + [0, 0] + [1, 0, 0, 0, 0, 0]
        + [0, 0, 0, 0] + [0] * L3_STEPS + [0, 0])
assert sum(PLAN) <= FRONT_STEPS, (sum(PLAN), FRONT_STEPS)


class Ring:

    def __init__(self, nc, ctx, name, banks, uses, ps=None):
        self.ps = ps or [ctx.enter_context(nc.psum_tensor(f"{name}{i}", [D, T], F32)) for i in range(banks)]
        self.full_sems = [ctx.enter_context(nc.semaphore(f"{name}{i}_full")) for i in range(banks)]
        self.free_sems = [ctx.enter_context(nc.semaphore(f"{name}{i}_free")) for i in range(banks)]
        self.at = {u: (i % banks, i // banks) for i, u in enumerate(uses)}
        self.per = [len(range(b, len(uses), banks)) for b in range(banks)]

    def bank(self, use):
        return self.ps[self.at[use][0]]

    def full_sem(self, use):
        return self.full_sems[self.at[use][0]]

    def free_sem(self, use):
        return self.free_sems[self.at[use][0]]

    def count(self, it, use):
        b, n = self.at[use]
        return it * self.per[b] + n

    def empty(self, it, use):
        return self.free_sem(use), self.count(it, use) + 1

    def full(self, it, use):
        return self.full_sem(use), self.count(it, use) + 1

    def drained(self, it, use):
        return self.free_sem(use), self.count(it, use) + 2

    def last_in_banks(self, uses):
        return {self.at[u][0]: u for u in uses}.values()


class Count:

    def __init__(self, nc, ctx, name, per):
        self.sem = ctx.enter_context(nc.semaphore(name))
        self.per = per

    def nth(self, it, n):
        return self.sem, it * self.per + n + 1


class Chain:

    def __init__(self, nc, ctx, name, per):
        self.sem = ctx.enter_context(nc.semaphore(name))
        self.per = per
        self.n = 0

    def last(self, it):
        self.n += 1
        return self.sem, it * self.per + self.n


def weave(front, back):
    done = 0
    for follow in PLAN:
        next(back)
        for _ in range(follow):
            next(front)
            done += 1
    for _ in range(FRONT_STEPS - done):
        next(front)
    for stream in (front, back):
        assert next(stream, "end") == "end"


def alone(stream):
    for _ in stream:
        pass


def build(nc, t, out):
    front_uses = []
    for s in range(ATT_STEPS):
        if s // 2 < C0:
            front_uses += [f"q_{s // 2}", f"k_{s // 2}"] if s % 2 == 0 else [f"v_{s // 2}"]
        if s >= 6 and s % 2 == 0 and (s - 6) // 2 < C0:
            front_uses.append(f"a_{(s - 6) // 2}")
        if s == UA + 3:
            front_uses.append("ln0")
    front_uses += ["o0", "y0"]
    back_uses = []
    for l in range(3):
        if l == 1:
            back_uses += ["ln2", "q1", "k1", "v1", "a1", "o1", "y1"]
        if l == 2:
            back_uses += ["ln4", "k2", "q2", "v2", "a2", "o2", "y2"]
        back_uses += [f"ln{2 * l + 1}"] + [f"f{l}_{c}" for c in range(FF)] + [f"g{l}", f"z{l}"]
    back_uses += ["adj", "xt3", "sum3", "self3", "q3_0", "q3_1", "k3"]
    back_uses += [f"vbd_{c}_{i}" for c in range(3) for i in range(G // 2)] + ["a3", "y3"]

    with ExitStack() as ctx:
        def sb(name, shape, dt=F32):
            return ctx.enter_context(nc.sbuf_tensor(name, shape, dt))

        def sem(name):
            return ctx.enter_context(nc.semaphore(name))

        def count(name, per):
            return Count(nc, ctx, name, per)

        def flat(ap):
            return ap.rearrange("p a b -> p (a b)")

        def wide(ap, n):
            p, a = ap.shape
            return ap.unsqueeze(2).to_broadcast([p, a, n])

        def tok(b):
            return slice(b * D, (b + 1) * D)

        w_qkv = sb("w_qkv", [D, 3 * H0 * DH0])
        w_out = sb("w_out", [D, C0, D])
        w_up = sb("w_up", [D, 3, FF * D])
        w_down = sb("w_down", [D, 3, FF, D])
        w_l1 = sb("w_l1", [D, 4, D])
        w_l2 = sb("w_l2", [D, 4, D])
        w3 = sb("w3", [D, 8, D])
        col = sb("col", [D, NROWS])
        condT = sb("condT", [D, 2, B])
        mod = sb("mod", [D, NMOD, B + G])
        bout3 = sb("bout3", [D, 1])
        ident = sb("ident", [D, D])
        ones = sb("ones", [D, D])
        held = sb("held", [D, 2])
        half = sb("half", [D, G])
        head16 = sb("head16", [D, H3])
        head4 = sb("head4", [D, 4])
        blk3 = sb("blk3", [HC * NK3, 3, H3, DH3])
        wlab = sb("wlab", [D, L3])
        blab = sb("blab", [D, 1])

        x_norm = sb("x_norm", [D, G, D])
        x_res = sb("x_res", [D, G, D])
        fmod = sb("fmod", [D, 3, G])
        fz = sb("fz", [D, G, D])
        fhT = sb("fhT", [D, T])
        fq = sb("fq", [D, 2, T])
        fk = sb("fk", [D, 2, 2, T])
        fv = sb("fv", [D, 3, G, D])
        fattnT = sb("fattnT", [D, C0, T])
        w_mod = fattnT[:, 0:4, :].rearrange("p c (k d) -> p (c k) d", d=D)
        w3_raw = fattnT[:, 4:6, :].rearrange("p c (k d) -> p (c k) d", d=D)
        bias_rows = fattnT[0:NROWS, 6, 0:D]
        cond_raw = fattnT[0:B, 6, D:2 * D]
        cond = fattnT[0:B, 6, 2 * D:4 * D].rearrange("p (a d) -> p a d", a=2)
        fyT = sb("fyT", [D, T])
        fprobs = sb("fprobs", [D, NP, 4, D])
        fprobsT = sb("fprobsT", [D, NP, 4, D])
        fnegmax = sb("fnegmax", [D, UA, 4])
        frsum = sb("frsum", [D, UA, 4])
        frinv = sb("frinv", [D, UA, 4])

        x = sb("x", [D, G, D])
        z = sb("z", [D, G, D])
        x_out = sb("x_out", [D, G, D])
        gmod = sb("gmod", [D, NMOD, G])
        gcond = sb("gcond", [D, G])
        stats = sb("stats", [D, 2, G, 6])
        mv = sb("mv", [D, 2, G, 2])
        msq = sb("msq", [D, G])
        veps = sb("veps", [D, 2, G])
        rstd = sb("rstd", [D, 2, G])
        hT = sb("hT", [D, T])
        qk = sb("qk", [D, 2, T])
        oT = sb("oT", [D, T])
        yT = sb("yT", [D, T])
        hid = sb("hid", [D, FF, T])
        v1 = sb("v1", [D, G, D])
        prob_space = sb("prob_space", [D, 2 * NP, T])
        probs = prob_space[:, 0:NP, :].rearrange("p s (i k) -> p s i k", i=4)
        probsT = prob_space[:, NP:2 * NP, :].rearrange("p s (i k) -> p s i k", i=4)
        negmax = sb("negmax", [D, UB, 4])
        rsum = sb("rsum", [D, UB, 4])
        rinv = sb("rinv", [D, UB, 4])
        km_space = sb("km_space", [D, 5, T])
        km = km_space[:, 0:4, :]
        VW = H2 * (D + DH2)
        vm = sb("vm", [D, 2, VW])
        adj0 = sb("adj0", [D, G * NK3 * L3], I32)
        adj1 = sb("adj1", [G * NK3, D * L3], I32)
        PW = 40 * L3
        adjf = sb("adjf", [D, 2, PW])
        adjw = sb("adjw", [D, 2, PW])
        edge0 = sb("edge0", [D, 2, 2, G * NK3])
        edge1 = sb("edge1", [G * NK3, 2, D])
        keep = sb("keep", [D, 2, G * NK3])
        nbias = sb("nbias", [D, 2, G * NK3])
        k3 = sb("k3", [D, 2, G * NK3])
        vbd = sb("vbd", [HC * NK3, 3, G, 2, D])
        nmax3 = sb("nmax3", [D, NJ, H3])
        rsum3 = sb("rsum3", [D, NJ, H3])
        rinv3 = sb("rinv3", [D, NJ, H3])
        p3 = flat(prob_space[:, 0:5, :]).rearrange("p (j h m) -> p j h m", j=NJ, h=H3)
        x3T = prob_space[:, 5, :]
        qx = prob_space[:, 6, :]
        sT = prob_space[:, 7, :]
        kbd = flat(km_space[:, :, :]).rearrange("p (d b h m) -> p d b h m", d=2, b=G, h=H3)
        q3 = qk
        kvrep = flat(hid[:, :, :])[:, 0:G * H3 * NK3].rearrange("p (b h m) -> p b h m", b=G, h=H3)
        p3T = flat(hid[0:HC * NK3, :, :])[:, G * H3 * NK3:].rearrange("p (s c q) -> p s c q", s=2, c=3)

        FM = Ring(nc, ctx, "front_misc", 2, front_uses)
        FS = Ring(nc, ctx, "front_scores", 1, range(UA))
        FT = Ring(nc, ctx, "front_probsT", 1, range(UA))
        M = Ring(nc, ctx, "misc", 2, back_uses)
        jobs = [("A", u) for u in range(UB)] + [("J", j) for j in range(NJ)]
        S = Ring(nc, ctx, "scores", 1, jobs)
        PT = Ring(nc, ctx, "probsT_ps", 1, jobs)
        FIRST = Ring(nc, ctx, "first_norm", 1, ["ln0"], ps=[M.ps[0]])

        weights_in = sem("weights_in")
        early_in = sem("early_in")
        pool_setup = sem("pool_setup")
        consts_ready = sem("consts_ready")
        silu_ready = sem("silu_ready")
        dve_setup = sem("dve_setup")
        pe_setup = sem("pe_setup")
        setup_done = sem("setup_done")
        x_norm_in = sem("x_norm_in")
        x_res_in = sem("x_res_in")
        adj_loaded = sem("adj_loaded")
        x_stored = sem("x_stored")
        fmod_ready = count("fmod_ready", 1)
        fvar_ready = count("fvar_ready", 1)
        fgate_ready = count("fgate_ready", 1)
        frstd_ready = count("frstd_ready", 1)
        fz_ready = count("fz_ready", 1)
        fmax_ready = count("fmax_ready", UA)
        frinv_ready = count("frinv_ready", UA)
        fnormed = count("fnormed", UA)
        var_ready = count("var_ready", 5)
        rstd_ready = count("rstd_ready", 5)
        z_ready = count("z_ready", 5)
        max_ready = count("max_ready", UB)
        rinv_ready = count("rinv_ready", UB)
        normed = count("normed", UB)
        km_ready = count("km_ready", G)
        vm_ready = count("vm_ready", G)
        vm_used = count("vm_used", G - 1)
        adjf_ready = count("adjf_ready", len(PIECES))
        adjw_ready = count("adjw_ready", len(PIECES))
        adj_summed = count("adj_summed", len(PIECES))
        kbd_ready = count("kbd_ready", G)
        kvrep_ready = count("kvrep_ready", 1)
        bias_ready = count("bias_ready", 1)
        biased3 = count("biased3", NJ)
        max3_ready = count("max3_ready", NJ)
        shifted3 = count("shifted3", NJ)
        exp3_ready = count("exp3_ready", NJ)
        rinv3_ready = count("rinv3_ready", NJ)
        normed3 = count("normed3", NJ)
        rel_ready = count("rel_ready", 1)
        dve_chain = Chain(nc, ctx, "dve_chain", DVE_LINKS)
        front_chain = Chain(nc, ctx, "front_chain", 2)

        def edge_views(p, src):
            d, _, n = PIECES[p]
            rows = G * NK3 if d else D
            return src[0:rows, p % 2, 0:n * L3].rearrange("p (e l) -> p e l", l=L3)

        EARLY = [0]
        block = ctx.enter_context(nc.Block())

        @block.sync
        def _(sp):
            def early(dst, src):
                sp.dma_start(dst, src).then_inc(early_in, 16)
                EARLY[0] += 16

            def group(dram, g):
                return dram[bass.ds(g * G, G)].rearrange("b t d -> t b d")

            def load_norm(g):
                sp.dma_start(x_norm[:, :, :], group(t["x"], g)).then_inc(x_norm_in, 16)

            def load_res(g):
                sp.dma_start(x_res[:, :, :], group(t["x"], g)).then_inc(x_res_in, 16)

            mask = t["mask_BxSxSx11_ik0"]

            def load_edges(g):
                sp.dma_start(adj0[:, :].rearrange("n (b k) -> n b k", b=G),
                             mask[bass.ds(g * G, G), :, 0:NK3, :].rearrange("b n m l -> n b (m l)")).then_inc(adj_loaded, 16)
                for b in range(G):
                    sp.dma_start(adj1[b * NK3:(b + 1) * NK3, :],
                                 mask[bass.ds(g * G + b, 1), 0:NK3, :, :].rearrange("b m n l -> (b m) (n l)")).then_inc(adj_loaded, 16)

            def store(g):
                sp.wait_ge(*M.drained(g, "y3"))
                sp.dma_start(group(out, g), x_out[:, :, :]).then_inc(x_stored, 16)

            load_norm(0)
            r = 0
            early(cond_raw[:, :], t["cond_1024"])
            for name, k in BIAS_ROWS:
                src = t[name]
                src = src if len(src.shape) == 2 else src.rearrange("(k d) -> k d", d=D)
                early(bias_rows[r:r + k, :], src)
                r += k
            m = 0
            for name in ("L0_cond_W_mod", "L1_cond_film1_w", "L1_cond_film2_w", "L2_cond_W_ada"):
                k = t[name].shape[1] // D
                early(w_mod[:, m:m + k, :], t[name].rearrange("i (k d) -> i k d", d=D))
                m += k
            early(w3_raw[:, 0:2, :], t["L3_cond_W_self"].rearrange("o (k i) -> o k i", i=D))
            early(w3_raw[:, 2:4, :], t["L3_cond_Wq"].rearrange("d o i -> o d i"))
            early(w3_raw[:, 4:6, :], t["L3_cond_Wk"].rearrange("d o i -> o d i"))
            early(w3_raw[:, 6:8, :], t["L3_cond_Wout"].rearrange("d h g i -> (h g) d i"))
            early(wlab[:, :], t["L3_cond_w_bias"].rearrange("(a l) -> a l", a=1).to_broadcast([D, L3]))
            early(blab[:, :], t["L3_cond_b_bias"].rearrange("(a l) -> a l", a=1).to_broadcast([D, 1]))
            load_res(0)
            load_edges(0)
            sp.wait_ge(*fz_ready.nth(0, 0))
            load_norm(1)
            sp.wait_ge(*FM.drained(0, "y0"))
            load_res(1)
            with sp.Fori(1, NG - 1) as it:
                adj_ready = len(PIECES) - 1
                sp.wait_ge(*adjf_ready.nth(it - 1, adj_ready))
                load_edges(it)
                sp.wait_ge(*fz_ready.nth(it, 0))
                load_norm(it + 1)
                store(it - 1)
                sp.wait_ge(*FM.drained(it, "y0"))
                load_res(it + 1)
            sp.wait_ge(*adjf_ready.nth(NG - 2, len(PIECES) - 1))
            load_edges(NG - 1)
            sp.wait_ge(*fz_ready.nth(NG - 1, 0))
            load_norm(NG - 1)
            store(NG - 2)
            store(NG - 1)
            sp.wait_ge(x_norm_in, 16 * (NG + 1))
            sp.wait_ge(x_stored, 16 * NG + 16)

        NWEIGHTS = 1 + 1 + 3 + 3 + 4 + 4

        def run(eng, prologue, front, back):
            prologue()
            alone(front(0))
            with eng.Fori(1, NG) as it:
                weave(front(it), back(it - 1))
            alone(back(NG - 1))

        @block.gpsimd
        def _(pool):
            n = [0]

            def step(ins):
                ins.then_inc(pool_setup, 1)
                n[0] += 1
                pool.wait_ge(pool_setup, n[0])

            step(pool.memset(ident[:, :], 0.0))
            step(pool.affine_select(out=ident[:, :], in_=ident[:, :], compare_op=ALU.not_equal, fill=1.0,
                                    base=0, pattern=[[-1, D]], channel_multiplier=1))
            step(pool.memset(ones[:, :], 1.0))
            step(pool.memset(half[:, :], -0.5))
            step(pool.memset(fk[:, :, :, :], 0.0))
            step(pool.memset(vm[:, :, :], 0.0))
            step(pool.memset(head16[:, :], 1.0))
            step(pool.affine_select(out=head16[:, :], in_=head16[:, :], compare_op=ALU.is_ge, fill=0.0,
                                    base=0, pattern=[[-DH3, H3]], channel_multiplier=1))
            step(pool.affine_select(out=head16[:, :], in_=head16[:, :], compare_op=ALU.is_ge, fill=0.0,
                                    base=DH3 - 1, pattern=[[DH3, H3]], channel_multiplier=-1))
            step(pool.memset(blk3[:, :, :, :], 1.0))
            step(pool.affine_select(out=blk3[:, :, :, :], in_=blk3[:, :, :, :], compare_op=ALU.is_ge, fill=0.0,
                                    base=0, pattern=[[HC * NK3, 3], [-NK3, H3], [0, DH3]], channel_multiplier=1))
            pool.affine_select(out=blk3[:, :, :, :], in_=blk3[:, :, :, :], compare_op=ALU.is_ge, fill=0.0,
                               base=NK3 - 1, pattern=[[-HC * NK3, 3], [NK3, H3], [0, DH3]],
                               channel_multiplier=-1).then_inc(consts_ready, 1)
            pool.wait_ge(setup_done, 1)

            def front_rsqrt(g):
                pool.wait_ge(*fvar_ready.nth(g, 0))
                pool.tensor_tensor(rstd[:, 0, :], veps[:, 0, :], half[:, :], ALU.pow).then_inc(frstd_ready.sem, 1)

            def front(g):
                for s in range(ATT_STEPS):
                    if 0 <= s - 3 < UA:
                        pool.wait_ge(*frinv_ready.nth(g, s - 3))
                        p = fprobs[:, (s - 3) % NP, :, :]
                        pool.tensor_tensor(p, p, wide(frinv[:, s - 3, :], D), ALU.mult).then_inc(fnormed.sem, 1)
                    if s == UA + 1:
                        front_rsqrt(g + 1)
                    yield
                yield
                yield
                yield

            def back(g):
                tick = [0]

                def edges():
                    p = tick[0] - 1
                    tick[0] += 1
                    if not 0 <= p < len(PIECES):
                        return
                    d, e0, n = PIECES[p]
                    if p == 0:
                        pool.wait_ge(adj_loaded, (g + 1) * (16 * (1 + G)))
                    if p >= 2:
                        pool.wait_ge(*adj_summed.nth(g, p - 2))
                    pool.tensor_tensor(held[:, 1:2], half[:, 0:1], half[:, 1:2], ALU.mult)
                    src = (adj1 if d else adj0)[:, e0 * L3:(e0 + n) * L3].rearrange("p (e l) -> p e l", l=L3)
                    f = edge_views(p, adjf)
                    pool.tensor_copy(f, src).then_inc(adjf_ready.sem, 1)
                    pool.wait_ge(*adjf_ready.nth(g, p))
                    wl = wlab[0:f.shape[0], :].unsqueeze(1).to_broadcast([f.shape[0], n, L3])
                    pool.tensor_tensor(edge_views(p, adjw), f, wl, ALU.mult).then_inc(adjw_ready.sem, 1)

                def rsqrt(k):
                    pool.wait_ge(*var_ready.nth(g, k - 1))
                    pool.tensor_tensor(rstd[:, 1, :], veps[:, 1, :], half[:, :], ALU.pow).then_inc(rstd_ready.sem, 1)

                def norm(u):
                    pool.wait_ge(*rinv_ready.nth(g, u))
                    p = probs[:, u % NP, :, :]
                    pool.tensor_tensor(p, p, wide(rinv[:, u, :], D), ALU.mult).then_inc(normed.sem, 1)

                def mlp(l):
                    rsqrt(2 * l + 1)
                    for _ in range(6):
                        edges()
                        yield

                yield from mlp(0)
                rsqrt(2)
                for i in range(8):
                    edges()
                    if i == 3:
                        norm(0)
                    yield
                yield from mlp(1)
                rsqrt(4)
                yield
                yield
                pool.wait_ge(*M.drained(g, "k2"))
                for b in range(G):
                    kb = qk[:, 1, tok(b)].unsqueeze(1).to_broadcast([D, 4, D])
                    pool.tensor_tensor(km[:, :, tok(b)], kb, wide(head4[:, :], D), ALU.mult).then_inc(km_ready.sem, 1)
                yield
                yield
                for s in range(L2_STEPS):
                    if 1 <= s <= UB - 1:
                        norm(s)
                    yield
                yield
                yield
                yield from mlp(2)
                yield
                yield
                yield

                def block_keys(b):
                    for d in range(2):
                        kk = k3[:, d, b * NK3:(b + 1) * NK3].unsqueeze(1).to_broadcast([D, H3, NK3])
                        ins = pool.tensor_tensor(kbd[:, d, b, :, :], kk, wide(head16[:, :], NK3), ALU.mult)
                    ins.then_inc(kbd_ready.sem, 1)

                pool.wait_ge(*M.drained(g, "k3"))
                block_keys(0)
                yield
                pool.wait_ge(*bias_ready.nth(g, 0))
                for s in range(L3_STEPS):
                    if s < NJ:
                        pool.wait_ge(*S.drained(g, ("J", s)))
                        b, d = s // 2, s % 2
                        nb = nbias[:, d, b * NK3:(b + 1) * NK3].unsqueeze(1).to_broadcast([D, H3, NK3])
                        pool.tensor_tensor(p3[:, s, :, :], p3[:, s, :, :], nb, ALU.add).then_inc(biased3.sem, 1)
                    if 0 <= s - 1 < NJ:
                        j = s - 1
                        pool.wait_ge(*max3_ready.nth(g, j))
                        pool.tensor_tensor(p3[:, j, :, :], p3[:, j, :, :], wide(nmax3[:, j, :], NK3), ALU.add).then_inc(shifted3.sem, 1)
                    if s % 2 == 0 and s // 2 + 1 < G:
                        block_keys(s // 2 + 1)
                    if 0 <= s - 3 < NJ:
                        j = s - 3
                        pool.wait_ge(*rinv3_ready.nth(g, j))
                        pool.tensor_tensor(p3[:, j, :, :], p3[:, j, :, :], wide(rinv3[:, j, :], NK3), ALU.mult).then_inc(normed3.sem, 1)
                    yield
                yield
                yield

            run(pool, lambda: front_rsqrt(0), front, back)

        @block.scalar
        def _(act):
            for dst, src in ((w_qkv[:, :], t["L0_cond_W_qkv"]),
                             (w_out[:, :, :], t["L0_cond_W_out"].rearrange("(c p) d -> p c d", p=D))):
                act.dma_start(dst, src).then_inc(weights_in, 16)
            for i, w in enumerate(("L1_cond_q_w", "L1_cond_k_w", "L1_cond_v_w", "L1_cond_proj_w")):
                act.dma_start(w_l1[:, i, :], t[w]).then_inc(weights_in, 16)
            for i, w in enumerate(("L2_cond_Wq", "L2_cond_Wk", "L2_cond_Wv", "L2_cond_Wo")):
                act.dma_start(w_l2[:, i, :], t[w]).then_inc(weights_in, 16)
            for i, (up, down) in enumerate((("L0_cond_W1", "L0_cond_W2"), ("L1_cond_mlp_w1", "L1_cond_mlp_w2"),
                                            ("L2_cond_W1", "L2_cond_W2"))):
                act.dma_start(w_up[:, i, :], t[up]).then_inc(weights_in, 16)
                act.dma_start(w_down[:, i, :, :], t[down].rearrange("(c p) d -> p c d", p=D)).then_inc(weights_in, 16)
            act.wait_ge(early_in, EARLY[0])
            act.activation(cond[:, 0, :], cond_raw[:, :], ACT.Silu).then_inc(silu_ready, 1)
            act.activation(cond[:, 1, :], cond_raw[:, :], ACT.Copy).then_inc(silu_ready, 1)
            act.wait_ge(setup_done, 1)

            def front(g):
                for s in range(ATT_STEPS):
                    if s % 2 == 0 and s // 2 < C0:
                        c = s // 2
                        act.wait_ge(*FM.full(g, f"k_{c}"))
                        ps = FM.bank(f"k_{c}")
                        for r in range(2):
                            rows = slice(r * DH0, (r + 1) * DH0)
                            ins = act.activation(fk[rows, c % 2, r, :], ps[rows, :], ACT.Copy)
                        ins.then_inc(FM.free_sem(f"k_{c}"), 1)
                    if 0 <= s - 2 < UA:
                        u = s - 2
                        act.wait_ge(*fmax_ready.nth(g, u))
                        if u >= NP:
                            act.wait_ge(*FT.full(g, u - NP))
                        ps = FS.bank(u)
                        for i in range(4):
                            ins = act.activation(fprobs[:, u % NP, i, :], ps[:, tok(i)], ACT.Exp,
                                                 bias=fnegmax[:, u, i:i + 1], accum_out=frsum[:, u, i:i + 1])
                        ins.then_inc(FS.free_sem(u), 1)
                    if 0 <= s - 4 < UA:
                        u = s - 4
                        act.wait_ge(*FT.full(g, u))
                        ps = FT.bank(u)
                        act.activation(flat(fprobsT[:, u % NP, :, :]), ps[:, :], ACT.Copy).then_inc(FT.free_sem(u), 1)
                    yield
                yield
                yield
                yield

            def back(g):
                def biased(use, dst, b):
                    act.wait_ge(*M.full(g, use))
                    ps = M.bank(use)
                    act.activation(dst, ps[:, :], ACT.Identity, bias=col[:, b:b + 1]).then_inc(M.free_sem(use), 1)

                def exps(u):
                    act.wait_ge(*max_ready.nth(g, u))
                    if u >= NP:
                        act.wait_ge(*PT.full(g, ("A", u - NP)))
                    ps = S.bank(("A", u))
                    for i in range(4):
                        ins = act.activation(probs[:, u % NP, i, :], ps[:, tok(i)], ACT.Exp,
                                             bias=negmax[:, u, i:i + 1], accum_out=rsum[:, u, i:i + 1])
                    ins.then_inc(S.free_sem(("A", u)), 1)

                def probs_out(u):
                    act.wait_ge(*PT.full(g, ("A", u)))
                    ps = PT.bank(("A", u))
                    act.activation(flat(probsT[:, u % NP, :, :]), ps[:, :], ACT.Copy).then_inc(PT.free_sem(("A", u)), 1)

                def mlp(l, b1):
                    yield
                    yield
                    for i in range(2):
                        for c in range(2 * i, 2 * i + 2):
                            act.wait_ge(*M.full(g, f"f{l}_{c}"))
                            ps = M.bank(f"f{l}_{c}")
                            act.activation(hid[:, c, :], ps[:, :], ACT.Gelu, bias=col[:, b1 + c:b1 + c + 1]).then_inc(M.free_sem(f"f{l}_{c}"), 1)
                        yield
                    yield
                    yield

                yield from mlp(0, ROW["L0_cond_b1"])
                yield
                yield
                biased("k1", qk[:, 1, :], ROW["L1_cond_k_b"])
                yield
                exps(0)
                yield
                probs_out(0)
                yield
                yield
                yield
                yield
                yield from mlp(1, ROW["L1_cond_mlp_b1"])
                yield
                yield
                biased("k2", qk[:, 1, :], ROW["L2_cond_bk"])
                yield
                yield
                for s in range(L2_STEPS):
                    if s < UB - 1:
                        exps(s + 1)
                    if 2 <= s <= UB:
                        probs_out(s - 1)
                    yield
                yield
                yield
                yield from mlp(2, ROW["L2_cond_b1"])
                act.wait_ge(*M.full(g, "xt3"))
                ps = M.bank("xt3")
                act.activation(x3T, ps[:, :], ACT.Copy).then_inc(M.free_sem("xt3"), 1)
                yield
                yield
                yield
                yield
                for s in range(L3_STEPS):
                    if 0 <= s - 1 < NJ:
                        act.wait_ge(*shifted3.nth(g, s - 1))
                        act.activation(p3[:, s - 1, :, :], p3[:, s - 1, :, :], ACT.Exp).then_inc(exp3_ready.sem, 1)
                    if 0 <= s - 4 < NJ:
                        j = s - 4
                        act.wait_ge(*PT.full(g, ("J", j)))
                        ps = PT.bank(("J", j))
                        act.activation(p3T[:, j % 2, 0:2, :], ps[0:HC * NK3, 0:2 * D].rearrange("p (c q) -> p c q", c=2), ACT.Copy)
                        rows = CH3[2][1] * NK3
                        act.activation(p3T[0:rows, j % 2, 2, :], ps[0:rows, 2 * D:3 * D], ACT.Copy).then_inc(PT.free_sem(("J", j)), 1)
                    yield
                yield
                yield

            run(act, lambda: None, front, back)

        @block.tensor
        def _(pe):
            pe.wait_ge(consts_ready, 1)
            pe.wait_ge(early_in, EARLY[0])
            for i in range(8):
                pe.transpose(M.ps[i // 4][:, tok(i % 4)], w3_raw[:, i, :], ident[:, :])
            pe.transpose(S.ps[0][:, 0:NROWS], bias_rows[:, :], ident[0:NROWS, 0:NROWS])
            pe.wait_ge(silu_ready, 2)
            for i in range(2):
                ins = pe.transpose(S.ps[0][:, D + i * B:D + (i + 1) * B], cond[:, i, :], ident[0:B, 0:B])
            ins.then_inc(pe_setup, 1)
            pe.wait_ge(dve_setup, 3)
            for m in range(NMOD):
                ins = pe.matmul(PT.ps[0][:, m * B:(m + 1) * B], w_mod[:, m, :], condT[:, 0 if m < 6 else 1, :],
                                start=True, stop=True)
            ins.then_inc(pe_setup, 1)
            for ring in (FM, FS, FT, M, S, PT, FIRST):
                for free in ring.free_sems:
                    pe.sem_inc(free, 1)
            pe.wait_ge(setup_done, 1)

            def turn(ring, g, use, src):
                pe.wait_ge(*ring.empty(g, use))
                ps = ring.bank(use)
                for b in range(G):
                    ins = pe.transpose(ps[:, tok(b)], src[:, b, :] if len(src.shape) == 3 else src[:, tok(b)], ident[:, :])
                ins.then_inc(ring.full_sem(use), 1)

            def front_norm(g, ring, ring_g):
                pe.wait_ge(*fz_ready.nth(g, 0))
                turn(ring, ring_g, "ln0", fz)

            def front(g):
                def linear(use, w):
                    pe.wait_ge(*FM.empty(g, use))
                    ps = FM.bank(use)
                    pe.matmul(ps[:, :], w, fhT[:, :], start=True, stop=True).then_inc(FM.full_sem(use), 1)

                for s in range(ATT_STEPS):
                    if s // 2 < C0:
                        c = s // 2
                        if s % 2 == 0:
                            linear(f"q_{c}", w_qkv[:, tok(c)])
                            linear(f"k_{c}", w_qkv[:, tok(C0 + c)])
                        else:
                            pe.wait_ge(*FM.empty(g, f"v_{c}"))
                            ps = FM.bank(f"v_{c}")
                            for b in range(G):
                                ins = pe.matmul(ps[:, tok(b)], fhT[:, tok(b)], w_qkv[:, tok(2 * C0 + c)], start=True, stop=True)
                            ins.then_inc(FM.full_sem(f"v_{c}"), 1)
                    if 0 <= s - 2 < UA:
                        u = s - 2
                        c = u // 2
                        if u % 2 == 0:
                            for use in FM.last_in_banks([f"q_{c}", f"k_{c}"]):
                                pe.wait_ge(*FM.drained(g, use))
                        pe.wait_ge(*FS.empty(g, u))
                        ps = FS.bank(u)
                        for i in range(2):
                            b = 2 * (u % 2) + i
                            ins = pe.matmul(ps[:, 2 * i * D:2 * (i + 1) * D], fq[:, c % 2, tok(b)], fk[:, c % 2, :, tok(b)],
                                            start=True, stop=True)
                        ins.then_inc(FS.full_sem(u), 1)
                    if 0 <= s - 4 < UA:
                        u = s - 4
                        pe.wait_ge(*fnormed.nth(g, u))
                        pe.wait_ge(*FT.empty(g, u))
                        ps = FT.bank(u)
                        for i in range(4):
                            ins = pe.transpose(ps[:, tok(i)], fprobs[:, u % NP, i, :], ident[:, :])
                        ins.then_inc(FT.full_sem(u), 1)
                    if s >= 6 and s % 2 == 0 and (s - 6) // 2 < C0:
                        c = (s - 6) // 2
                        pe.wait_ge(*FM.drained(g, f"v_{c}"))
                        pe.wait_ge(*FT.drained(g, 2 * c + 1))
                        pe.wait_ge(*FM.empty(g, f"a_{c}"))
                        ps = FM.bank(f"a_{c}")
                        for b in range(G):
                            for r in range(2):
                                u = 2 * c + b // 2
                                ins = pe.matmul(ps[r * DH0:(r + 1) * DH0, tok(b)], fv[:, c % 3, b, r * DH0:(r + 1) * DH0],
                                                fprobsT[:, u % NP, 2 * (b % 2) + r, :], start=True, stop=True)
                        ins.then_inc(FM.full_sem(f"a_{c}"), 1)
                    if s == UA + 3:
                        front_norm(g + 1, FM, g)
                    yield
                for i in range(2):
                    if i == 0:
                        pe.wait_ge(*FM.empty(g, "o0"))
                        ps = FM.bank("o0")
                    else:
                        pe.wait_ge(*FM.drained(g, f"a_{C0 - 1}"))
                    for c in range(C0 // 2 * i, C0 // 2 * (i + 1)):
                        ins = pe.matmul(ps[:, :], w_out[:, c, :], fattnT[:, c, :], start=(c == 0), stop=(c == C0 - 1))
                    if i:
                        ins.then_inc(FM.full_sem("o0"), 1)
                    yield
                pe.wait_ge(*FM.drained(g, "o0"))
                turn(FM, g, "y0", fyT)
                yield

            def back(g):
                def linear(use, terms):
                    pe.wait_ge(*M.empty(g, use))
                    ps = M.bank(use)
                    for i, (w, a) in enumerate(terms):
                        ins = pe.matmul(ps[:, :], w, a, start=(i == 0), stop=(i == len(terms) - 1))
                    ins.then_inc(M.full_sem(use), 1)

                def norm_turn(k):
                    yield
                    pe.wait_ge(*z_ready.nth(g, k - 1))
                    turn(M, g, f"ln{k}", z)
                    yield
                    pe.wait_ge(*M.drained(g, f"ln{k}"))

                def probs_turn(u):
                    pe.wait_ge(*normed.nth(g, u))
                    pe.wait_ge(*PT.empty(g, ("A", u)))
                    ps = PT.bank(("A", u))
                    for i in range(4):
                        ins = pe.transpose(ps[:, tok(i)], probs[:, u % NP, i, :], ident[:, :])
                    ins.then_inc(PT.full_sem(("A", u)), 1)

                def output(use, turned, terms):
                    linear(use, terms)
                    yield
                    pe.wait_ge(*M.drained(g, use))
                    turn(M, g, turned, yT)
                    yield

                def mlp(l):
                    yield from norm_turn(2 * l + 1)
                    for i in range(2):
                        for c in range(2 * i, 2 * i + 2):
                            linear(f"f{l}_{c}", [(w_up[:, l, tok(c)], hT[:, :])])
                        yield
                    for use in M.last_in_banks([f"f{l}_{c}" for c in range(FF)]):
                        pe.wait_ge(*M.drained(g, use))
                    yield from output(f"g{l}", f"z{l}", [(w_down[:, l, c, :], hid[:, c, :]) for c in range(FF)])

                def token_values(l, w):
                    pe.wait_ge(*M.empty(g, f"v{l}"))
                    ps = M.bank(f"v{l}")
                    for b in range(G):
                        ins = pe.matmul(ps[:, tok(b)], hT[:, tok(b)], w, start=True, stop=True)
                    ins.then_inc(M.full_sem(f"v{l}"), 1)

                yield from mlp(0)

                yield from norm_turn(2)
                linear("q1", [(w_l1[:, 0, :], hT[:, :])])
                linear("k1", [(w_l1[:, 1, :], hT[:, :])])
                token_values(1, w_l1[:, 2, :])
                yield
                for use in M.last_in_banks(["q1", "k1"]):
                    pe.wait_ge(*M.drained(g, use))
                pe.wait_ge(*S.empty(g, ("A", 0)))
                ps = S.bank(("A", 0))
                for b in range(G):
                    ins = pe.matmul(ps[:, tok(b)], qk[:, 0, tok(b)], qk[:, 1, tok(b)], start=True, stop=True)
                ins.then_inc(S.full_sem(("A", 0)), 1)
                yield
                probs_turn(0)
                yield
                pe.wait_ge(*PT.drained(g, ("A", 0)))
                pe.wait_ge(*M.drained(g, "v1"))
                pe.wait_ge(*M.empty(g, "a1"))
                ps = M.bank("a1")
                for b in range(G):
                    ins = pe.matmul(ps[:, tok(b)], v1[:, b, :], probsT[:, 0, b, :], start=True, stop=True)
                ins.then_inc(M.full_sem("a1"), 1)
                yield
                pe.wait_ge(*M.drained(g, "a1"))
                yield from output("o1", "y1", [(w_l1[:, 3, :], oT[:, :])])
                yield from mlp(1)

                yield from norm_turn(4)
                linear("k2", [(w_l2[:, 1, :], hT[:, :])])
                linear("q2", [(w_l2[:, 0, :], hT[:, :])])
                yield
                token_values(2, w_l2[:, 2, :])
                yield
                pe.wait_ge(*M.drained(g, "q2"))
                for s in range(L2_STEPS):
                    if s < UB - 1:
                        b, strip = s // 4, s % 4
                        rows = slice(32 * strip, 32 * strip + 32)
                        if strip == 0:
                            pe.wait_ge(*km_ready.nth(g, b))
                        pe.wait_ge(*S.empty(g, ("A", s + 1)))
                        ps = S.bank(("A", s + 1))
                        pe.matmul(ps[:, :], qk[rows, 0, tok(b)], km[rows, :, tok(b)], start=True, stop=True).then_inc(S.full_sem(("A", s + 1)), 1)
                    if 2 <= s <= UB:
                        probs_turn(s - 1)
                    if 3 <= s <= UB + 1:
                        u = s - 2
                        b, strip = (u - 1) // 4, (u - 1) % 4
                        pe.wait_ge(*PT.drained(g, ("A", u)))
                        if strip == 0:
                            pe.wait_ge(*vm_ready.nth(g, b))
                        if u == 1:
                            pe.wait_ge(*M.empty(g, "a2"))
                            ps = M.bank("a2")
                        ps = M.bank("a2")
                        for i in range(4):
                            h = 4 * strip + i
                            ins = pe.matmul(ps[:, tok(b)], vm[:, b % 2, h * D:(h + 1) * D], probsT[:, u % NP, i, :],
                                            start=(h == 0), stop=(h == H2 - 1))
                        if u == UB - 1:
                            ins.then_inc(M.full_sem("a2"), 1)
                        elif strip == 3:
                            ins.then_inc(vm_used.sem, 1)
                    yield
                pe.wait_ge(*M.drained(g, "a2"))
                yield from output("o2", "y2", [(w_l2[:, 3, :], oT[:, :])])
                yield from mlp(2)

                pe.wait_ge(*adj_summed.nth(g, len(PIECES) - 1))
                pe.wait_ge(*M.empty(g, "adj"))
                ps = M.bank("adj")
                for i in range(2):
                    ins = pe.transpose(ps[:, i * G * NK3:(i + 1) * G * NK3], edge1[:, i, :], ident[0:G * NK3, 0:G * NK3])
                ins.then_inc(M.full_sem("adj"), 1)
                pe.wait_ge(*M.drained(g, "z2"))
                turn(M, g, "xt3", x)
                yield
                pe.wait_ge(*M.drained(g, "xt3"))
                linear("sum3", [(ones[:, :], x3T)])
                yield
                pe.wait_ge(*M.drained(g, "sum3"))
                linear("self3", [(w3[:, 0, :], x3T), (w3[:, 1, :], qx)])
                yield
                pe.wait_ge(*M.drained(g, "self3"))
                for d in range(2):
                    linear(f"q3_{d}", [(w3[:, 2 + d, :], sT[:, :])])
                pe.wait_ge(*M.empty(g, "k3"))
                ps = M.bank("k3")
                for d in range(2):
                    ins = pe.matmul(ps[:, d * G * NK3:(d + 1) * G * NK3], w3[:, 4 + d, :],
                                    sT[:, :].rearrange("p (b n) -> p b n", b=G)[:, :, 0:NK3], start=True, stop=True)
                ins.then_inc(M.full_sem("k3"), 1)
                yield
                for s in range(L3_STEPS):
                    if s < 3:
                        h0, nh = CH3[s]
                        if s == 0:
                            pe.wait_ge(*kvrep_ready.nth(g, 0))
                        for i in range(G // 2):
                            pe.wait_ge(*M.empty(g, f"vbd_{s}_{i}"))
                            ps = M.bank(f"vbd_{s}_{i}")
                            for b2 in range(2):
                                kv = kvrep[:, 2 * i + b2, h0:h0 + nh, :].rearrange("p h m -> p (h m)")
                                ins = pe.matmul(ps[0:nh * NK3, b2 * 2 * D:(b2 + 1) * 2 * D], kv,
                                                w3[:, 6:8, :].rearrange("p d g -> p (d g)"), start=True, stop=True)
                            ins.then_inc(M.full_sem(f"vbd_{s}_{i}"), 1)
                    if s < NJ:
                        b, d = s // 2, s % 2
                        if d == 0:
                            pe.wait_ge(*kbd_ready.nth(g, b))
                        pe.wait_ge(*S.empty(g, ("J", s)))
                        ps = S.bank(("J", s))
                        pe.matmul(ps[:, 0:H3 * NK3], q3[:, d, tok(b)],
                                  kbd[:, d, b, :, :].rearrange("p h m -> p (h m)"), start=True, stop=True).then_inc(S.full_sem(("J", s)), 1)
                    if 0 <= s - 4 < NJ:
                        j = s - 4
                        pe.wait_ge(*normed3.nth(g, j))
                        pe.wait_ge(*PT.empty(g, ("J", j)))
                        ps = PT.bank(("J", j))
                        for c, (h0, nh) in enumerate(CH3):
                            ins = pe.transpose(ps[0:nh * NK3, tok(c)],
                                               p3[:, j, h0:h0 + nh, :].rearrange("p h m -> p (h m)"), ident[:, :])
                        ins.then_inc(PT.full_sem(("J", j)), 1)
                    if 0 <= s - 5 < NJ:
                        j = s - 5
                        b, d = j // 2, j % 2
                        pe.wait_ge(*PT.drained(g, ("J", j)))
                        if j == 0:
                            for use in M.last_in_banks([f"vbd_{c}_{i}" for c in range(3) for i in range(G // 2)]):
                                pe.wait_ge(*M.drained(g, use))
                            pe.wait_ge(*M.empty(g, "a3"))
                            ps = M.bank("a3")
                        else:
                            ps = M.bank("a3")
                        for c, (h0, nh) in enumerate(CH3):
                            rows = nh * NK3
                            ins = pe.matmul(ps[:, tok(b)], vbd[0:rows, c, b, d, :], p3T[0:rows, j % 2, c, :],
                                            start=(d == 0 and c == 0), stop=(d == 1 and c == 2))
                        if j == NJ - 1:
                            ins.then_inc(M.full_sem("a3"), 1)
                    yield
                yield
                pe.wait_ge(*rel_ready.nth(g, 0))
                turn(M, g, "y3", yT)
                yield

            def prologue():
                front_norm(0, FIRST, 0)
                pe.wait_ge(*FIRST.drained(0, "ln0"))
                pe.wait_ge(weights_in, 16 * NWEIGHTS)

            run(pe, prologue, front, back)

        @block.vector
        def _(dve):
            def setup_step(ins):
                ins.then_inc(dve_setup, 1)

            dve.wait_ge(pe_setup, 1)
            setup_step(dve.tensor_copy(condT[:, :, :], S.ps[0][:, D:D + 2 * B].rearrange("p (a b) -> p a b", a=2)))
            setup_step(dve.tensor_copy(col[:, :], S.ps[0][:, 0:NROWS]))
            for i in range(2):
                ins = dve.tensor_copy(w3[:, 4 * i:4 * i + 4, :], M.ps[i][:, :].rearrange("p (a b) -> p a b", a=4))
            setup_step(ins)
            dve.wait_ge(pe_setup, 2)
            dve.wait_ge(dve_setup, 3)
            dve.memset(mod[:, :, B:B + G], 0.0)
            setup_step(dve.tensor_tensor(mod[:, :, 0:B], PT.ps[0][:, :].rearrange("p (m b) -> p m b", m=NMOD),
                                         wide(col[:, 0:NMOD], B), ALU.add))
            dve.wait_ge(dve_setup, 4)
            for k in range(6):
                m = SCALE[k]
                if RMS[k]:
                    w = ROW["L1_cond_norm1_w"] + (k - 2)
                    dve.tensor_scalar(mod[:, m, :], mod[:, m, :], 1.0, col[:, w:w + 1], ALU.add, ALU.mult)
                else:
                    dve.tensor_scalar(mod[:, m, :], mod[:, m, :], 1.0, None, ALU.add)
            dve.wait_ge(consts_ready, 1)
            dve.tensor_reduce(head4[:, :], head16[:, :].rearrange("p (s h) -> p h s", h=4), AX.X, ALU.add)
            r = ROW["L3_cond_bout"]
            dve.tensor_tensor(bout3[:, :], col[:, r:r + 1], col[:, r + 1:r + 2], ALU.add).then_inc(setup_done, 1)
            dve.wait_ge(setup_done, 1)
            dve.sem_inc(x_stored, 16)

            def statistics(chain, g, i, src, k):
                for b in range(G):
                    ins = dve.bn_stats(stats[:, i, b, :], src[:, b, :])
                ins.then_inc(chain.sem, 1)
                dve.wait_ge(*chain.last(g))
                dve.memset(held[:, 0:1], 0.0)
                for b in range(G):
                    ins = dve.bn_aggr(mv[:, i, b, :], stats[:, i, b, :])
                ins.then_inc(chain.sem, 1)
                dve.wait_ge(*chain.last(g))
                if RMS[k]:
                    dve.tensor_tensor(msq[:, :], mv[:, i, :, 0], mv[:, i, :, 0], ALU.mult).then_inc(chain.sem, 1)
                    dve.wait_ge(*chain.last(g))
                    return dve.scalar_tensor_tensor(veps[:, i, :], mv[:, i, :, 1], EPS[k], msq[:, :], ALU.add, ALU.add)
                return dve.tensor_scalar(veps[:, i, :], mv[:, i, :, 1], EPS[k], None, ALU.add)

            def normalize(i, dst, src, k):
                for b in range(G):
                    r = rstd[:, i, b:b + 1]
                    if RMS[k]:
                        ins = dve.tensor_scalar(dst[:, b, :], src[:, b, :], r, None, ALU.mult)
                    else:
                        ins = dve.tensor_scalar(dst[:, b, :], src[:, b, :], mv[:, i, b, 0:1], r, ALU.subtract, ALU.mult)
                return ins

            def modulate(dst, ps, scale, shift):
                for b in range(G):
                    ins = dve.tensor_scalar(dst[:, tok(b)], ps[:, tok(b)], scale[:, b:b + 1], shift[:, b:b + 1], ALU.mult, ALU.add)
                return ins

            def gate(dst, ps, bias, g_):
                for b in range(G):
                    ins = dve.tensor_scalar(dst[:, tok(b)], ps[:, tok(b)], col[:, bias:bias + 1], g_[:, b:b + 1], ALU.add, ALU.mult)
                return ins

            def front_norm_a(g):
                front_chain.n = 0
                dve.wait_ge(x_norm_in, g * 16 + 16)
                statistics(front_chain, g, 0, x_norm, 0).then_inc(fvar_ready.sem, 1)
                assert front_chain.n == front_chain.per
                dve.wait_ge(*frstd_ready.nth(g, 0))
                normalize(0, fz, x_norm, 0).then_inc(fz_ready.sem, 1)

            def front_norm_b(g, ring, ring_g):
                dve.tensor_copy(fmod[:, 0:2, :], mod[:, 0:2, bass.ds(g * G, G)]).then_inc(fmod_ready.sem, 1)
                dve.wait_ge(*fmod_ready.nth(g, 0))
                dve.wait_ge(*ring.full(ring_g, "ln0"))
                ps = ring.bank("ln0")
                modulate(fhT, ps, fmod[:, 1, :], fmod[:, 0, :]).then_inc(ring.free_sem("ln0"), 1)

            def front(g):
                for s in range(ATT_STEPS):
                    if s // 2 < C0:
                        c = s // 2
                        if s % 2 == 0:
                            dve.wait_ge(*FM.full(g, f"q_{c}"))
                            ps = FM.bank(f"q_{c}")
                            dve.tensor_scalar(fq[:, c % 2, :], ps[:, :], DH0 ** -0.5, None, ALU.mult).then_inc(FM.free_sem(f"q_{c}"), 1)
                        else:
                            dve.wait_ge(*FM.full(g, f"v_{c}"))
                            ps = FM.bank(f"v_{c}")
                            dve.tensor_copy(flat(fv[:, c % 3, :, :]), ps[:, :]).then_inc(FM.free_sem(f"v_{c}"), 1)
                    if 0 <= s - 2 < UA:
                        dve.wait_ge(*FS.full(g, s - 2))
                        ps = FS.bank(s - 2)
                        dve.tensor_reduce(fnegmax[:, s - 2, :], ps[:, :].rearrange("p (h k) -> p h k", h=4),
                                          AX.X, ALU.max, negate=True).then_inc(fmax_ready.sem, 1)
                    if 0 <= s - 3 < UA:
                        dve.wait_ge(*FS.drained(g, s - 3))
                        dve.reciprocal(frinv[:, s - 3, :], frsum[:, s - 3, :]).then_inc(frinv_ready.sem, 1)
                    if s >= 6 and s % 2 == 0 and (s - 6) // 2 < C0:
                        c = (s - 6) // 2
                        dve.wait_ge(*FM.full(g, f"a_{c}"))
                        ps = FM.bank(f"a_{c}")
                        dve.tensor_copy(fattnT[:, c, :], ps[:, :]).then_inc(FM.free_sem(f"a_{c}"), 1)
                    if s == UA + 1:
                        front_norm_a(g + 1)
                    if s == UA + 3:
                        front_norm_b(g + 1, FM, g)
                    yield
                yield
                dve.tensor_copy(fmod[:, 2, :], mod[:, GATE["o0"], bass.ds(g * G, G)]).then_inc(fgate_ready.sem, 1)
                dve.wait_ge(*fgate_ready.nth(g, 0))
                dve.wait_ge(*FM.full(g, "o0"))
                ps = FM.bank("o0")
                gate(fyT, ps, ROW["L0_cond_b_out"], fmod[:, 2, :]).then_inc(FM.free_sem("o0"), 1)
                yield
                dve.wait_ge(x_res_in, g * 16 + 16)
                dve.wait_ge(*FM.full(g, "y0"))
                ps = FM.bank("y0")
                dve.tensor_tensor(flat(x[:, :, :]), ps[:, :], flat(x_res[:, :, :]), ALU.add).then_inc(FM.free_sem("y0"), 1)
                yield

            def back(g):
                dve_chain.n = 0

                def norm(k):
                    statistics(dve_chain, g, 1, x, k).then_inc(var_ready.sem, 1)
                    dve.wait_ge(*rstd_ready.nth(g, k - 1))
                    normalize(1, z, x, k).then_inc(z_ready.sem, 1)
                    yield
                    dve.wait_ge(*M.full(g, f"ln{k}"))
                    ps = M.bank(f"ln{k}")
                    modulate(hT, ps, gmod[:, SCALE[k], :], gmod[:, SHIFT[k], :]).then_inc(M.free_sem(f"ln{k}"), 1)
                    yield

                def biased(use, dst, bias):
                    dve.wait_ge(*M.full(g, use))
                    ps = M.bank(use)
                    dve.tensor_scalar(dst, ps[:, :], col[:, bias:bias + 1], None, ALU.add).then_inc(M.free_sem(use), 1)

                def scaled_q(use, dst, bias, scale):
                    dve.wait_ge(*M.full(g, use))
                    ps = M.bank(use)
                    dve.tensor_scalar(dst, ps[:, :], col[:, bias:bias + 1], scale, ALU.add, ALU.mult).then_inc(M.free_sem(use), 1)

                def output(use, turned, bias):
                    if use in GATE:
                        dve.wait_ge(*M.full(g, use))
                        ps = M.bank(use)
                        gate(yT, ps, bias, gmod[:, GATE[use], :]).then_inc(M.free_sem(use), 1)
                    else:
                        biased(use, yT[:, :], bias)
                    yield
                    dve.wait_ge(*M.full(g, turned))
                    ps = M.bank(turned)
                    dve.tensor_tensor(flat(x[:, :, :]), ps[:, :], flat(x[:, :, :]), ALU.add).then_inc(M.free_sem(turned), 1)
                    dve.wait_ge(*M.drained(g, turned))
                    yield

                def row_max(u):
                    dve.wait_ge(*S.full(g, ("A", u)))
                    ps = S.bank(("A", u))
                    dve.tensor_reduce(negmax[:, u, :], ps[:, :].rearrange("p (h k) -> p h k", h=4), AX.X,
                                      ALU.max, negate=True).then_inc(max_ready.sem, 1)

                def inverse(u):
                    dve.wait_ge(*S.drained(g, ("A", u)))
                    dve.reciprocal(rinv[:, u, :], rsum[:, u, :]).then_inc(rinv_ready.sem, 1)

                tick = [0]

                def edges():
                    p = tick[0] - 2
                    tick[0] += 1
                    if not 0 <= p < len(PIECES):
                        return
                    d, e0, n = PIECES[p]
                    dst = edge1[:, :, e0:e0 + n] if d else edge0[:, :, 0, e0:e0 + n]
                    dve.wait_ge(*adjw_ready.nth(g, p))
                    dve.tensor_reduce(dst[:, 0, :], edge_views(p, adjf), AX.X, ALU.add)
                    dve.tensor_reduce(dst[:, 1, :], edge_views(p, adjw), AX.X, ALU.add).then_inc(adj_summed.sem, 1)

                def with_edges(steps):
                    for _ in steps:
                        edges()
                        yield

                def mlp(l, b2):
                    yield from norm(2 * l + 1)
                    yield
                    yield
                    yield from output(f"g{l}", f"z{l}", b2)

                dve.tensor_copy(gmod[:, :, :], mod[:, :, bass.ds(g * G, G)]).then_inc(dve_chain.sem, 1)
                dve.wait_ge(*dve_chain.last(g))
                dve.tensor_copy(gcond[:, :], condT[:, 1, bass.ds(g * G, G)]).then_inc(dve_chain.sem, 1)
                dve.wait_ge(*dve_chain.last(g))
                dve.wait_ge(*FM.drained(g, "y0"))
                yield from with_edges(mlp(0, ROW["L0_cond_b2"]))

                def layer1():
                    yield from norm(2)
                    scaled_q("q1", qk[:, 0, :], ROW["L1_cond_q_b"], D ** -0.5)
                    dve.wait_ge(*M.full(g, "v1"))
                    ps = M.bank("v1")
                    dve.tensor_copy(flat(v1[:, :, :]), ps[:, :]).then_inc(M.free_sem("v1"), 1)
                    yield
                    row_max(0)
                    inverse(0)
                    yield
                    yield
                    biased("a1", oT[:, :], ROW["L1_cond_v_b"])
                    yield
                    yield from output("o1", "y1", ROW["L1_cond_proj_b"])

                yield from with_edges(layer1())
                yield from mlp(1, ROW["L1_cond_mlp_b2"])

                yield from norm(4)
                scaled_q("q2", qk[:, 0, :], ROW["L2_cond_bq"], DH2 ** -0.5)
                yield
                dve.wait_ge(*M.full(g, "v2"))
                ps = M.bank("v2")
                dve.tensor_copy(flat(v1[:, :, :]), ps[:, :]).then_inc(M.free_sem("v2"), 1)
                yield
                dve.wait_ge(*M.drained(g, "v2"))
                for s in range(L2_STEPS):
                    if s < UB - 1:
                        row_max(s + 1)
                    if s % 4 == 0 and s // 4 < G:
                        b = s // 4
                        if b >= 2:
                            dve.wait_ge(*vm_used.nth(g, b - 2))
                        dve.tensor_copy(vm[:, b % 2, :].rearrange("p (h e) -> p h e", h=H2)[:, :, 0:DH2],
                                        v1[:, b, :].rearrange("p (h e) -> p h e", h=H2)).then_inc(vm_ready.sem, 1)
                    if 1 <= s <= UB - 1:
                        inverse(s)
                    yield
                biased("a2", oT[:, :], ROW["L2_cond_bv"])
                yield from output("o2", "y2", ROW["L2_cond_bo"])
                yield from mlp(2, ROW["L2_cond_b2"])

                dve.wait_ge(*M.full(g, "adj"))
                ps = M.bank("adj")
                dve.tensor_copy(edge0[:, :, 1, :], ps[:, 0:2 * G * NK3].rearrange("p (a e) -> p a e", a=2)).then_inc(M.free_sem("adj"), 1)
                dve.wait_ge(*M.drained(g, "adj"))
                dve.tensor_scalar(keep[:, :, :], edge0[:, 0, :, :], 0.0, None, ALU.is_gt).then_inc(dve_chain.sem, 1)
                dve.wait_ge(*dve_chain.last(g))
                dve.tensor_scalar(nbias[:, :, :], keep[:, :, :], -NEG, NEG, ALU.mult, ALU.add).then_inc(dve_chain.sem, 1)
                dve.wait_ge(*dve_chain.last(g))
                dve.scalar_tensor_tensor(nbias[:, :, :], edge0[:, 1, :, :], blab[:, 0:1], nbias[:, :, :],
                                         ALU.add, ALU.add).then_inc(bias_ready.sem, 1)
                yield
                dve.wait_ge(*M.full(g, "sum3"))
                ps = M.bank("sum3")
                for b in range(G):
                    ins = dve.tensor_scalar(qx[:, tok(b)], ps[:, tok(b)], 0.0, gcond[:, b:b + 1], ALU.not_equal, ALU.mult)
                ins.then_inc(M.free_sem("sum3"), 1)
                yield
                biased("self3", sT[:, :], ROW["L3_cond_b_self"])
                dve.wait_ge(*M.drained(g, "self3"))
                kv = sT[:, :].rearrange("p (b n) -> p b n", b=G)[:, :, 0:NK3]
                for b in range(G):
                    ins = dve.tensor_copy(kvrep[:, b, :, :], kv[:, b, :].unsqueeze(1).to_broadcast([D, H3, NK3]))
                ins.then_inc(kvrep_ready.sem, 1)
                yield
                for d in range(2):
                    scaled_q(f"q3_{d}", q3[:, d, :], ROW["L3_cond_bq"] + d, DH3 ** -0.5)
                dve.wait_ge(*M.full(g, "k3"))
                ps = M.bank("k3")
                for d in range(2):
                    c = ROW["L3_cond_bk"] + d
                    ins = dve.tensor_scalar(k3[:, d, :], ps[:, d * G * NK3:(d + 1) * G * NK3], col[:, c:c + 1], None, ALU.add)
                ins.then_inc(M.free_sem("k3"), 1)
                yield
                for s in range(L3_STEPS):
                    if s < 3:
                        rows = CH3[s][1] * NK3
                        mask = blk3[0:rows, s, :, :].rearrange("p h g -> p (h g)").unsqueeze(1).to_broadcast([rows, G, D])
                        for i in range(G // 2):
                            dve.wait_ge(*M.full(g, f"vbd_{s}_{i}"))
                            ps = M.bank(f"vbd_{s}_{i}")
                            dst = vbd[0:rows, s, 2 * i:2 * i + 2, :, :].rearrange("p b d g -> p (b d) g")
                            dve.tensor_tensor(dst, ps[0:rows, :].rearrange("p (a g) -> p a g", a=4), mask, ALU.mult).then_inc(M.free_sem(f"vbd_{s}_{i}"), 1)
                    if s < NJ:
                        b, d = s // 2, s % 2
                        dve.wait_ge(*S.full(g, ("J", s)))
                        ps = S.bank(("J", s))
                        kp = keep[:, d, b * NK3:(b + 1) * NK3].unsqueeze(1).to_broadcast([D, H3, NK3])
                        dve.tensor_tensor(p3[:, s, :, :], ps[:, 0:H3 * NK3].rearrange("p (h m) -> p h m", h=H3), kp,
                                          ALU.mult).then_inc(S.free_sem(("J", s)), 1)
                    if 0 <= s - 1 < NJ:
                        dve.wait_ge(*biased3.nth(g, s - 1))
                        dve.tensor_reduce(nmax3[:, s - 1, :], p3[:, s - 1, :, :], AX.X, ALU.max, negate=True).then_inc(max3_ready.sem, 1)
                    if 0 <= s - 3 < NJ:
                        j = s - 3
                        dve.wait_ge(*exp3_ready.nth(g, j))
                        dve.tensor_reduce(rsum3[:, j, :], p3[:, j, :, :], AX.X, ALU.add).then_inc(dve_chain.sem, 1)
                        dve.wait_ge(*dve_chain.last(g))
                        dve.reciprocal(rinv3[:, j, :], rsum3[:, j, :]).then_inc(rinv3_ready.sem, 1)
                    yield
                dve.wait_ge(*M.full(g, "a3"))
                ps = M.bank("a3")
                dve.scalar_tensor_tensor(yT[:, :], ps[:, :], bout3[:, 0:1], sT[:, :], ALU.add, ALU.add).then_inc(M.free_sem("a3"), 1)
                dve.wait_ge(*M.drained(g, "a3"))
                dve.tensor_scalar(yT[:, :], yT[:, :], 0.0, None, ALU.max).then_inc(rel_ready.sem, 1)
                yield
                dve.wait_ge(x_stored, g * 16 + 16)
                dve.wait_ge(*M.full(g, "y3"))
                ps = M.bank("y3")
                dve.tensor_tensor(flat(x_out[:, :, :]), ps[:, :], flat(x[:, :, :]), ALU.add).then_inc(M.free_sem("y3"), 1)
                dve.wait_ge(*M.drained(g, "y3"))
                yield
                assert dve_chain.n == DVE_LINKS, dve_chain.n

            def prologue():
                front_norm_a(0)
                front_norm_b(0, FIRST, 0)

            run(dve, prologue, front, back)


def kernel(**inputs):
    import numpy as np
    import concourse.bacc as bacc
    from concourse.bass_utils import run_bass_kernel_spmd

    nc = bacc.Bacc("TRN2", target_bir_lowering=False, num_devices=1)
    arrays, t = {}, {}
    for name, a in inputs.items():
        a = np.ascontiguousarray(a)
        a = a.reshape(1) if a.shape == () else a
        arrays[f"in_{name}"] = a
        t[name] = nc.dram_tensor(f"in_{name}", a.shape, mybir.dt.from_np(a.dtype), kind="ExternalInput").ap()
    out = nc.dram_tensor("out_0", (B, D, D), F32, kind="ExternalOutput").ap()
    build(nc, t, out)
    r = run_bass_kernel_spmd(nc, [arrays], core_ids=[0])
    return r.results[0]["out_0"]
```

```python
from collections import namedtuple
from contextlib import ExitStack

import concourse.bass as bass
from concourse import mybir

F32 = mybir.dt.float32
I32 = mybir.dt.int32
ALU = mybir.AluOpType
ACT = mybir.ActivationFunctionType
AX = mybir.AxisListType

D = 128
B = 32
G = 4
NG = B // G
T = G * D
H0, DH0 = 16, 64
C0 = H0 * DH0 // D
H2, DH2 = 16, 8
FF = 4
NK3 = 20
L3 = 11
H3, DH3 = 16, 8
HC = 6
CH3 = [(0, 6), (6, 6), (12, 4)]
NEG = -9000000000000000.0
EPS = (1e-5, 1e-5, 1e-6, 1e-6, 1e-5, 1e-5)
RMS = (False, False, True, True, False, False)

BIAS_ROWS = [("L0_cond_b_mod", 6), ("L1_cond_film1_b", 2), ("L1_cond_film2_b", 2), ("L2_cond_b_ada", 6),
             ("L0_cond_b_out", 1), ("L0_cond_b1", 4), ("L0_cond_b2", 1), ("L1_cond_norm1_w", 1),
             ("L1_cond_norm2_w", 1), ("L1_cond_q_b", 1), ("L1_cond_k_b", 1), ("L1_cond_v_b", 1),
             ("L1_cond_proj_b", 1), ("L1_cond_mlp_b1", 4), ("L1_cond_mlp_b2", 1), ("L2_cond_bq", 1),
             ("L2_cond_bk", 1), ("L2_cond_bv", 1), ("L2_cond_bo", 1), ("L2_cond_b1", 4), ("L2_cond_b2", 1),
             ("L3_cond_b_self", 1), ("L3_cond_bq", 2), ("L3_cond_bk", 2), ("L3_cond_bout", 2)]
ROW = {}
_n = 0
for _name, _k in BIAS_ROWS:
    ROW[_name] = _n
    _n += _k
NROWS = _n
NMOD = 16
SHIFT = (0, 3, 7, 9, 10, 13)
SCALE = (1, 4, 6, 8, 11, 14)
GATE = {"o0": 2, "g0": 5, "o2": 12, "g2": 15}

UA = 2 * C0
UB = G * H2 // 4
NJ = 2 * G
NP = 4
NPF = 3
MID_LINKS = 9
BACK_LINKS = 16
PIECES = [(0, e, 20) for e in range(0, G * NK3, 20)] + [(1, e, 16) for e in range(0, D, 16)]

ATT_STEPS = UA + 4
L2_STEPS = UB + 3
L3_STEPS = NJ + 5
STEPS = {"F": 2 * ATT_STEPS + 4, "M": 6 + 9 + 5, "B": 4 + L2_STEPS + 2 + 6 + 4 + L3_STEPS + 2}
SCHEDULE = ("BMBFMFBFMFBBFFBFFMBFBMBFFBFMBBFBFMBFMBBFBFBFMBFBFBMBBFBFMBFBFMBFBMFBFBMBFBMBFMBFFBMFBMFBFF"
            "BFBMFFBFBBFFBBMBFBBFFBBB")
START_SCHEDULE = ("MFFMFMFFFFFMFMFFFMFFMFMFFFMFFMFFMFFMFMFMFMFFFMFMFMFFFFMFFFFFMFFF")
END_SCHEDULE = ("BMBMBMBBBMBBMBBMBBBMBMBBBBMBBBMBBBMMBBMBBMBBMBBMBMBBBMBBBMBBBBBMBBBBBB")


def place(schedule, stream, n):
    return [i for i, s in enumerate(schedule) if s == stream][n]


for _order in (SCHEDULE, START_SCHEDULE, END_SCHEDULE):
    assert all(_order.count(s) in (0, n) for s, n in STEPS.items())
    assert "B" not in _order or place(_order, "M", STEPS["M"] - 1) > place(_order, "B", 4 + L2_STEPS + 1)
    assert "F" not in _order or place(_order, "F", STEPS["F"] - 1) > place(_order, "M", 5)


def in_turn(uses, banks):
    return [(use, banks[i % len(banks)]) for i, use in enumerate(uses)]


class Ring:

    def __init__(self, nc, ctx, name, banks, uses, ps=None):
        self.ps = ps or [ctx.enter_context(nc.psum_tensor(f"{name}{i}", [D, T], F32)) for i in range(banks)]
        self.full_sems = [ctx.enter_context(nc.semaphore(f"{name}{i}_full")) for i in range(banks)]
        self.free_sems = [ctx.enter_context(nc.semaphore(f"{name}{i}_free")) for i in range(banks)]
        self.at = {}
        self.per = [0] * banks
        for use, bank in uses:
            self.at[use] = (bank, self.per[bank])
            self.per[bank] += 1

    def bank(self, use):
        return self.ps[self.at[use][0]]

    def full_sem(self, use):
        return self.full_sems[self.at[use][0]]

    def free_sem(self, use):
        return self.free_sems[self.at[use][0]]

    def count(self, it, use):
        b, n = self.at[use]
        return it * self.per[b] + n

    def empty(self, it, use):
        return self.free_sem(use), self.count(it, use) + 1

    def full(self, it, use):
        return self.full_sem(use), self.count(it, use) + 1

    def drained(self, it, use):
        return self.free_sem(use), self.count(it, use) + 2

    def last_in_banks(self, uses):
        return {self.at[u][0]: u for u in uses}.values()


class Count:

    def __init__(self, nc, ctx, name, per):
        self.sem = ctx.enter_context(nc.semaphore(name))
        self.per = per

    def nth(self, it, n):
        return self.sem, it * self.per + n + 1


class Chain:

    def __init__(self, nc, ctx, name, per):
        self.sem = ctx.enter_context(nc.semaphore(name))
        self.per = per
        self.n = 0

    def last(self, it):
        self.n += 1
        return self.sem, it * self.per + self.n


Part = namedtuple("Part", "ring x z hT yT hid qk oT v1 probs probsT negmax rsum rinv gmod stat norm0 "
                          "var_ready rstd_ready z_ready max_ready rinv_ready normed chain")


def weave(schedule, streams):
    for letter in schedule:
        next(streams[letter])
    for stream in streams.values():
        assert next(stream, "end") == "end"


def build(nc, t, out):
    front_uses = []
    for s in range(ATT_STEPS):
        if s // 2 < C0:
            front_uses += [(f"q_{s // 2}", 0), (f"k_{s // 2}", 1)] if s % 2 == 0 else [(f"v_{s // 2}", 1)]
        if 0 <= s - 2 < UA:
            front_uses.append((("S", s - 2), 2))
        if s == UA + 2:
            front_uses.append(("ln0", 1))
        if 0 <= s - 3 < UA:
            front_uses.append((("T", s - 3), 0))
        if s >= 5 and s % 2 == 1 and (s - 5) // 2 < C0:
            front_uses.append((f"a_{(s - 5) // 2}", 1))
    front_uses += [("o0", 0), ("y0", 1)]

    def mlp_uses(l):
        return [f"ln{2 * l + 1}"] + [f"f{l}_{c}" for c in range(FF)] + ([f"g{l}"] if l == 1 else [f"g{l}", f"z{l}"])

    mid_uses = in_turn(mlp_uses(0) + ["ln2", "q1", "k1", "v1", ("A", 0), ("T", 0), "a1", "o1"] + mlp_uses(1), [0, 1])
    back_uses = in_turn(["ln4", "k2", "q2", "v2"], range(3))
    back_uses += [("a2", 0)] + in_turn([("T", u) for u in range(UB)], [1]) + in_turn([("A", u) for u in range(UB)], [2])
    back_uses += in_turn(["o2", "y2"] + mlp_uses(2) + ["adj", "xt3", "sum3", "self3", "q3_0", "q3_1", "k3"], range(3))
    back_uses += in_turn([f"vbd_{c}_{i}" for c in range(3) for i in range(G // 2)], [0, 1])
    back_uses += [("a3", 0)] + in_turn([("S3", j) for j in range(NJ)], [2]) + in_turn([("T3", j) for j in range(NJ)], [1])
    back_uses += [("y3", 2)]

    with ExitStack() as ctx:
        def sb(name, shape, dt=F32):
            return ctx.enter_context(nc.sbuf_tensor(name, shape, dt))

        def sem(name):
            return ctx.enter_context(nc.semaphore(name))

        def count(name, per):
            return Count(nc, ctx, name, per)

        def flat(ap):
            return ap.rearrange("p a b -> p (a b)")

        def wide(ap, n):
            p, a = ap.shape
            return ap.unsqueeze(2).to_broadcast([p, a, n])

        def tok(b):
            return slice(b * D, (b + 1) * D)

        w_qkv = sb("w_qkv", [D, 3 * H0 * DH0])
        w_out = sb("w_out", [D, C0, D])
        w_up = sb("w_up", [D, 3, FF * D])
        w_down = sb("w_down", [D, 3, FF, D])
        w_l1 = sb("w_l1", [D, 4, D])
        w_l2 = sb("w_l2", [D, 4, D])
        w3 = sb("w3", [D, 8, D])
        col = sb("col", [D, NROWS])
        condT = sb("condT", [D, 2, B])
        mod = sb("mod", [D, NMOD, B + G])
        bout3 = sb("bout3", [D, 1])
        ident = sb("ident", [D, D])
        ones = sb("ones", [D, D])
        held = sb("held", [D, 2])
        half = sb("half", [D, G])
        head16 = sb("head16", [D, H3])
        head4 = sb("head4", [D, 4])
        blk3 = sb("blk3", [HC * NK3, 3, H3, DH3])
        labels3 = sb("labels3", [D, L3 + 1])
        wlab = labels3[:, 0:L3]
        blab = labels3[:, L3:L3 + 1]
        rows1 = sb("rows1", [D, 2, D])

        x_norm = sb("x_norm", [D, G, D])
        x_res = sb("x_res", [D, G, D])
        fmod = sb("fmod", [D, 3, G])
        fz = sb("fz", [D, G, D])
        fhT = sb("fhT", [D, T])
        fq = sb("fq", [D, 2, T])
        fk = sb("fk", [D, 2, 2, T])
        fv = sb("fv", [D, 3, G, D])
        fattnT = sb("fattnT", [D, C0, T])
        w_mod = fattnT[:, 0:4, :].rearrange("p c (k d) -> p (c k) d", d=D)
        w3_raw = fattnT[:, 4:6, :].rearrange("p c (k d) -> p (c k) d", d=D)
        bias_rows = fattnT[0:NROWS, 6, 0:D]
        cond_raw = fattnT[0:B, 6, D:2 * D]
        cond = fattnT[0:B, 6, 2 * D:4 * D].rearrange("p (a d) -> p a d", a=2)
        fyT = flat(fz[:, :, :])
        fprobs = sb("fprobs", [D, NPF, 4, D])
        fprobsT = sb("fprobsT", [D, NPF, 4, D])
        fnegmax = sb("fnegmax", [D, UA, 4])
        frsum = sb("frsum", [D, UA, 4])
        frinv = sb("frinv", [D, UA, 4])

        mx = sb("mx", [D, G, D])
        mz = sb("mz", [D, G, D])
        mhT = sb("mhT", [D, T])
        mhid = sb("mhid", [D, FF, T])
        mgmod = sb("mgmod", [D, NMOD, G])
        msums = sb("msums", [D, 3, 1, 4])

        x1 = sb("x1", [D, G, D])
        x = sb("x", [D, G, D])
        z = sb("z", [D, G, D])
        x_out = z
        gmod = sb("gmod", [D, NMOD, G])
        gcond = sb("gcond", [D, G])
        stats = sb("stats", [D, 3, G, 6])
        mv = sb("mv", [D, 3, G, 2])
        msq = sb("msq", [D, G])
        veps = sb("veps", [D, 3, G])
        rstd = sb("rstd", [D, 3, G])
        hT = sb("hT", [D, T])
        oT = hT
        yT = flat(z[:, :, :])
        qk = sb("qk", [D, 2, T])
        hid = sb("hid", [D, FF, T])
        v1 = hid[:, 2, :].rearrange("p (b d) -> p b d", b=G)
        prob_space = sb("prob_space", [D, 2 * NP, T])
        probs = prob_space[:, 0:NP, :].rearrange("p s (i k) -> p s i k", i=4)
        probsT = prob_space[:, NP:2 * NP, :].rearrange("p s (i k) -> p s i k", i=4)
        negmax = sb("negmax", [D, UB, 4])
        rsum = sb("rsum", [D, UB, 4])
        rinv = sb("rinv", [D, UB, 4])
        km_space = sb("km_space", [D, 5, T])
        km = km_space[:, 0:4, :]
        VW = H2 * (D + DH2)
        vm = sb("vm", [D, 2, VW])
        adj0 = sb("adj0", [D, G * NK3 * L3], I32)
        adj1 = sb("adj1", [G * NK3, D * L3], I32)
        PW = max(n for _, _, n in PIECES) * L3
        adjf = sb("adjf", [D, 2, PW])
        adjw = sb("adjw", [D, 2, PW])
        edge0 = sb("edge0", [D, 2, 2, G * NK3])
        edge1 = sb("edge1", [G * NK3, 2, D])
        keep = sb("keep", [D, 2, G * NK3])
        nbias = sb("nbias", [D, 2, G * NK3])
        k3 = sb("k3", [D, 2, G * NK3])
        vbd = sb("vbd", [HC * NK3, 3, G, 2, D])
        nmax3 = sb("nmax3", [D, NJ, H3])
        rsum3 = sb("rsum3", [D, NJ, H3])
        rinv3 = sb("rinv3", [D, NJ, H3])
        p3 = flat(prob_space[:, 0:5, :]).rearrange("p (j h m) -> p j h m", j=NJ, h=H3)
        x3T = prob_space[:, 5, :]
        qx = prob_space[:, 6, :]
        sT = prob_space[:, 7, :]
        kbd = flat(km_space[:, :, :]).rearrange("p (d b h m) -> p d b h m", d=2, b=G, h=H3)
        q3 = qk
        kvrep = flat(hid[:, :, :])[:, 0:G * H3 * NK3].rearrange("p (b h m) -> p b h m", b=G, h=H3)
        p3T = flat(hid[0:HC * NK3, :, :])[:, G * H3 * NK3:].rearrange("p (s c q) -> p s c q", s=2, c=3)

        FM = Ring(nc, ctx, "front", 3, front_uses)
        MM = Ring(nc, ctx, "middle", 2, mid_uses)
        BM = Ring(nc, ctx, "back", 3, back_uses)
        SETUP = BM.ps + [MM.ps[0]]
        FIRST = Ring(nc, ctx, "first_norm", 1, [("ln0", 0)], ps=[MM.ps[1]])

        w_qkv_in = sem("w_qkv_in")
        weights_in = sem("weights_in")
        cond_in = sem("cond_in")
        mod_in = sem("mod_in")
        layer3_in = sem("layer3_in")
        pool_setup = sem("pool_setup")
        consts_ready = sem("consts_ready")
        silu_ready = sem("silu_ready")
        dve_setup = sem("dve_setup")
        pe_setup = sem("pe_setup")
        setup_done = sem("setup_done")
        x_norm_in = sem("x_norm_in")
        x_res_in = sem("x_res_in")
        adj_loaded = sem("adj_loaded")
        x_stored = sem("x_stored")
        fmod_ready = count("fmod_ready", 1)
        fvar_ready = count("fvar_ready", 1)
        fgate_ready = count("fgate_ready", 1)
        frstd_ready = count("frstd_ready", 1)
        fz_ready = count("fz_ready", 1)
        fmax_ready = count("fmax_ready", UA)
        frinv_ready = count("frinv_ready", UA)
        fnormed = count("fnormed", UA)
        xb_ready = count("xb_ready", 2)
        km_ready = count("km_ready", G)
        vm_ready = count("vm_ready", G)
        vm_used = count("vm_used", G - 1)
        adjf_ready = count("adjf_ready", len(PIECES))
        adjw_ready = count("adjw_ready", len(PIECES))
        adj_summed = count("adj_summed", len(PIECES))
        kbd_ready = count("kbd_ready", G)
        kvrep_ready = count("kvrep_ready", 1)
        bias_ready = count("bias_ready", 1)
        biased3 = count("biased3", NJ)
        max3_ready = count("max3_ready", NJ)
        shifted3 = count("shifted3", NJ)
        exp3_ready = count("exp3_ready", NJ)
        rinv3_ready = count("rinv3_ready", NJ)
        normed3 = count("normed3", NJ)
        rel_ready = count("rel_ready", 1)
        front_chain = Chain(nc, ctx, "front_chain", 2)

        def part(name, units, norms, links, **tiles):
            counts = {f"{c}_ready": count(f"{name}_{c}_ready", norms) for c in ("var", "rstd", "z")}
            counts |= {c: count(f"{name}_{c}", units) for c in ("max_ready", "rinv_ready", "normed")}
            return Part(**tiles, **counts, chain=Chain(nc, ctx, f"{name}_chain", links))

        MID = part("mid", 1, 3, MID_LINKS, ring=MM, x=mx, z=mz, hT=mhT, yT=flat(mz[:, :, :]), hid=mhid,
                   qk=mhid[:, 0:2, :], oT=mhid[:, 3, :], v1=mhid[:, 2, :].rearrange("p (b d) -> p b d", b=G),
                   probs=mhid[:, 3:4, :].rearrange("p s (i k) -> p s i k", i=4),
                   probsT=mhT.rearrange("p (s i k) -> p s i k", s=1, i=4), negmax=msums[:, 0, :, :],
                   rsum=msums[:, 1, :, :], rinv=msums[:, 2, :, :], gmod=mgmod, stat=1, norm0=1)
        BACK = part("back", UB, 2, BACK_LINKS, ring=BM, x=x, z=z, hT=hT, yT=yT, hid=hid, qk=qk, oT=oT, v1=v1, probs=probs,
                    probsT=probsT, negmax=negmax, rsum=rsum, rinv=rinv, gmod=gmod, stat=2, norm0=4)

        def edge_views(p):
            d, e0, n = PIECES[p]
            rows = G * NK3 if d else D
            loaded = (adj1 if d else adj0)[:, e0 * L3:(e0 + n) * L3]
            copies = [a[0:rows, p % 2, 0:n * L3] for a in (adjf, adjw)]
            return [a.rearrange("p (e l) -> p e l", l=L3) for a in [loaded] + copies]

        block = ctx.enter_context(nc.Block())

        @block.sync
        def _(sp):
            def group(dram, g):
                return dram[bass.ds(g * G, G)].rearrange("b t d -> t b d")

            def load_norm(g):
                sp.dma_start(x_norm[:, :, :], group(t["x"], g)).then_inc(x_norm_in, 16)

            def load_res(g):
                sp.dma_start(x_res[:, :, :], group(t["x"], g)).then_inc(x_res_in, 16)

            mask = t["mask_BxSxSx11_ik0"]

            def load_edges(g):
                sp.dma_start(adj0[:, :].rearrange("n (b k) -> n b k", b=G),
                             mask[bass.ds(g * G, G), :, 0:NK3, :].rearrange("b n m l -> n b (m l)")).then_inc(adj_loaded, 16)
                for b in range(G):
                    sp.dma_start(adj1[b * NK3:(b + 1) * NK3, :],
                                 mask[bass.ds(g * G + b, 1), 0:NK3, :, :].rearrange("b m n l -> (b m) (n l)")).then_inc(adj_loaded, 16)

            def store(g):
                sp.wait_ge(*BM.drained(g, "y3"))
                sp.dma_start(group(out, g), x_out[:, :, :]).then_inc(x_stored, 16)

            load_norm(0)
            sp.dma_start(cond_raw[:, :], t["cond_1024"]).then_inc(cond_in, 16)
            sp.dma_start(bias_rows[:, :], t["bias_rows"]).then_inc(mod_in, 16)
            sp.dma_start(w_mod[:, :, :], t["w_mod"].rearrange("i (k d) -> i k d", d=D)).then_inc(mod_in, 16)
            sp.dma_start(w3_raw[:, :, :], t["w3"].rearrange("o (k i) -> o k i", i=D)).then_inc(layer3_in, 16)
            sp.dma_start(labels3[:, :], t["labels3"].to_broadcast([D, L3 + 1])).then_inc(layer3_in, 16)
            sp.dma_start(rows1[:, :, :].rearrange("p a d -> p (a d)"), t["rows1"].to_broadcast([D, 2 * D])).then_inc(layer3_in, 16)
            load_res(0)
            load_edges(0)
            sp.wait_ge(*fz_ready.nth(0, 0))
            load_norm(1)
            sp.wait_ge(*MM.drained(0, "z0"))
            load_res(1)
            sp.wait_ge(*fz_ready.nth(1, 0))
            load_norm(2)
            with sp.Fori(2, NG - 1) as it:
                sp.wait_ge(*MM.drained(it - 1, "z0"))
                load_res(it)
                sp.wait_ge(*adj_summed.nth(it - 2, len(PIECES) - 1))
                load_edges(it - 1)
                sp.wait_ge(*fz_ready.nth(it, 0))
                load_norm(it + 1)
                store(it - 2)
            sp.wait_ge(*MM.drained(NG - 2, "z0"))
            load_res(NG - 1)
            sp.wait_ge(*adj_summed.nth(NG - 3, len(PIECES) - 1))
            load_edges(NG - 2)
            sp.wait_ge(*fz_ready.nth(NG - 1, 0))
            load_norm(NG - 1)
            store(NG - 3)
            sp.wait_ge(*adj_summed.nth(NG - 2, len(PIECES) - 1))
            load_edges(NG - 1)
            store(NG - 2)
            store(NG - 1)
            sp.wait_ge(x_norm_in, 16 * (NG + 1))
            sp.wait_ge(x_stored, 16 * NG + 16)

        NWEIGHTS = 5

        def run(eng, prologue, front, rest):
            def mid(g):
                return rest(g, MID)

            def last(g):
                return rest(g, BACK)

            prologue()
            weave("F" * STEPS["F"], {"F": front(0)})
            weave(START_SCHEDULE, {"F": front(1), "M": mid(0)})
            with eng.Fori(2, NG) as it:
                weave(SCHEDULE, {"F": front(it), "M": mid(it - 1), "B": last(it - 2)})
            weave(END_SCHEDULE, {"M": mid(NG - 1), "B": last(NG - 2)})
            weave("B" * STEPS["B"], {"B": last(NG - 1)})

        @block.gpsimd
        def _(pool):
            n = [0]

            def step(ins):
                ins.then_inc(pool_setup, 1)
                n[0] += 1
                pool.wait_ge(pool_setup, n[0])

            def front_rsqrt(g):
                pool.wait_ge(*fvar_ready.nth(g, 0))
                pool.tensor_tensor(rstd[:, 0, :], veps[:, 0, :], half[:, :], ALU.pow).then_inc(frstd_ready.sem, 1)

            step(pool.memset(ident[:, :], 0.0))
            step(pool.affine_select(out=ident[:, :], in_=ident[:, :], compare_op=ALU.not_equal, fill=1.0,
                                    base=0, pattern=[[-1, D]], channel_multiplier=1))
            step(pool.memset(ones[:, :], 1.0))
            step(pool.memset(half[:, :], -0.5))
            step(pool.memset(fk[:, :, :, :], 0.0))
            front_rsqrt(0)
            step(pool.memset(vm[:, :, :], 0.0))
            step(pool.memset(head16[:, :], 1.0))
            step(pool.affine_select(out=head16[:, :], in_=head16[:, :], compare_op=ALU.is_ge, fill=0.0,
                                    base=0, pattern=[[-DH3, H3]], channel_multiplier=1))
            step(pool.affine_select(out=head16[:, :], in_=head16[:, :], compare_op=ALU.is_ge, fill=0.0,
                                    base=DH3 - 1, pattern=[[DH3, H3]], channel_multiplier=-1))
            step(pool.memset(blk3[:, :, :, :], 1.0))
            step(pool.affine_select(out=blk3[:, :, :, :], in_=blk3[:, :, :, :], compare_op=ALU.is_ge, fill=0.0,
                                    base=0, pattern=[[HC * NK3, 3], [-NK3, H3], [0, DH3]], channel_multiplier=1))
            pool.affine_select(out=blk3[:, :, :, :], in_=blk3[:, :, :, :], compare_op=ALU.is_ge, fill=0.0,
                               base=NK3 - 1, pattern=[[-HC * NK3, 3], [NK3, H3], [0, DH3]],
                               channel_multiplier=-1).then_inc(consts_ready, 1)
            pool.wait_ge(setup_done, 1)

            def front(g):
                for s in range(ATT_STEPS):
                    if 0 <= s - 3 < UA:
                        pool.wait_ge(*frinv_ready.nth(g, s - 3))
                        p = fprobs[:, (s - 3) % NPF, :, :]
                        pool.tensor_tensor(p, p, wide(frinv[:, s - 3, :], D), ALU.mult).then_inc(fnormed.sem, 1)
                    yield
                    if s == UA:
                        front_rsqrt(g + 1)
                    yield
                for _ in range(4):
                    yield

            def rest(g, part):
                M, x, z, qk, probs, rinv = part.ring, part.x, part.z, part.qk, part.probs, part.rinv

                def edges(tick):
                    p = tick - 2
                    if not 0 <= p < len(PIECES):
                        return
                    pool.wait_ge(*adjf_ready.nth(g, p))
                    if p >= 2:
                        pool.wait_ge(*adj_summed.nth(g, p - 2))
                    _, labels, weighted = edge_views(p)
                    rows, n, _ = labels.shape
                    wl = wlab[0:rows, :].unsqueeze(1).to_broadcast([rows, n, L3])
                    pool.tensor_tensor(weighted, labels, wl, ALU.mult).then_inc(adjw_ready.sem, 1)

                def rsqrt(k):
                    pool.wait_ge(*part.var_ready.nth(g, k - part.norm0))
                    pool.tensor_tensor(rstd[:, part.stat, :], veps[:, part.stat, :], half[:, :], ALU.pow).then_inc(part.rstd_ready.sem, 1)

                def norm(u):
                    pool.wait_ge(*part.rinv_ready.nth(g, u))
                    p = probs[:, u % NP, :, :]
                    pool.tensor_tensor(p, p, wide(rinv[:, u, :], D), ALU.mult).then_inc(part.normed.sem, 1)

                def residual(i):
                    pool.wait_ge(*M.drained(g, f"ln{2 + i}"))
                    row = rows1[:, i, :].unsqueeze(1).to_broadcast([D, G, D])
                    pool.tensor_tensor(z[:, :, :], x[:, :, :], row, ALU.add).then_inc(xb_ready.sem, 1)

                def head_keys(b):
                    kb = qk[:, 1, tok(b)].unsqueeze(1).to_broadcast([D, 4, D])
                    pool.tensor_tensor(km[:, :, tok(b)], kb, wide(head4[:, :], D), ALU.mult).then_inc(km_ready.sem, 1)

                def block_keys(b):
                    for d in range(2):
                        kk = k3[:, d, b * NK3:(b + 1) * NK3].unsqueeze(1).to_broadcast([D, H3, NK3])
                        ins = pool.tensor_tensor(kbd[:, d, b, :, :], kk, wide(head16[:, :], NK3), ALU.mult)
                    ins.then_inc(kbd_ready.sem, 1)

                def mlp(l):
                    rsqrt(2 * l + 1)
                    for step in range(5 if l == 1 else 6):
                        if l == 1 and step == 3:
                            residual(1)
                        yield

                def layer1():
                    rsqrt(2)
                    for step in range(9):
                        if step == 3:
                            residual(0)
                        if step == 5:
                            norm(0)
                        yield

                def layer2():
                    rsqrt(4)
                    yield
                    yield
                    yield
                    pool.wait_ge(*M.drained(g, "k2"))
                    head_keys(0)
                    yield
                    for s in range(L2_STEPS):
                        if 0 <= s - 1 < UB:
                            norm(s - 1)
                        if s % 4 == 1 and s // 4 + 1 < G:
                            head_keys(s // 4 + 1)
                        yield
                    yield
                    yield

                if part is MID:
                    yield from mlp(0)
                    yield from layer1()
                    yield from mlp(1)
                    return
                for tick, _ in enumerate(layer2()):
                    edges(tick)
                    yield
                yield from mlp(2)
                yield
                yield
                yield
                pool.wait_ge(*M.drained(g, "k3"))
                block_keys(0)
                yield
                for s in range(L3_STEPS):
                    if 0 <= s - 3 < NJ:
                        j = s - 3
                        pool.wait_ge(*rinv3_ready.nth(g, j))
                        pool.tensor_tensor(p3[:, j, :, :], p3[:, j, :, :], wide(rinv3[:, j, :], NK3),
                                           ALU.mult).then_inc(normed3.sem, 1)
                    if 0 <= s - 1 < NJ:
                        j = s - 1
                        pool.wait_ge(*max3_ready.nth(g, j))
                        pool.tensor_tensor(p3[:, j, :, :], p3[:, j, :, :], wide(nmax3[:, j, :], NK3),
                                           ALU.add).then_inc(shifted3.sem, 1)
                    if s % 2 == 0 and s // 2 + 1 < G:
                        block_keys(s // 2 + 1)
                    yield
                yield
                yield

            run(pool, lambda: None, front, rest)

        @block.scalar
        def _(act):
            act.dma_start(w_qkv[:, :], t["L0_cond_W_qkv"]).then_inc(w_qkv_in, 16)
            act.wait_ge(cond_in, 16)
            act.activation(cond[:, 0, :], cond_raw[:, :], ACT.Silu).then_inc(silu_ready, 1)
            act.activation(cond[:, 1, :], cond_raw[:, :], ACT.Copy).then_inc(silu_ready, 1)
            act.wait_ge(mod_in, 32)
            for dst, src in ((w_out[:, :, :], t["L0_cond_W_out"].rearrange("(c p) d -> p c d", p=D)),
                             (w_up[:, :, :], t["w_up"].rearrange("i (l f) -> i l f", l=3)),
                             (w_down[:, :, :, :].rearrange("p l c d -> p (l c) d"), t["w_down"].rearrange("(k p) d -> p k d", p=D)),
                             (w_l1[:, :, :], t["w_l1"].rearrange("i (k d) -> i k d", d=D)),
                             (w_l2[:, :, :], t["w_l2"].rearrange("i (k d) -> i k d", d=D))):
                act.dma_start(dst, src).then_inc(weights_in, 16)
            act.wait_ge(setup_done, 1)

            def front(g):
                for s in range(ATT_STEPS):
                    if s % 2 == 0 and s // 2 < C0:
                        c = s // 2
                        act.wait_ge(*FM.full(g, f"k_{c}"))
                        ps = FM.bank(f"k_{c}")
                        for r in range(2):
                            rows = slice(r * DH0, (r + 1) * DH0)
                            ins = act.activation(fk[rows, c % 2, r, :], ps[rows, :], ACT.Copy)
                        ins.then_inc(FM.free_sem(f"k_{c}"), 1)
                    if 0 <= s - 2 < UA:
                        u = s - 2
                        act.wait_ge(*fmax_ready.nth(g, u))
                        if u >= NPF:
                            act.wait_ge(*FM.full(g, ("T", u - NPF)))
                        ps = FM.bank(("S", u))
                        for i in range(4):
                            ins = act.activation(fprobs[:, u % NPF, i, :], ps[:, tok(i)], ACT.Exp,
                                                 bias=fnegmax[:, u, i:i + 1], accum_out=frsum[:, u, i:i + 1])
                        ins.then_inc(FM.free_sem(("S", u)), 1)
                    yield
                    if 0 <= s - 3 < UA:
                        u = s - 3
                        act.wait_ge(*FM.full(g, ("T", u)))
                        ps = FM.bank(("T", u))
                        act.activation(flat(fprobsT[:, u % NPF, :, :]), ps[:, :], ACT.Copy).then_inc(FM.free_sem(("T", u)), 1)
                    yield
                for _ in range(4):
                    yield

            def rest(g, part):
                M, qk, hid, probs, probsT = part.ring, part.qk, part.hid, part.probs, part.probsT

                def biased(use, dst, b):
                    act.wait_ge(*M.full(g, use))
                    ps = M.bank(use)
                    act.activation(dst, ps[:, :], ACT.Identity, bias=col[:, b:b + 1]).then_inc(M.free_sem(use), 1)

                def exps(u):
                    act.wait_ge(*part.max_ready.nth(g, u))
                    if u >= NP:
                        act.wait_ge(*M.full(g, ("T", u - NP)))
                    ps = M.bank(("A", u))
                    for i in range(4):
                        ins = act.activation(probs[:, u % NP, i, :], ps[:, tok(i)], ACT.Exp,
                                             bias=part.negmax[:, u, i:i + 1], accum_out=part.rsum[:, u, i:i + 1])
                    ins.then_inc(M.free_sem(("A", u)), 1)

                def probs_out(u):
                    act.wait_ge(*M.full(g, ("T", u)))
                    ps = M.bank(("T", u))
                    act.activation(flat(probsT[:, u % NP, :, :]), ps[:, :], ACT.Copy).then_inc(M.free_sem(("T", u)), 1)

                def mlp(l, b1):
                    yield
                    yield
                    yield
                    for c in range(FF):
                        act.wait_ge(*M.full(g, f"f{l}_{c}"))
                        ps = M.bank(f"f{l}_{c}")
                        act.activation(hid[:, c, :], ps[:, :], ACT.Gelu,
                                       bias=col[:, b1 + c:b1 + c + 1]).then_inc(M.free_sem(f"f{l}_{c}"), 1)
                    yield
                    yield
                    if l != 1:
                        yield

                def edges(tick):
                    p = tick - 1
                    if not 0 <= p < len(PIECES):
                        return
                    if p == 0:
                        act.wait_ge(adj_loaded, (g + 1) * (16 * (1 + G)))
                    if p >= 2:
                        act.wait_ge(*adj_summed.nth(g, p - 2))
                    loaded, labels, _ = edge_views(p)
                    act.activation(labels, loaded, ACT.Copy).then_inc(adjf_ready.sem, 1)

                def layer1():
                    yield
                    yield
                    yield
                    biased("k1", qk[:, 1, :], ROW["L1_cond_k_b"])
                    yield
                    exps(0)
                    yield
                    yield
                    probs_out(0)
                    yield
                    yield
                    yield

                def layer2():
                    yield
                    yield
                    yield
                    biased("k2", qk[:, 1, :], ROW["L2_cond_bk"])
                    yield
                    for s in range(L2_STEPS):
                        if 0 <= s - 2 < UB:
                            probs_out(s - 2)
                        if s < UB:
                            exps(s)
                        yield
                    yield
                    yield

                if part is MID:
                    yield from mlp(0, ROW["L0_cond_b1"])
                    yield from layer1()
                    yield from mlp(1, ROW["L1_cond_mlp_b1"])
                    return
                for tick, _ in enumerate(layer2()):
                    edges(tick)
                    yield
                yield from mlp(2, ROW["L2_cond_b1"])
                act.wait_ge(*M.full(g, "xt3"))
                ps = M.bank("xt3")
                act.activation(x3T, ps[:, :], ACT.Copy).then_inc(M.free_sem("xt3"), 1)
                yield
                yield
                yield
                yield
                for s in range(L3_STEPS):
                    if 0 <= s - 4 < NJ:
                        j = s - 4
                        act.wait_ge(*M.full(g, ("T3", j)))
                        ps = M.bank(("T3", j))
                        act.activation(p3T[:, j % 2, 0:2, :], ps[0:HC * NK3, 0:2 * D].rearrange("p (c q) -> p c q", c=2), ACT.Copy)
                        rows = CH3[2][1] * NK3
                        act.activation(p3T[0:rows, j % 2, 2, :], ps[0:rows, 2 * D:3 * D],
                                       ACT.Copy).then_inc(M.free_sem(("T3", j)), 1)
                    if 0 <= s - 2 < NJ:
                        act.wait_ge(*shifted3.nth(g, s - 2))
                        act.activation(p3[:, s - 2, :, :], p3[:, s - 2, :, :], ACT.Exp).then_inc(exp3_ready.sem, 1)
                    yield
                yield
                yield

            run(act, lambda: None, front, rest)

        @block.tensor
        def _(pe):
            def turn(ring, g, use, src):
                pe.wait_ge(*ring.empty(g, use))
                ps = ring.bank(use)
                for b in range(G):
                    ins = pe.transpose(ps[:, tok(b)], src[:, b, :] if len(src.shape) == 3 else src[:, tok(b)], ident[:, :])
                ins.then_inc(ring.full_sem(use), 1)

            def front_norm(g, ring, ring_g):
                pe.wait_ge(*fz_ready.nth(g, 0))
                turn(ring, ring_g, "ln0", fz)

            def front(g):
                def linear(use, w):
                    pe.wait_ge(*FM.empty(g, use))
                    ps = FM.bank(use)
                    pe.matmul(ps[:, :], w, fhT[:, :], start=True, stop=True).then_inc(FM.full_sem(use), 1)

                for s in range(ATT_STEPS):
                    if s // 2 < C0:
                        c = s // 2
                        if s % 2 == 0:
                            linear(f"q_{c}", w_qkv[:, tok(c)])
                            linear(f"k_{c}", w_qkv[:, tok(C0 + c)])
                        else:
                            pe.wait_ge(*FM.empty(g, f"v_{c}"))
                            ps = FM.bank(f"v_{c}")
                            for b in range(G):
                                ins = pe.matmul(ps[:, tok(b)], fhT[:, tok(b)], w_qkv[:, tok(2 * C0 + c)], start=True, stop=True)
                            ins.then_inc(FM.full_sem(f"v_{c}"), 1)
                    if 0 <= s - 2 < UA:
                        u = s - 2
                        c = u // 2
                        if u % 2 == 0:
                            for use in FM.last_in_banks([f"q_{c}", f"k_{c}"]):
                                pe.wait_ge(*FM.drained(g, use))
                        pe.wait_ge(*FM.empty(g, ("S", u)))
                        ps = FM.bank(("S", u))
                        for i in range(2):
                            b = 2 * (u % 2) + i
                            ins = pe.matmul(ps[:, 2 * i * D:2 * (i + 1) * D], fq[:, c % 2, tok(b)], fk[:, c % 2, :, tok(b)],
                                            start=True, stop=True)
                        ins.then_inc(FM.full_sem(("S", u)), 1)
                    if s == UA + 2:
                        front_norm(g + 1, FM, g)
                    yield
                    if s >= 5 and s % 2 == 1 and (s - 5) // 2 < C0:
                        c = (s - 5) // 2
                        pe.wait_ge(*FM.drained(g, f"v_{c}"))
                        pe.wait_ge(*FM.drained(g, ("T", 2 * c + 1)))
                        pe.wait_ge(*FM.empty(g, f"a_{c}"))
                        ps = FM.bank(f"a_{c}")
                        for b in range(G):
                            for r in range(2):
                                u = 2 * c + b // 2
                                ins = pe.matmul(ps[r * DH0:(r + 1) * DH0, tok(b)], fv[:, c % 3, b, r * DH0:(r + 1) * DH0],
                                                fprobsT[:, u % NPF, 2 * (b % 2) + r, :], start=True, stop=True)
                        ins.then_inc(FM.full_sem(f"a_{c}"), 1)
                    if 0 <= s - 3 < UA:
                        u = s - 3
                        pe.wait_ge(*fnormed.nth(g, u))
                        pe.wait_ge(*FM.empty(g, ("T", u)))
                        ps = FM.bank(("T", u))
                        for i in range(4):
                            ins = pe.transpose(ps[:, tok(i)], fprobs[:, u % NPF, i, :], ident[:, :])
                        ins.then_inc(FM.full_sem(("T", u)), 1)
                    yield
                for i in range(2):
                    if i == 0:
                        if isinstance(g, int) and g == 0:
                            pe.wait_ge(weights_in, 16 * NWEIGHTS)
                            pe.wait_ge(setup_done, 1)
                        pe.wait_ge(*FM.empty(g, "o0"))
                    else:
                        pe.wait_ge(*FM.drained(g, f"a_{C0 - 1}"))
                    ps = FM.bank("o0")
                    for c in range(C0 // 2 * i, C0 // 2 * (i + 1)):
                        ins = pe.matmul(ps[:, :], w_out[:, c, :], fattnT[:, c, :], start=(c == 0), stop=(c == C0 - 1))
                    if i:
                        ins.then_inc(FM.full_sem("o0"), 1)
                    yield
                yield
                pe.wait_ge(*FM.drained(g, "o0"))
                turn(FM, g, "y0", fyT)
                yield

            def rest(g, part):
                M, x, z, hT, yT, hid, qk = part.ring, part.x, part.z, part.hT, part.yT, part.hid, part.qk
                oT, v1, probs, probsT = part.oT, part.v1, part.probs, part.probsT

                def linear(use, terms):
                    pe.wait_ge(*M.empty(g, use))
                    ps = M.bank(use)
                    for i, (w, a) in enumerate(terms):
                        ins = pe.matmul(ps[:, :], w, a, start=(i == 0), stop=(i == len(terms) - 1))
                    ins.then_inc(M.full_sem(use), 1)

                def norm_turn(k):
                    yield
                    yield
                    pe.wait_ge(*part.z_ready.nth(g, k - part.norm0))
                    turn(M, g, f"ln{k}", z)
                    yield
                    pe.wait_ge(*M.drained(g, f"ln{k}"))

                def probs_turn(u):
                    pe.wait_ge(*part.normed.nth(g, u))
                    pe.wait_ge(*M.empty(g, ("T", u)))
                    ps = M.bank(("T", u))
                    for i in range(4):
                        ins = pe.transpose(ps[:, tok(i)], probs[:, u % NP, i, :], ident[:, :])
                    ins.then_inc(M.full_sem(("T", u)), 1)

                def output(use, turned, terms):
                    linear(use, terms)
                    yield
                    pe.wait_ge(*M.drained(g, use))
                    turn(M, g, turned, yT)
                    yield

                def mlp(l):
                    yield from norm_turn(2 * l + 1)
                    for c in range(FF):
                        linear(f"f{l}_{c}", [(w_up[:, l, tok(c)], hT[:, :])])
                    yield
                    for use in M.last_in_banks([f"f{l}_{c}" for c in range(FF)]):
                        pe.wait_ge(*M.drained(g, use))
                    if l == 1:
                        to_tokens("g1", [(hid[:, c, :], w_down[:, 1, c, :]) for c in range(FF)])
                        yield
                        return
                    yield from output(f"g{l}", f"z{l}", [(w_down[:, l, c, :], hid[:, c, :]) for c in range(FF)])

                def to_tokens(use, terms):
                    pe.wait_ge(*M.empty(g, use))
                    ps = M.bank(use)
                    for b in range(G):
                        for i, (a, w) in enumerate(terms):
                            ins = pe.matmul(ps[:, tok(b)], a[:, tok(b)], w, start=(i == 0), stop=(i == len(terms) - 1))
                    ins.then_inc(M.full_sem(use), 1)

                if part is MID:
                    yield from mlp(0)

                    yield from norm_turn(2)
                    linear("q1", [(w_l1[:, 0, :], hT[:, :])])
                    linear("k1", [(w_l1[:, 1, :], hT[:, :])])
                    to_tokens("v1", [(hT, w_l1[:, 2, :])])
                    yield
                    for use in M.last_in_banks(["q1", "k1"]):
                        pe.wait_ge(*M.drained(g, use))
                    pe.wait_ge(*M.empty(g, ("A", 0)))
                    ps = M.bank(("A", 0))
                    for b in range(G):
                        ins = pe.matmul(ps[:, tok(b)], qk[:, 0, tok(b)], qk[:, 1, tok(b)], start=True, stop=True)
                    ins.then_inc(M.full_sem(("A", 0)), 1)
                    yield
                    yield
                    probs_turn(0)
                    yield
                    pe.wait_ge(*M.drained(g, ("T", 0)))
                    pe.wait_ge(*M.drained(g, "v1"))
                    pe.wait_ge(*M.empty(g, "a1"))
                    ps = M.bank("a1")
                    for b in range(G):
                        ins = pe.matmul(ps[:, tok(b)], v1[:, b, :], probsT[:, 0, b, :], start=True, stop=True)
                    ins.then_inc(M.full_sem("a1"), 1)
                    yield
                    pe.wait_ge(*M.drained(g, "a1"))
                    to_tokens("o1", [(oT, w_l1[:, 3, :])])
                    yield
                    yield from mlp(1)
                    return

                yield from norm_turn(4)
                linear("k2", [(w_l2[:, 1, :], hT[:, :])])
                linear("q2", [(w_l2[:, 0, :], hT[:, :])])
                to_tokens("v2", [(hT, w_l2[:, 2, :])])
                yield
                pe.wait_ge(*M.drained(g, "q2"))
                for s in range(L2_STEPS):
                    if 0 <= s - 2 < UB:
                        probs_turn(s - 2)
                    if 0 <= s - 3 < UB:
                        u = s - 3
                        b, strip = u // 4, u % 4
                        pe.wait_ge(*M.drained(g, ("T", u)))
                        if strip == 0:
                            pe.wait_ge(*vm_ready.nth(g, b))
                        if u == 0:
                            pe.wait_ge(*M.empty(g, "a2"))
                        ps = M.bank("a2")
                        for i in range(4):
                            h = 4 * strip + i
                            ins = pe.matmul(ps[:, tok(b)], vm[:, b % 2, h * D:(h + 1) * D], probsT[:, u % NP, i, :],
                                            start=(h == 0), stop=(h == H2 - 1))
                        if u == UB - 1:
                            ins.then_inc(M.full_sem("a2"), 1)
                        elif strip == 3:
                            ins.then_inc(vm_used.sem, 1)
                    if s < UB:
                        b, strip = s // 4, s % 4
                        rows = slice(32 * strip, 32 * strip + 32)
                        if strip == 0:
                            pe.wait_ge(*km_ready.nth(g, b))
                        pe.wait_ge(*M.empty(g, ("A", s)))
                        ps = M.bank(("A", s))
                        pe.matmul(ps[:, :], qk[rows, 0, tok(b)], km[rows, :, tok(b)], start=True,
                                  stop=True).then_inc(M.full_sem(("A", s)), 1)
                    yield
                pe.wait_ge(*M.drained(g, "a2"))
                yield from output("o2", "y2", [(w_l2[:, 3, :], oT[:, :])])
                yield from mlp(2)

                pe.wait_ge(*adj_summed.nth(g, len(PIECES) - 1))
                pe.wait_ge(*M.empty(g, "adj"))
                ps = M.bank("adj")
                for i in range(2):
                    ins = pe.transpose(ps[:, i * G * NK3:(i + 1) * G * NK3], edge1[:, i, :], ident[0:G * NK3, 0:G * NK3])
                ins.then_inc(M.full_sem("adj"), 1)
                pe.wait_ge(*M.drained(g, "z2"))
                turn(M, g, "xt3", x)
                yield
                pe.wait_ge(*M.drained(g, "xt3"))
                linear("sum3", [(ones[:, :], x3T)])
                yield
                pe.wait_ge(*M.drained(g, "sum3"))
                linear("self3", [(w3[:, 0, :], x3T), (w3[:, 1, :], qx)])
                yield
                pe.wait_ge(*M.drained(g, "self3"))
                for d in range(2):
                    linear(f"q3_{d}", [(w3[:, 2 + d, :], sT[:, :])])
                pe.wait_ge(*M.empty(g, "k3"))
                ps = M.bank("k3")
                for d in range(2):
                    ins = pe.matmul(ps[:, d * G * NK3:(d + 1) * G * NK3], w3[:, 4 + d, :],
                                    sT[:, :].rearrange("p (b n) -> p b n", b=G)[:, :, 0:NK3], start=True, stop=True)
                ins.then_inc(M.full_sem("k3"), 1)
                yield
                for s in range(L3_STEPS):
                    if s < 3:
                        h0, nh = CH3[s]
                        if s == 0:
                            pe.wait_ge(*kvrep_ready.nth(g, 0))
                        for i in range(G // 2):
                            pe.wait_ge(*M.empty(g, f"vbd_{s}_{i}"))
                            ps = M.bank(f"vbd_{s}_{i}")
                            for b2 in range(2):
                                kv = kvrep[:, 2 * i + b2, h0:h0 + nh, :].rearrange("p h m -> p (h m)")
                                ins = pe.matmul(ps[0:nh * NK3, b2 * 2 * D:(b2 + 1) * 2 * D], kv,
                                                w3[:, 6:8, :].rearrange("p d g -> p (d g)"), start=True, stop=True)
                            ins.then_inc(M.full_sem(f"vbd_{s}_{i}"), 1)
                    if 0 <= s - 4 < NJ:
                        j = s - 4
                        pe.wait_ge(*normed3.nth(g, j))
                        pe.wait_ge(*M.empty(g, ("T3", j)))
                        ps = M.bank(("T3", j))
                        for c, (h0, nh) in enumerate(CH3):
                            ins = pe.transpose(ps[0:nh * NK3, tok(c)],
                                               p3[:, j, h0:h0 + nh, :].rearrange("p h m -> p (h m)"), ident[:, :])
                        ins.then_inc(M.full_sem(("T3", j)), 1)
                    if 0 <= s - 5 < NJ:
                        j = s - 5
                        b, d = j // 2, j % 2
                        pe.wait_ge(*M.drained(g, ("T3", j)))
                        if j == 0:
                            for use in M.last_in_banks([f"vbd_{c}_{i}" for c in range(3) for i in range(G // 2)]):
                                pe.wait_ge(*M.drained(g, use))
                            pe.wait_ge(*M.empty(g, "a3"))
                            ps = M.bank("a3")
                        else:
                            ps = M.bank("a3")
                        for c, (h0, nh) in enumerate(CH3):
                            rows = nh * NK3
                            ins = pe.matmul(ps[:, tok(b)], vbd[0:rows, c, b, d, :], p3T[0:rows, j % 2, c, :],
                                            start=(d == 0 and c == 0), stop=(d == 1 and c == 2))
                        if j == NJ - 1:
                            ins.then_inc(M.full_sem("a3"), 1)
                    if s < NJ:
                        b, d = s // 2, s % 2
                        if d == 0:
                            pe.wait_ge(*kbd_ready.nth(g, b))
                        pe.wait_ge(*M.empty(g, ("S3", s)))
                        ps = M.bank(("S3", s))
                        pe.matmul(ps[:, 0:H3 * NK3], q3[:, d, tok(b)],
                                  kbd[:, d, b, :, :].rearrange("p h m -> p (h m)"), start=True, stop=True).then_inc(M.full_sem(("S3", s)), 1)
                    yield
                yield
                pe.wait_ge(*rel_ready.nth(g, 0))
                turn(M, g, "y3", yT)
                yield

            def prologue():
                pe.wait_ge(pool_setup, 2)
                pe.wait_ge(silu_ready, 2)
                for i in range(2):
                    pe.transpose(SETUP[2][:, D + i * B:D + (i + 1) * B], cond[:, i, :], ident[0:B, 0:B])
                pe.wait_ge(mod_in, 32)
                pe.transpose(SETUP[2][:, 0:NROWS], bias_rows[:, :], ident[0:NROWS, 0:NROWS]).then_inc(pe_setup, 1)
                pe.wait_ge(dve_setup, 1)
                for m in range(NMOD):
                    ins = pe.matmul(SETUP[3][:, m * B:(m + 1) * B], w_mod[:, m, :], condT[:, 0 if m < 6 else 1, :],
                                    start=True, stop=True)
                ins.then_inc(pe_setup, 1)
                for ring in (FM, MM, BM, FIRST):
                    for free in ring.free_sems:
                        pe.sem_inc(free, 1)
                front_norm(0, FIRST, 0)
                pe.wait_ge(layer3_in, 48)
                for i in range(8):
                    ins = pe.transpose(SETUP[i // 4][:, tok(i % 4)], w3_raw[:, i, :], ident[:, :])
                ins.then_inc(pe_setup, 1)
                pe.wait_ge(*FIRST.drained(0, "ln0"))
                pe.wait_ge(consts_ready, 1)
                pe.wait_ge(w_qkv_in, 16)

            run(pe, prologue, front, rest)

        @block.vector
        def _(dve):
            def statistics(chain, g, i, src, k):
                for b in range(G):
                    ins = dve.bn_stats(stats[:, i, b, :], src[:, b, :])
                ins.then_inc(chain.sem, 1)
                dve.wait_ge(*chain.last(g))
                dve.memset(held[:, 0:1], 0.0)
                for b in range(G):
                    ins = dve.bn_aggr(mv[:, i, b, :], stats[:, i, b, :])
                ins.then_inc(chain.sem, 1)
                dve.wait_ge(*chain.last(g))
                if RMS[k]:
                    dve.tensor_tensor(msq[:, :], mv[:, i, :, 0], mv[:, i, :, 0], ALU.mult).then_inc(chain.sem, 1)
                    dve.wait_ge(*chain.last(g))
                    return dve.scalar_tensor_tensor(veps[:, i, :], mv[:, i, :, 1], EPS[k], msq[:, :], ALU.add, ALU.add)
                return dve.tensor_scalar(veps[:, i, :], mv[:, i, :, 1], EPS[k], None, ALU.add)

            def normalize(i, dst, src, k):
                for b in range(G):
                    r = rstd[:, i, b:b + 1]
                    if RMS[k]:
                        ins = dve.tensor_scalar(dst[:, b, :], src[:, b, :], r, None, ALU.mult)
                    else:
                        ins = dve.tensor_scalar(dst[:, b, :], src[:, b, :], mv[:, i, b, 0:1], r, ALU.subtract, ALU.mult)
                return ins

            def modulate(dst, ps, scale, shift):
                for b in range(G):
                    ins = dve.tensor_scalar(dst[:, tok(b)], ps[:, tok(b)], scale[:, b:b + 1], shift[:, b:b + 1], ALU.mult, ALU.add)
                return ins

            def gate(dst, ps, bias, g_):
                for b in range(G):
                    ins = dve.tensor_scalar(dst[:, tok(b)], ps[:, tok(b)], col[:, bias:bias + 1], g_[:, b:b + 1], ALU.add, ALU.mult)
                return ins

            def front_statistics(g):
                front_chain.n = 0
                dve.wait_ge(x_norm_in, g * 16 + 16)
                statistics(front_chain, g, 0, x_norm, 0).then_inc(fvar_ready.sem, 1)
                assert front_chain.n == front_chain.per

            def front_normalize(g):
                dve.wait_ge(*frstd_ready.nth(g, 0))
                normalize(0, fz, x_norm, 0).then_inc(fz_ready.sem, 1)

            def front_modulate(g, ring, ring_g):
                dve.tensor_copy(fmod[:, 0:2, :], mod[:, 0:2, bass.ds(g * G, G)]).then_inc(fmod_ready.sem, 1)
                dve.wait_ge(*fmod_ready.nth(g, 0))
                dve.wait_ge(*ring.full(ring_g, "ln0"))
                ps = ring.bank("ln0")
                modulate(fhT, ps, fmod[:, 1, :], fmod[:, 0, :]).then_inc(ring.free_sem("ln0"), 1)

            def front(g):
                for s in range(ATT_STEPS):
                    if 0 <= s - 3 < UA:
                        dve.wait_ge(*FM.drained(g, ("S", s - 3)))
                        dve.reciprocal(frinv[:, s - 3, :], frsum[:, s - 3, :]).then_inc(frinv_ready.sem, 1)
                    if s // 2 < C0:
                        c = s // 2
                        if s % 2 == 0:
                            dve.wait_ge(*FM.full(g, f"q_{c}"))
                            ps = FM.bank(f"q_{c}")
                            dve.tensor_scalar(fq[:, c % 2, :], ps[:, :], DH0 ** -0.5, None,
                                              ALU.mult).then_inc(FM.free_sem(f"q_{c}"), 1)
                        else:
                            dve.wait_ge(*FM.full(g, f"v_{c}"))
                            ps = FM.bank(f"v_{c}")
                            dve.tensor_copy(flat(fv[:, c % 3, :, :]), ps[:, :]).then_inc(FM.free_sem(f"v_{c}"), 1)
                    if 0 <= s - 2 < UA:
                        dve.wait_ge(*FM.full(g, ("S", s - 2)))
                        ps = FM.bank(("S", s - 2))
                        dve.tensor_reduce(fnegmax[:, s - 2, :], ps[:, :].rearrange("p (h k) -> p h k", h=4),
                                          AX.X, ALU.max, negate=True).then_inc(fmax_ready.sem, 1)
                    if s == UA + 2:
                        front_modulate(g + 1, FM, g)
                    yield
                    if s >= 5 and s % 2 == 1 and (s - 5) // 2 < C0:
                        c = (s - 5) // 2
                        dve.wait_ge(*FM.full(g, f"a_{c}"))
                        ps = FM.bank(f"a_{c}")
                        dve.tensor_copy(fattnT[:, c, :], ps[:, :]).then_inc(FM.free_sem(f"a_{c}"), 1)
                    if s == UA:
                        front_statistics(g + 1)
                    if s == UA + 1:
                        front_normalize(g + 1)
                    yield
                yield
                dve.tensor_copy(fmod[:, 2, :], mod[:, GATE["o0"], bass.ds(g * G, G)]).then_inc(fgate_ready.sem, 1)
                yield
                dve.wait_ge(*fgate_ready.nth(g, 0))
                dve.wait_ge(*FM.full(g, "o0"))
                ps = FM.bank("o0")
                gate(fyT, ps, ROW["L0_cond_b_out"], fmod[:, 2, :]).then_inc(FM.free_sem("o0"), 1)
                yield
                dve.wait_ge(x_res_in, g * 16 + 16)
                dve.wait_ge(*FM.full(g, "y0"))
                ps = FM.bank("y0")
                dve.tensor_tensor(flat(x_res[:, :, :]), ps[:, :], flat(x_res[:, :, :]), ALU.add).then_inc(FM.free_sem("y0"), 1)
                yield

            def rest(g, part):
                M, x, z, hT, yT, hid, qk = part.ring, part.x, part.z, part.hT, part.yT, part.hid, part.qk
                oT, v1, rsum, gmod, chain = part.oT, part.v1, part.rsum, part.gmod, part.chain

                chain.n = 0

                def source(k):
                    return {1: x_res, 4: x1}.get(k, x)

                def norm(k):
                    statistics(chain, g, part.stat, source(k), k).then_inc(part.var_ready.sem, 1)
                    yield
                    dve.wait_ge(*part.rstd_ready.nth(g, k - part.norm0))
                    if k == 4:
                        dve.wait_ge(x_stored, g * 16 + 16)
                    normalize(part.stat, z, source(k), k).then_inc(part.z_ready.sem, 1)
                    yield
                    dve.wait_ge(*M.full(g, f"ln{k}"))
                    ps = M.bank(f"ln{k}")
                    modulate(hT, ps, gmod[:, SCALE[k], :], gmod[:, SHIFT[k], :]).then_inc(M.free_sem(f"ln{k}"), 1)
                    yield

                def biased(use, dst, bias):
                    dve.wait_ge(*M.full(g, use))
                    ps = M.bank(use)
                    dve.tensor_scalar(dst, ps[:, :], col[:, bias:bias + 1], None, ALU.add).then_inc(M.free_sem(use), 1)

                def scaled_q(use, dst, bias, scale):
                    dve.wait_ge(*M.full(g, use))
                    ps = M.bank(use)
                    dve.tensor_scalar(dst, ps[:, :], col[:, bias:bias + 1], scale, ALU.add, ALU.mult).then_inc(M.free_sem(use), 1)

                def output(use, turned, bias):
                    if use in GATE:
                        dve.wait_ge(*M.full(g, use))
                        ps = M.bank(use)
                        gate(yT, ps, bias, gmod[:, GATE[use], :]).then_inc(M.free_sem(use), 1)
                    else:
                        biased(use, yT[:, :], bias)
                    yield
                    dve.wait_ge(*M.full(g, turned))
                    ps = M.bank(turned)
                    before = {"z0": x_res, "y2": x1}.get(turned, x)
                    dve.tensor_tensor(flat(x[:, :, :]), ps[:, :], flat(before[:, :, :]), ALU.add).then_inc(M.free_sem(turned), 1)
                    dve.wait_ge(*M.drained(g, turned))
                    yield

                def add_to_residual(use, i):
                    dve.wait_ge(*xb_ready.nth(g, i))
                    dve.wait_ge(*M.full(g, use))
                    ps = M.bank(use)
                    to = x1 if use == "g1" else x
                    dve.tensor_tensor(flat(to[:, :, :]), ps[:, :], flat(z[:, :, :]), ALU.add).then_inc(M.free_sem(use), 1)
                    dve.wait_ge(*M.drained(g, use))

                def row_max(u):
                    dve.wait_ge(*M.full(g, ("A", u)))
                    ps = M.bank(("A", u))
                    dve.tensor_reduce(part.negmax[:, u, :], ps[:, :].rearrange("p (h k) -> p h k", h=4), AX.X,
                                      ALU.max, negate=True).then_inc(part.max_ready.sem, 1)

                def inverse(u):
                    dve.wait_ge(*M.drained(g, ("A", u)))
                    dve.reciprocal(part.rinv[:, u, :], rsum[:, u, :]).then_inc(part.rinv_ready.sem, 1)

                def edges(tick):
                    p = tick - 3
                    if not 0 <= p < len(PIECES):
                        return
                    d, e0, n = PIECES[p]
                    dst = edge1[:, :, e0:e0 + n] if d else edge0[:, :, 0, e0:e0 + n]
                    dve.wait_ge(*adjw_ready.nth(g, p))
                    _, labels, weighted = edge_views(p)
                    dve.tensor_reduce(dst[:, 0, :], labels, AX.X, ALU.add)
                    dve.tensor_reduce(dst[:, 1, :], weighted, AX.X, ALU.add).then_inc(adj_summed.sem, 1)

                def with_edges(steps):
                    for tick, _ in enumerate(steps):
                        edges(tick)
                        yield

                def mlp(l, b2):
                    yield from norm(2 * l + 1)
                    yield
                    if l == 1:
                        add_to_residual("g1", 1)
                        yield
                        return
                    yield from output(f"g{l}", f"z{l}", b2)

                dve.tensor_copy(gmod[:, :, :], mod[:, :, bass.ds(g * G, G)]).then_inc(chain.sem, 1)
                dve.wait_ge(*chain.last(g))
                def layer1():
                    yield from norm(2)
                    scaled_q("q1", qk[:, 0, :], ROW["L1_cond_q_b"], D ** -0.5)
                    dve.wait_ge(*M.full(g, "v1"))
                    ps = M.bank("v1")
                    dve.tensor_copy(flat(v1[:, :, :]), ps[:, :]).then_inc(M.free_sem("v1"), 1)
                    yield
                    row_max(0)
                    yield
                    inverse(0)
                    yield
                    yield
                    biased("a1", oT[:, :], ROW["L1_cond_v_b"])
                    yield
                    add_to_residual("o1", 0)
                    yield

                if part is MID:
                    dve.wait_ge(*FM.drained(g, "y0"))
                    yield from mlp(0, ROW["L0_cond_b2"])
                    yield from layer1()
                    yield from mlp(1, None)
                    assert chain.n == chain.per, chain.n
                    return

                def layer2():
                    yield from norm(4)
                    scaled_q("q2", qk[:, 0, :], ROW["L2_cond_bq"], DH2 ** -0.5)
                    dve.wait_ge(*M.full(g, "v2"))
                    ps = M.bank("v2")
                    dve.tensor_copy(flat(v1[:, :, :]), ps[:, :]).then_inc(M.free_sem("v2"), 1)
                    yield
                    dve.wait_ge(*M.drained(g, "v2"))
                    for s in range(L2_STEPS):
                        if 0 <= s - 1 < UB:
                            inverse(s - 1)
                        if s % 4 == 0 and s // 4 < G:
                            b = s // 4
                            if b >= 2:
                                dve.wait_ge(*vm_used.nth(g, b - 2))
                            dve.tensor_copy(vm[:, b % 2, :].rearrange("p (h e) -> p h e", h=H2)[:, :, 0:DH2],
                                            v1[:, b, :].rearrange("p (h e) -> p h e", h=H2)).then_inc(vm_ready.sem, 1)
                        if s < UB:
                            row_max(s)
                        yield
                    biased("a2", oT[:, :], ROW["L2_cond_bv"])
                    yield from output("o2", "y2", ROW["L2_cond_bo"])

                dve.wait_ge(*MM.drained(g, "g1"))
                yield from with_edges(layer2())
                yield from mlp(2, ROW["L2_cond_b2"])

                dve.tensor_copy(gcond[:, :], condT[:, 1, bass.ds(g * G, G)]).then_inc(chain.sem, 1)
                dve.wait_ge(*chain.last(g))
                dve.wait_ge(*M.full(g, "adj"))
                ps = M.bank("adj")
                dve.tensor_copy(edge0[:, :, 1, :], ps[:, 0:2 * G * NK3].rearrange("p (a e) -> p a e", a=2)).then_inc(M.free_sem("adj"), 1)
                dve.wait_ge(*M.drained(g, "adj"))
                dve.tensor_scalar(keep[:, :, :], edge0[:, 0, :, :], 0.0, None, ALU.is_gt).then_inc(chain.sem, 1)
                dve.wait_ge(*chain.last(g))
                dve.tensor_scalar(nbias[:, :, :], keep[:, :, :], -NEG, NEG, ALU.mult, ALU.add).then_inc(chain.sem, 1)
                dve.wait_ge(*chain.last(g))
                dve.scalar_tensor_tensor(nbias[:, :, :], edge0[:, 1, :, :], blab[:, 0:1], nbias[:, :, :],
                                         ALU.add, ALU.add).then_inc(bias_ready.sem, 1)
                yield
                dve.wait_ge(*M.full(g, "sum3"))
                ps = M.bank("sum3")
                for b in range(G):
                    ins = dve.tensor_scalar(qx[:, tok(b)], ps[:, tok(b)], 0.0, gcond[:, b:b + 1], ALU.not_equal, ALU.mult)
                ins.then_inc(M.free_sem("sum3"), 1)
                yield
                biased("self3", sT[:, :], ROW["L3_cond_b_self"])
                dve.wait_ge(*M.drained(g, "self3"))
                kv = sT[:, :].rearrange("p (b n) -> p b n", b=G)[:, :, 0:NK3]
                for b in range(G):
                    ins = dve.tensor_copy(kvrep[:, b, :, :], kv[:, b, :].unsqueeze(1).to_broadcast([D, H3, NK3]))
                ins.then_inc(kvrep_ready.sem, 1)
                yield
                for d in range(2):
                    scaled_q(f"q3_{d}", q3[:, d, :], ROW["L3_cond_bq"] + d, DH3 ** -0.5)
                dve.wait_ge(*M.full(g, "k3"))
                ps = M.bank("k3")
                for d in range(2):
                    c = ROW["L3_cond_bk"] + d
                    ins = dve.tensor_scalar(k3[:, d, :], ps[:, d * G * NK3:(d + 1) * G * NK3], col[:, c:c + 1], None, ALU.add)
                ins.then_inc(M.free_sem("k3"), 1)
                yield
                dve.wait_ge(*bias_ready.nth(g, 0))
                for s in range(L3_STEPS):
                    if 0 <= s - 3 < NJ:
                        j = s - 3
                        dve.wait_ge(*exp3_ready.nth(g, j))
                        dve.tensor_reduce(rsum3[:, j, :], p3[:, j, :, :], AX.X, ALU.add).then_inc(chain.sem, 1)
                        dve.wait_ge(*chain.last(g))
                        dve.reciprocal(rinv3[:, j, :], rsum3[:, j, :]).then_inc(rinv3_ready.sem, 1)
                    if s < 3:
                        rows = CH3[s][1] * NK3
                        mask = blk3[0:rows, s, :, :].rearrange("p h g -> p (h g)").unsqueeze(1).to_broadcast([rows, G, D])
                        for i in range(G // 2):
                            dve.wait_ge(*M.full(g, f"vbd_{s}_{i}"))
                            ps = M.bank(f"vbd_{s}_{i}")
                            dst = vbd[0:rows, s, 2 * i:2 * i + 2, :, :].rearrange("p b d g -> p (b d) g")
                            dve.tensor_tensor(dst, ps[0:rows, :].rearrange("p (a g) -> p a g", a=4), mask, ALU.mult).then_inc(M.free_sem(f"vbd_{s}_{i}"), 1)
                    if s < NJ:
                        b, d = s // 2, s % 2
                        dve.wait_ge(*M.full(g, ("S3", s)))
                        ps = M.bank(("S3", s))
                        kp = keep[:, d, b * NK3:(b + 1) * NK3].unsqueeze(1).to_broadcast([D, H3, NK3])
                        dve.tensor_tensor(p3[:, s, :, :], ps[:, 0:H3 * NK3].rearrange("p (h m) -> p h m", h=H3), kp,
                                          ALU.mult).then_inc(M.free_sem(("S3", s)), 1)
                        nb = nbias[:, d, b * NK3:(b + 1) * NK3].unsqueeze(1).to_broadcast([D, H3, NK3])
                        dve.wait_ge(*M.drained(g, ("S3", s)))
                        dve.tensor_tensor(p3[:, s, :, :], p3[:, s, :, :], nb, ALU.add).then_inc(biased3.sem, 1)
                        dve.wait_ge(*biased3.nth(g, s))
                        dve.tensor_reduce(nmax3[:, s, :], p3[:, s, :, :], AX.X, ALU.max, negate=True).then_inc(max3_ready.sem, 1)
                    yield
                dve.wait_ge(*M.full(g, "a3"))
                ps = M.bank("a3")
                dve.scalar_tensor_tensor(yT[:, :], ps[:, :], bout3[:, 0:1], sT[:, :], ALU.add, ALU.add).then_inc(M.free_sem("a3"), 1)
                dve.wait_ge(*M.drained(g, "a3"))
                dve.tensor_scalar(yT[:, :], yT[:, :], 0.0, None, ALU.max).then_inc(rel_ready.sem, 1)
                yield
                dve.wait_ge(*M.full(g, "y3"))
                ps = M.bank("y3")
                dve.tensor_tensor(flat(x_out[:, :, :]), ps[:, :], flat(x[:, :, :]), ALU.add).then_inc(M.free_sem("y3"), 1)
                dve.wait_ge(*M.drained(g, "y3"))
                yield
                assert chain.n == chain.per, chain.n

            def prologue():
                front_statistics(0)
                front_normalize(0)
                dve.memset(mod[:, :, B:B + G], 0.0)
                dve.wait_ge(pe_setup, 1)
                dve.tensor_copy(condT[:, :, :], SETUP[2][:, D:D + 2 * B].rearrange("p (a b) -> p a b", a=2)).then_inc(dve_setup, 1)
                dve.tensor_copy(col[:, :], SETUP[2][:, 0:NROWS]).then_inc(dve_setup, 1)
                dve.wait_ge(pe_setup, 2)
                dve.wait_ge(dve_setup, 2)
                dve.tensor_tensor(mod[:, :, 0:B], SETUP[3][:, :].rearrange("p (m b) -> p m b", m=NMOD),
                                  wide(col[:, 0:NMOD], B), ALU.add).then_inc(dve_setup, 1)
                dve.wait_ge(dve_setup, 3)
                for k in range(6):
                    m = SCALE[k]
                    if RMS[k]:
                        w = ROW["L1_cond_norm1_w"] + (k - 2)
                        ins = dve.tensor_scalar(mod[:, m, :], mod[:, m, :], 1.0, col[:, w:w + 1], ALU.add, ALU.mult)
                    else:
                        ins = dve.tensor_scalar(mod[:, m, :], mod[:, m, :], 1.0, None, ALU.add)
                ins.then_inc(dve_setup, 1)
                dve.wait_ge(dve_setup, 4)
                front_modulate(0, FIRST, 0)
                dve.wait_ge(pe_setup, 3)
                for i in range(2):
                    dve.tensor_copy(w3[:, 4 * i:4 * i + 4, :], SETUP[i][:, :].rearrange("p (a b) -> p a b", a=4))
                dve.wait_ge(consts_ready, 1)
                dve.tensor_reduce(head4[:, :], head16[:, :].rearrange("p (s h) -> p h s", h=4), AX.X, ALU.add)
                r = ROW["L3_cond_bout"]
                dve.tensor_tensor(bout3[:, :], col[:, r:r + 1], col[:, r + 1:r + 2], ALU.add).then_inc(setup_done, 1)
                dve.wait_ge(setup_done, 1)
                dve.sem_inc(x_stored, 16)

            run(dve, prologue, front, rest)


def lay_out(inputs):
    import numpy as np

    a = {name: np.ascontiguousarray(v) for name, v in inputs.items()}
    t = {name: a[name] for name in ("x", "cond_1024", "mask_BxSxSx11_ik0", "L0_cond_W_qkv", "L0_cond_W_out")}
    t["bias_rows"] = np.concatenate([a[name].reshape(k, D) for name, k in BIAS_ROWS])
    t["w_mod"] = np.concatenate([a[name] for name in ("L0_cond_W_mod", "L1_cond_film1_w", "L1_cond_film2_w", "L2_cond_W_ada")],
                                axis=1)
    t["w3"] = np.concatenate([a["L3_cond_W_self"]]
                             + [a[name].transpose(1, 0, 2).reshape(D, 2 * D) for name in ("L3_cond_Wq", "L3_cond_Wk")]
                             + [a["L3_cond_Wout"].transpose(1, 2, 0, 3).reshape(D, 2 * D)], axis=1)
    t["labels3"] = np.concatenate([a["L3_cond_w_bias"], a["L3_cond_b_bias"].reshape(1)]).reshape(1, L3 + 1)
    t["rows1"] = np.concatenate([a["L1_cond_proj_b"], a["L1_cond_mlp_b2"]]).reshape(1, 2 * D)
    t["w_up"] = np.concatenate([a[name] for name in ("L0_cond_W1", "L1_cond_mlp_w1", "L2_cond_W1")], axis=1)
    t["w_down"] = np.concatenate([a[name] for name in ("L0_cond_W2", "L1_cond_mlp_w2", "L2_cond_W2")])
    t["w_l1"] = np.concatenate([a[f"L1_cond_{name}_w"] for name in ("q", "k", "v", "proj")], axis=1)
    t["w_l2"] = np.concatenate([a[f"L2_cond_W{name}"] for name in "qkvo"], axis=1)
    return t


def kernel(**inputs):
    import numpy as np
    import concourse.bacc as bacc
    from concourse.bass_utils import run_bass_kernel_spmd

    nc = bacc.Bacc("TRN2", target_bir_lowering=False, num_devices=1)
    arrays, t = {}, {}
    for name, a in lay_out(inputs).items():
        arrays[f"in_{name}"] = a = np.ascontiguousarray(a)
        t[name] = nc.dram_tensor(f"in_{name}", a.shape, mybir.dt.from_np(a.dtype), kind="ExternalInput").ap()
    out = nc.dram_tensor("out_0", (B, D, D), F32, kind="ExternalOutput").ap()
    build(nc, t, out)
    r = run_bass_kernel_spmd(nc, [arrays], core_ids=[0])
    return r.results[0]["out_0"]
```
